# Optimizing a Trainium2 kernel written in Bass

```python
import numpy as np
import jax
import jax.numpy as jnp

def _softmax(x, axis=-1):
    return jax.nn.softmax(x, axis=axis)

def _gelu(x):
    return jax.nn.gelu(x, approximate=True)

def _silu(x):
    return jax.nn.silu(x)

def _sigmoid(x):
    return jax.nn.sigmoid(x)

def _layernorm(x, axis=-1, eps=1e-05):
    m = jnp.mean(x, axis=axis, keepdims=True)
    v = jnp.var(x, axis=axis, keepdims=True)
    return (x - m) / jnp.sqrt(v + eps)

def _scatter_add(tgt, idx, src, axis=0):
    return tgt.at[idx].add(src)

def _segment_sum(src, seg, n):
    return jax.ops.segment_sum(src, seg, n)
kernel_name = 'mk_adaln_d1_jaxref_r4_e3b177'

def setup_inputs(seed: int=0):
    np.random.seed(seed)
    _w = jnp.asarray

    def _L0_attn_setup():
        import jax, jax.numpy as jnp
        import numpy as np
        B, S, HID = (2, 512, 512)
        NH, HD, RD = (16, 128, 64)
        KVC, QC = (128, 384)

        def _apply_rope(t):
            R = t.shape[-1]
            s = t.shape[-2]
            inv_freq = 1.0 / 10000.0 ** (jnp.arange(0, R, 2, dtype=jnp.float32) / R)
            ang = jnp.arange(s, dtype=jnp.float32)[:, None] * inv_freq[None, :]
            cos, sin = (jnp.cos(ang), jnp.sin(ang))
            t1, t2 = (t[..., :R // 2], t[..., R // 2:])
            return jnp.concatenate([t1 * cos - t2 * sin, t2 * cos + t1 * sin], axis=-1)
        key = jax.random.key(seed)
        ks = jax.random.split(key, 20)

        def lin(k, fan_in, fan_out):
            bound = 1.0 / np.sqrt(fan_in)
            kw, kb = jax.random.split(k)
            W = jax.random.uniform(kw, (fan_in, fan_out), jnp.float32, -bound, bound)
            b = jax.random.uniform(kb, (fan_out,), jnp.float32, -bound, bound)
            return (W, b)
        x = jax.random.normal(ks[0], (B, S, HID), jnp.float32)
        W_kvd, b_kvd = lin(ks[1], HID, KVC)
        W_ku, b_ku = lin(ks[2], KVC, NH * HD)
        W_vu, b_vu = lin(ks[3], KVC, NH * HD)
        W_kr, b_kr = lin(ks[4], KVC, NH * RD)
        W_qd, b_qd = lin(ks[5], HID, QC)
        W_qu, b_qu = lin(ks[6], QC, NH * HD)
        W_qr, b_qr = lin(ks[7], QC, NH * RD)
        W_o, b_o = lin(ks[8], NH * HD, HID)
        return dict(x=x, W_kvd=W_kvd, b_kvd=b_kvd, W_ku=W_ku, b_ku=b_ku, W_vu=W_vu, b_vu=b_vu, W_kr=W_kr, b_kr=b_kr, W_qd=W_qd, b_qd=b_qd, W_qu=W_qu, b_qu=b_qu, W_qr=W_qr, b_qr=b_qr, W_o=W_o, b_o=b_o)
    _L0_attn_in = _L0_attn_setup()

    def _L0_ffn_setup():
        import jax, jax.numpy as jnp
        import numpy as np
        B, S, D_IN, D_OUT, E, R = (4, 512, 512, 512, 8, 16)
        SCALING = 32.0 / 16.0
        key = jax.random.key(seed)
        ks = jax.random.split(key, 7)
        return {'x': jax.random.normal(ks[0], (B, S, D_IN), jnp.float32), 'base_w': jax.random.normal(ks[1], (D_OUT, D_IN), jnp.float32) * 0.02, 'base_b': jax.random.normal(ks[2], (D_OUT,), jnp.float32) * 0.02, 'router_w': jax.random.normal(ks[3], (E, D_IN), jnp.float32) * 0.02, 'router_b': jax.random.normal(ks[4], (E,), jnp.float32) * 0.02, 'lora_A': jax.random.normal(ks[5], (E, D_IN, R), jnp.float32) * 0.02, 'lora_B': jax.random.normal(ks[6], (E, R, D_OUT), jnp.float32) * 0.02}
    _L0_ffn_in = _L0_ffn_setup()
    _L0_c = _w((lambda *s: np.random.randn(*s).astype(np.float32) * 0.05)(8, 512))
    _L0_wmod = _w((lambda *s: np.random.randn(*s).astype(np.float32) * 0.05)(512, 6 * 512) * 512 ** (-0.5))
    _d = {'L0_attn_x': _L0_attn_in['x'], 'L0_attn_W_kvd': _L0_attn_in['W_kvd'], 'L0_attn_b_kvd': _L0_attn_in['b_kvd'], 'L0_attn_W_ku': _L0_attn_in['W_ku'], 'L0_attn_b_ku': _L0_attn_in['b_ku'], 'L0_attn_W_vu': _L0_attn_in['W_vu'], 'L0_attn_b_vu': _L0_attn_in['b_vu'], 'L0_attn_W_kr': _L0_attn_in['W_kr'], 'L0_attn_b_kr': _L0_attn_in['b_kr'], 'L0_attn_W_qd': _L0_attn_in['W_qd'], 'L0_attn_b_qd': _L0_attn_in['b_qd'], 'L0_attn_W_qu': _L0_attn_in['W_qu'], 'L0_attn_b_qu': _L0_attn_in['b_qu'], 'L0_attn_W_qr': _L0_attn_in['W_qr'], 'L0_attn_b_qr': _L0_attn_in['b_qr'], 'L0_attn_W_o': _L0_attn_in['W_o'], 'L0_attn_b_o': _L0_attn_in['b_o'], 'L0_ffn_base_w': _L0_ffn_in['base_w'], 'L0_ffn_base_b': _L0_ffn_in['base_b'], 'L0_ffn_router_w': _L0_ffn_in['router_w'], 'L0_ffn_router_b': _L0_ffn_in['router_b'], 'L0_ffn_lora_A': _L0_ffn_in['lora_A'], 'L0_ffn_lora_B': _L0_ffn_in['lora_B'], 'L0_c': _L0_c, 'L0_wmod': _L0_wmod}
    _x0 = _d['L0_attn_x']
    _d['L0_attn_x'] = jax.random.normal(jax.random.fold_in(jax.random.key(seed), 1), (8, 512, 512), dtype=_x0.dtype)
    del _x0
    return _d

def reference(L0_attn_x, L0_attn_W_kvd, L0_attn_b_kvd, L0_attn_W_ku, L0_attn_b_ku, L0_attn_W_vu, L0_attn_b_vu, L0_attn_W_kr, L0_attn_b_kr, L0_attn_W_qd, L0_attn_b_qd, L0_attn_W_qu, L0_attn_b_qu, L0_attn_W_qr, L0_attn_b_qr, L0_attn_W_o, L0_attn_b_o, L0_ffn_base_w, L0_ffn_base_b, L0_ffn_router_w, L0_ffn_router_b, L0_ffn_lora_A, L0_ffn_lora_B, L0_c, L0_wmod):

    def _L0_attn_ref(x, W_kvd, b_kvd, W_ku, b_ku, W_vu, b_vu, W_kr, b_kr, W_qd, b_qd, W_qu, b_qu, W_qr, b_qr, W_o, b_o):
        import jax, jax.numpy as jnp
        import numpy as np
        B, S, HID = (2, 512, 512)
        NH, HD, RD = (16, 128, 64)
        KVC, QC = (128, 384)

        def _apply_rope(t):
            R = t.shape[-1]
            s = t.shape[-2]
            inv_freq = 1.0 / 10000.0 ** (jnp.arange(0, R, 2, dtype=jnp.float32) / R)
            ang = jnp.arange(s, dtype=jnp.float32)[:, None] * inv_freq[None, :]
            cos, sin = (jnp.cos(ang), jnp.sin(ang))
            t1, t2 = (t[..., :R // 2], t[..., R // 2:])
            return jnp.concatenate([t1 * cos - t2 * sin, t2 * cos + t1 * sin], axis=-1)
        b, s, _ = x.shape

        def heads(t, d):
            return t.reshape(b, s, NH, d).transpose(0, 2, 1, 3)
        kv_c = x @ W_kvd + b_kvd
        keys_c = heads(kv_c @ W_ku + b_ku, HD)
        values = heads(kv_c @ W_vu + b_vu, HD)
        keys_r = _apply_rope(heads(kv_c @ W_kr + b_kr, RD))
        q_c = x @ W_qd + b_qd
        queries_c = heads(q_c @ W_qu + b_qu, HD)
        queries_r = _apply_rope(heads(q_c @ W_qr + b_qr, RD))
        q = jnp.concatenate([queries_c, queries_r], axis=-1)
        k = jnp.concatenate([keys_c, keys_r], axis=-1)
        scale = 1.0 / np.sqrt(HD + RD)
        scores = jnp.einsum('bhqd,bhkd->bhqk', q, k) * scale
        causal = jnp.triu(jnp.ones((s, s), dtype=bool), k=1)
        scores = jnp.where(causal[None, None], jnp.float32(-1000000000.0), scores)
        probs = jax.nn.softmax(scores, axis=-1)
        ctx = jnp.einsum('bhqk,bhkd->bhqd', probs, values)
        ctx = ctx.transpose(0, 2, 1, 3).reshape(b, s, NH * HD)
        return ctx @ W_o + b_o

    def _L0_ffn_ref(x, base_w, base_b, router_w, router_b, lora_A, lora_B):
        import jax, jax.numpy as jnp
        import numpy as np
        B, S, D_IN, D_OUT, E, R = (4, 512, 512, 512, 8, 16)
        SCALING = 32.0 / 16.0
        b, s, d_in = x.shape
        n = b * s
        e = lora_A.shape[0]
        d_out = lora_B.shape[-1]
        result = jnp.einsum('bsd,od->bso', x, base_w) + base_b
        logits = jnp.einsum('bsd,ed->bse', x, router_w) + router_b
        probs = jax.nn.softmax(logits.astype(jnp.float32), axis=-1)
        top_vals, top_idx = jax.lax.top_k(probs, 2)
        top_vals = top_vals / jnp.sum(top_vals, axis=-1, keepdims=True)
        top_vals = top_vals.astype(x.dtype)
        flat_idx = top_idx.reshape(n, 2)
        flat_val = top_vals.reshape(n, 2)
        gate = jnp.zeros((n, e), x.dtype).at[jnp.arange(n)[:, None], flat_idx].set(flat_val)
        xf = x.reshape(n, d_in)
        mid = jnp.einsum('nd,edr->ner', xf, lora_A)
        mid = mid * gate[:, :, None]
        lora_out = jnp.einsum('ner,erd->nd', mid, lora_B)
        return result + SCALING * lora_out.reshape(b, s, d_out)
    x = L0_attn_x
    mod = (_silu(L0_c) @ L0_wmod).reshape(L0_c.shape[0], 6, 1, -1)
    sa, ca, ga, sb, cb, gb = (mod[:, 0], mod[:, 1], mod[:, 2], mod[:, 3], mod[:, 4], mod[:, 5])
    ga = (2 * (ga >= 0) - 1) * jnp.maximum(jnp.abs(ga), 0.25)
    gb = (2 * (gb >= 0) - 1) * jnp.maximum(jnp.abs(gb), 0.25)
    h = _layernorm(x, axis=-1) * (1 + ca) + sa
    x = x + ga * _L0_attn_ref(h, L0_attn_W_kvd, L0_attn_b_kvd, L0_attn_W_ku, L0_attn_b_ku, L0_attn_W_vu, L0_attn_b_vu, L0_attn_W_kr, L0_attn_b_kr, L0_attn_W_qd, L0_attn_b_qd, L0_attn_W_qu, L0_attn_b_qu, L0_attn_W_qr, L0_attn_b_qr, L0_attn_W_o, L0_attn_b_o)
    h = _layernorm(x, axis=-1) * (1 + cb) + sb
    x = x + gb * _L0_ffn_ref(h, L0_ffn_base_w, L0_ffn_base_b, L0_ffn_router_w, L0_ffn_router_b, L0_ffn_lora_A, L0_ffn_lora_B)
    return x

_drawn_inputs = setup_inputs


def setup_inputs(seed=0):
    import zlib

    import numpy as np

    out = dict(_drawn_inputs(seed))
    spreads = {}
    factors = {'L0_attn_W_kvd': 8.0,
     'L0_attn_b_kvd': 8.0,
     'L0_attn_W_ku': 8.0,
     'L0_attn_b_ku': 200.0,
     'L0_attn_W_vu': 8.0,
     'L0_attn_b_vu': 24.106,
     'L0_attn_W_kr': 8.0,
     'L0_attn_b_kr': 8.0,
     'L0_attn_W_qd': 8.0,
     'L0_attn_b_qd': 8.0,
     'L0_attn_W_qu': 8.0,
     'L0_attn_b_qu': 8.0,
     'L0_attn_W_qr': 8.0,
     'L0_attn_b_qr': 8.0,
     'L0_attn_W_o': 5.969,
     'L0_attn_b_o': 200.0,
     'L0_ffn_base_b': 200.0,
     'L0_ffn_router_w': 21.057,
     'L0_ffn_router_b': 64.0,
     'L0_ffn_lora_A': 16.598,
     'L0_ffn_lora_B': 16.561,
     'L0_ffn_base_w': 8.0}
    for name, (base, spread) in spreads.items():
        noise = np.random.default_rng([zlib.crc32(name.encode()), seed]).standard_normal(out[name].shape)
        drawn = base * np.exp(spread * noise) if base else spread * noise
        out[name] = jnp.asarray(drawn.astype(out[name].dtype))
    for name, factor in factors.items():
        out[name] = (out[name] * factor).astype(out[name].dtype)
    return out
```

```python
from contextlib import ExitStack, contextmanager

import numpy as np
import concourse.bass as bass
from concourse import mybir

ALU = mybir.AluOpType
ACT = mybir.ActivationFunctionType
AX = mybir.AxisListType
F32 = mybir.dt.float32
F32R = mybir.dt.float32r
U32 = mybir.dt.uint32

P = 128
B, S, HID = 8, 512, 512
NH, HD, RD = 16, 128, 64
KVC, QC = 128, 384
NE, R = 8, 16
LORA_SCALING = 2.0
EPS = 1e-5
NT = S // P
NC = HID // P
NM = QC // P
GH = 4
NG = NH // GH
QW = GH * RD + GH
KW = GH * RD
FW = NE * R + NE
SCALE = 1.0 / float(np.sqrt(HD + RD))
HI, LO = 0, 1


class Count:

    def __init__(self):
        self.base, self.off = 0, 0
        self.seen = 0

    def at(self, more=0):
        return self.base + (self.off + more)

    def add(self, n=1):
        self.off += n
        self.seen += n


class Place:

    STAGES = {
        "mod": dict(m=2),
        "modT": dict(m=2),
        "normed": dict(var=1, xn=1, ln=2),
        "hT": dict(m=NC, h=NC),
        "latents": dict(m=NM + 1, hi=NM + 1),
        "kv_rows": dict(m=2),
        "absorb": dict(m=2, hi=2),
        "rotary": dict(m=2 * NT, ab=2 * NT, grp=1),
        "queries": dict(m=3, hi=3),
        "scores": dict(s=NT),
        "turn": dict(t=NT),
        "context": dict(m=1, hi=1),
        "project": dict(m=NT),
        "residual": dict(var=NT, xn=NT, ln=4 * NT),
        "experts": dict(m=NT, gate=15),
        "turn_mid": dict(t=2),
        "ffn_out": dict(y=NT),
        "batch": dict(batch=1),
    }
    NAMES = ("m", "hi", "h", "ab", "grp", "s", "t", "var", "xn", "ln", "gate", "y", "batch")

    def __init__(self):
        self.c = {n: Count() for n in self.NAMES}

    def at(self, name, more=0):
        return self.c[name].at(more)

    def bank(self, name, more=0):
        return (self.c[name].seen + more) % 2

    def done(self, *stages):
        for stage in stages:
            for name, n in self.STAGES[stage].items():
                self.c[name].add(n)


HEADS = ["scores", "queries", "scores", "turn", "context", "queries", "scores", "turn", "context",
         "scores", "turn", "context"]
GROUP = ["rotary", "turn", "context", "queries", "project", "queries"] + HEADS
LAST = ["turn", "context", "project", "residual", "hT", "experts", "turn_mid", "ffn_out", "batch"]
NEXT = ["normed", "hT", "latents", "kv_rows", "rotary"]
BATCH = ["queries", "queries"] + HEADS + GROUP * (NG - 1) + LAST + NEXT
SETUP = ["mod"] * 3 + ["modT", "normed", "hT", "latents"] + ["absorb"] * NH + ["kv_rows", "rotary"]


@contextmanager
def passes(eng, place, lo, hi, stages):
    total = Place()
    total.done(*stages)
    per = {n: c.off for n, c in total.c.items()}
    assert per["m"] % 2 == 0 and per["t"] % 2 == 0
    before = {n: c.at() for n, c in place.c.items()}
    seen = {n: c.seen for n, c in place.c.items()}
    with eng.Fori(lo, hi) as i:
        for n, c in place.c.items():
            c.base, c.off = (before[n] + (i - lo) * per[n] if per[n] else before[n]), 0
        yield i
        assert all(c.seen - seen[n] == per[n] for n, c in place.c.items())
    for n, c in place.c.items():
        c.base, c.off, c.seen = before[n] + (hi - lo) * per[n], 0, seen[n] + (hi - lo) * per[n]


def build(nc, x, inputs, consts, b_o, wmod, w_qd, w_kvd, heads_w, w_qr, w_kr, base_wT, ffn_a, ffn_b,
          q_row, k_row, f_row, out):
    with ExitStack() as ctx:
        def sb(name, shape, dt=F32):
            return ctx.enter_context(nc.sbuf_tensor(name, shape, dt))

        def sem(name):
            return ctx.enter_context(nc.semaphore(name))

        wqd = sb("wqd", [P, 2, NC, QC], F32R)
        wkvd = sb("wkvd", [P, 2, NC, KVC], F32R)
        wk = sb("wk", [P, 2, NG * KW], F32R)
        wp = sb("wp", [P, 2, 2, NM, KVC], F32R)
        wvo = sb("wvo", [P, 2 * GH * HID], F32R)
        wr = sb("wr", [P, 2, NM, QW], F32R)
        brow = sb("brow", [P, NG * QW], F32R)
        selr = sb("selr", [P, 3, P], F32R)
        cst = sb("cst", [P, P + S + 2 * NT * RD + NE])
        idf = cst[:, 0:P]
        maskt = cst[:, P:P + S]
        cost = cst[:, P + S:P + S + NT * RD].rearrange("p (t n) -> p t n", t=NT)
        sint = cst[:, P + S + NT * RD:P + S + 2 * NT * RD].rearrange("p (t n) -> p t n", t=NT)
        iotat = cst[:, P + S + 2 * NT * RD:]
        inp = sb("inp", [P, NC * B + NM + 1 + 3 * NH])
        sT = inp[:, 0:NC * B]
        bqd = inp[:, NC * B:NC * B + NM]
        bkvd = inp[:, NC * B + NM:NC * B + NM + 1]
        bqu = inp[:, NC * B + NM + 1:].rearrange("p (k h) -> p k h", k=3)
        qbias = sb("qbias", [P, NH])
        qbg = sb("qbg", [P, GH])
        modT = sb("modT", [P, 4 * NC, B])
        modb = sb("modb", [P, 4 * NC])
        nhalf = sb("nhalf", [P, NT])
        tiny = sb("tiny", [P, 4])
        tiny2 = sb("tiny2", [P, 3])
        xn = sb("xn", [P, NT, HID])
        acc = sb("acc", [P, NT, HID])
        gab = sb("gab", [P, 2, HID])
        hT = sb("hT", [P, 2, NC, S], F32R)
        qcT = sb("qcT", [P, 2, NM, S], F32R)
        kvT = sb("kvT", [P, 2, S], F32R)
        kvr = sb("kvr", [P, 2, NT, KVC], F32R)
        NR = 2 * NT * GH * 2 * RD
        rr = sb("rr", [P, NR + 4 * KW])
        rq = rr[:, 0:NR].rearrange("p (k t n) -> p k t n", k=2, t=NT)
        ab = rr[:, NR:NR + 4 * KW].rearrange("p (s k n) -> p s k n", s=2, k=2)
        cb = sb("cb", [P, NT, GH])
        qa = sb("qa", [P, 2, 2, S], F32R)
        q2 = sb("q2", [P, 2, S], F32R)
        kk = sb("kk", [P, 2, 2, S], F32R)
        NP_ = NT * (NT + 1) // 2 * P
        pr = sb("pr", [P, 2, NP_])
        pT = sb("pT", [P, 2 * NT * S], F32R)
        cxT = sb("cxT", [P, 2 * GH * S], F32R)
        nmx = sb("nmx", [P, 2, NT])
        nb = sb("nb", [P, 2, NT])
        sm = sb("sm", [P, 2, NT])
        rsm = sb("rsm", [P, 2, NT])
        stats = sb("stats", [P, NT, 6])
        mv = sb("mv", [P, NT, 2])
        ve = sb("ve", [P, NT])
        rstd = sb("rstd", [P, NT])
        sc = sb("sc", [P, 8, NT * NE])
        v8 = sb("v8", [P, NT, NE])
        i8 = sb("i8", [P, NT, NE], U32)
        gcol = sb("gcol", [P, NM, NH])
        gsp = sb("gsp", [P, 2, NM, NH], F32R)
        crow = sb("crow", [1, NH])
        sE = sb("sE", [P, 2, NC * B])
        bo_t = sb("bo_t", [1, HID])
        bias_s = sb("bias_s", [1, HID])

        pTv = pT[:, :].rearrange("p (k j s) -> p k j s", k=2, j=NT)
        cx = cxT[:, :].rearrange("p (k j s) -> p k j s", k=2, j=GH)
        wvov = wvo[:, :].rearrange("p (j k n) -> p j k n", j=GH, k=2)
        basew = pT[:, :].rearrange("p (k c n) -> p k c n", k=2, c=NC)
        NF = NC * FW + HID
        ffw = cxT[:, 0:2 * NF].rearrange("p (k n) -> p k n", k=2)
        fa = ffw[:, :, 0:NC * FW].rearrange("p k (c n) -> p k c n", c=NC)
        fb = ffw[:, :, NC * FW:NF]
        midT = cxT[:, 2 * NF:2 * NF + 2 * S].rearrange("p (k n) -> p k n", k=2)
        hf = pr[:, 0, 0:2 * S].rearrange("p (s n) -> p s n", s=2)
        mid = pr[:, 1, 0:NT * FW].rearrange("p (t n) -> p t n", t=NT)
        midg = pr[:, 1, 640:640 + NT * P].rearrange("p (t n) -> p t n", t=NT)
        HEADW = QC + KVC + 1 + KVC + HID
        hw = [rr[:, k * 1160:k * 1160 + HEADW] for k in range(2)]
        modw = [acc[:, :, :], rr[:, 2320:2320 + NC * HID].rearrange("p (c n) -> p c n", c=NC)]
        selt = rr[:, 4400:4400 + 3 * P]
        modrow = pr[0:B, :, :].rearrange("p k n -> p (k n)")
        raw = [pr[:, k, :] for k in range(2)]
        wps = [pT[:, k * 768:(k + 1) * 768].rearrange("p (k m n) -> p k m n", k=2, m=NM) for k in range(2)]
        wvs = [cxT[:, k * 1024:(k + 1) * 1024].rearrange("p (k n) -> p k n", k=2) for k in range(2)]
        stg = [wvo[:, k * 2048:(k + 1) * 2048].rearrange("p (k n) -> p k n", k=2) for k in range(2)]
        mrow = rr[0:B, 0:2 * HID]

        mb = [ctx.enter_context(nc.psum_tensor(f"mb{i}", [P, 512], F32)) for i in range(2)]
        tb = [ctx.enter_context(nc.psum_tensor(f"tb{i}", [P, 512], F32)) for i in range(2)]
        sk = [ctx.enter_context(nc.psum_tensor(f"sk{i}", [P, 512], F32)) for i in range(NT)]

        def scratch(name, shape):
            return nc.dram_tensor(name, shape, F32, kind="Internal").ap()

        wp_d = scratch("wp_d", [NH + 2, P, 2 * NM * KVC])
        wvo_d = scratch("wvo_d", [NH, P, 2 * HID])
        wr_d = scratch("wr_d", [NG + 1, P, 2, NM, QW])
        base_d = scratch("base_d", [P, 2, NC * HID])
        ff_d = scratch("ff_d", [P, 2, NF])
        gate_d = scratch("gate_d", [B, 2, HID])
        bias_d = scratch("bias_d", [1, HID])
        row_d = scratch("row_d", [6, NG * QW])

        names = ("c_in x_in wvo_in wr_in base_in ff_in gab_in acc_in brow_in "
                 "gcol_out gate_out bias_out y_out "
                 "m_full m_hi m_free t_full t_hi t_free s_full s_min s_bias s_exp s_rec p_norm "
                 "h_hi h_lo rotated grp_ready ln_var ln_rstd ln_xn ln_step mod_b "
                 "gate_step gate_max gate_exp mid_gated f_full y_mul y_done "
                 "raw_hi raw_lo g_hi g_lo set_step silu_e silu_done sel_ready bias_full bias_ev zeroed "
                 "crow_in hw_used brow_ok").split()
        (c_in, x_in, wvo_in, wr_in, base_in, ff_in, gab_in, acc_in, brow_in,
         gcol_out, gate_out, bias_out, y_out,
         m_full, m_hi, m_free, t_full, t_hi, t_free, s_full, s_min, s_bias, s_exp, s_rec, p_norm,
         h_hi, h_lo, rotated, grp_ready, ln_var, ln_rstd, ln_xn, ln_step, mod_b,
         gate_step, gate_max, gate_exp, mid_gated, f_full, y_mul, y_done,
         raw_hi, raw_lo, g_hi, g_lo, set_step, silu_e, silu_done, sel_ready, bias_full, bias_ev, zeroed,
         crow_in, hw_used, brow_ok) = [sem(n) for n in names]
        modw_in = [sem(f"modw_in{i}") for i in range(2)]
        hw_in = [sem(f"hw_in{i}") for i in range(2)]
        raw_in = [sem(f"raw_in{i}") for i in range(2)]
        wp_in = [sem(f"wp_in{i}") for i in range(2)]
        wps_out = [sem(f"wps_out{i}") for i in range(2)]
        wvs_out = [sem(f"wvs_out{i}") for i in range(2)]
        stg_out = [sem(f"stg_out{i}") for i in range(2)]
        T0, S0 = 2, NT

        block = ctx.enter_context(nc.Block())

        def v3(ap, a):
            return ap.rearrange("p (a n) -> p a n", a=a)

        wqd_v = w_qd.rearrange("(c p) n -> p c n", p=P)
        wqr_v = w_qr.rearrange("(m p) n -> m p n", p=P)
        base_v = base_wT.rearrange("(c p) n -> p c n", p=P)
        JOBS = []
        for k in range(2):
            JOBS.append((wqd_v[:, 2 * k:2 * k + 2, :], P, 2 * QC, 2, [wqd[:, hl, 2 * k:2 * k + 2, :] for hl in (HI, LO)], []))
        JOBS.append((w_kvd.rearrange("(c p) n -> p c n", p=P), P, NC * KVC, NC, [wkvd[:, hl, :, :] for hl in (HI, LO)], []))
        EARLY = len(JOBS)
        JOBS.append((w_kr, P, NG * KW, 1, [wk[:, hl, :] for hl in (HI, LO)], []))
        for m in range(NM):
            st = []
            for hl in (HI, LO):
                st.append((wr_d[0:NG, :, hl, m, 0:KW].rearrange("g p n -> p g n"), hl, NG, NG * KW))
                st.append((wr_d[NG:NG + 1, :, hl, m, 0:KW].rearrange("g p n -> p g n"), hl, 1, KW))
            JOBS.append((wqr_v[m], P, NG * KW, 1, None, st))
        for k in range(2):
            JOBS.append((base_v[:, 2 * k:2 * k + 2, :], P, 2 * HID, 2, None,
                         [(base_d[:, hl:hl + 1, 2 * k * HID:(2 * k + 2) * HID], hl, 1, 2 * HID) for hl in (HI, LO)]))
        JOBS.append((ffn_a.rearrange("(c p) n -> p c n", p=P), P, NC * FW, NC, None,
                     [(ff_d[:, hl:hl + 1, 0:NC * FW], hl, 1, NC * FW) for hl in (HI, LO)]))
        JOBS.append((ffn_b, P, HID, 1, None, [(ff_d[:, hl:hl + 1, NC * FW:NF], hl, 1, HID) for hl in (HI, LO)]))
        ROWS = len(JOBS)
        for src, n, r0, c0 in ((q_row[:, 0:2 * QW], 2 * QW, 0, 0), (q_row[:, 2 * QW:4 * QW], 2 * QW, 0, 2 * QW),
                               (k_row, NG * KW, 2, 0), (f_row, HID + FW, 4, 0)):
            JOBS.append((src, 1, n, 1, None, [(row_d[r0 + hl:r0 + hl + 1, c0:c0 + n].unsqueeze(1), hl, 1, n) for hl in (HI, LO)]))
        NJ = len(JOBS)
        stored, total = [], [0, 0]
        for k, job in enumerate(JOBS):
            total[k % 2] += 16 * len(job[5])
            stored.append(total[k % 2])

        def job_parts(k):
            _, rows, n, a, dst, _ = JOBS[k]
            src = raw[k % 2][0:rows, 0:n]
            if dst is None:
                return src, [stg[k % 2][0:rows, hl, 0:n] for hl in (HI, LO)]
            return (v3(src, a) if a > 1 else src), dst

        @block.sync
        def _(sp):
            pl = Place()
            sp.dma_start(inp[:, :], inputs).then_inc(c_in, 16)
            sp.dma_start(cst[:, :], consts[:, 0:P + S + 2 * NT * RD + NE]).then_inc(c_in, 16)
            sp.dma_start(selt, consts[:, P + S + 2 * NT * RD + NE:]).then_inc(c_in, 16)
            sp.dma_start(bo_t[:, :], b_o).then_inc(c_in, 16)
            sp.dma_start(xn[:, :, :], x[0].rearrange("(t p) n -> p t n", p=P)).then_inc(x_in, 16)
            wmod_v = wmod.rearrange("(c p) (k n) -> k p c n", p=P, n=HID)
            for k in range(6):
                if k >= 2:
                    sp.wait_ge(m_full, k - 1)
                sp.dma_start(modw[k % 2], wmod_v[k]).then_inc(modw_in[k % 2], 16)
            for h in range(NH):
                if h >= 2:
                    sp.wait_ge(hw_used, h - 1)
                else:
                    sp.wait_ge(sel_ready, 1)
                    sp.wait_ge(set_step, 8)
                sp.dma_start(hw[h % 2], heads_w[h * HD:(h + 1) * HD, :]).then_inc(hw_in[h % 2], 16)
            sp.wait_ge(bias_ev, 1)
            sp.dma_start(bias_d, bias_s[:, :]).then_inc(bias_out, 16)
            for k in (0, 1):
                sp.wait_ge(stg_out[k], total[k])
                sp.wait_ge(wps_out[k], 16 * (NH // 2 + 1))
                sp.wait_ge(wvs_out[k], 16 * (NH // 2))
            sp.wait_ge(gcol_out, 16 * 4 * NM)
            sp.wait_ge(zeroed, 1)
            for r0, n in ((0, NG * QW), (2, NG * KW), (4, HID + FW)):
                sp.dma_start(brow[r0:r0 + 2, 0:n].bitcast(F32), row_d[r0:r0 + 2, 0:n]).then_inc(brow_in, 16)
            sp.dma_start(wr[:, :, :, :].bitcast(F32), wr_d[0]).then_inc(wr_in, 16)

            def wp_load(k, h):
                sp.dma_start(wp[:, k, :, :, :].bitcast(F32).rearrange("p k m n -> p (k m n)"), wp_d[h]).then_inc(wp_in[k], 16)

            def wvo_load(h0):
                sp.dma_start(wvo[:, :].bitcast(F32).rearrange("p (j n) -> p j n", j=GH),
                             wvo_d[bass.ds(h0, GH)].rearrange("j p n -> p j n")).then_inc(wvo_in, 16)

            wp_load(0, 0)
            wp_load(1, 1)
            wvo_load(0)
            pl.done(*SETUP)
            sp.wait_ge(m_free, pl.at("m"))
            sp.dma_start(wr[:, :, :, :].bitcast(F32), wr_d[1]).then_inc(wr_in, 16)

            def wr_next(g):
                sp.wait_ge(m_free, pl.at("m", 2 * NT))
                sp.dma_start(wr[:, :, :, :].bitcast(F32), wr_d[g]).then_inc(wr_in, 16)
                pl.done("rotary")

            def wp_next(j, h):
                sp.wait_ge(m_full, pl.at("m", 1))
                wp_load(j % 2, h)
                pl.done("queries")

            def wvo_next(h0):
                sp.wait_ge(m_free, pl.at("m", NT))
                wvo_load(h0)
                pl.done("project")

            def heads(g):
                pl.done("scores")
                wp_next(2, GH * g + 4)
                pl.done("scores", "turn", "context")
                wp_next(3, GH * g + 5)
                pl.done("scores", "turn", "context", "scores", "turn", "context")

            def batch(b, last):
                sp.wait_ge(y_out, pl.at("batch") * (16 * NT))
                sp.wait_ge(bias_out, 16)
                sp.wait_ge(gate_out, 32)
                sp.dma_start(acc[:, :, :], bias_d.unsqueeze(1).broadcast_to([P, NT, HID])).then_inc(acc_in, 16)
                sp.dma_start(gab[:, :, :], gate_d[bass.ds(b, 1)].broadcast_to([P, 2, HID])).then_inc(gab_in, 16)
                if not last:
                    sp.dma_start(xn[:, :, :], x[b + 1].rearrange("(t p) n -> p t n", p=P)).then_inc(x_in, 16)
                wp_next(0, 2)
                wp_next(1, 3)
                heads(0)
                if not last:
                    pl.done("normed")
                with passes(sp, pl, 1, NG, GROUP) as g:
                    wr_next(g + 1)
                    pl.done("turn", "context")
                    wp_next(0, g * GH + 2)
                    wvo_next(g * GH)
                    wp_next(1, g * GH + 3)
                    heads(g)
                if not last:
                    sp.wait_ge(m_full, pl.at("m", NC))
                    pl.done("hT", "latents")
                sp.dma_start(xn[:, :, :], x[b].rearrange("(t p) n -> p t n", p=P)).then_inc(x_in, 16)
                pl.done("turn")
                sp.wait_ge(m_full, pl.at("m", 1))
                sp.dma_start(pT[:, :].bitcast(F32), base_d.rearrange("p k n -> p (k n)")).then_inc(base_in, 16)
                pl.done("context")
                if not last:
                    pl.done("kv_rows")
                sp.wait_ge(m_free, pl.at("m", NT))
                sp.dma_start(cxT[:, 0:2 * NF].bitcast(F32), ff_d.rearrange("p k n -> p (k n)")).then_inc(ff_in, 16)
                wvo_next(0)
                pl.done("residual")
                if not last:
                    wr_next(1)
                pl.done("hT", "experts", "turn_mid")
                for t in range(NT):
                    sp.wait_ge(y_done, pl.at("y", t + 1))
                    sp.dma_start(out[b, t * P:(t + 1) * P, :], xn[:, t, :]).then_inc(y_out, 16)
                pl.done("ffn_out", "batch")

            with passes(sp, pl, 0, B - 1, BATCH) as b:
                batch(b, False)
            batch(B - 1, True)
            sp.wait_ge(y_out, 16 * NT * B)
            sp.wait_ge(wvo_in, 16 * (NG * B + 1))
            for k in (0, 1):
                sp.wait_ge(wp_in[k], 16 * (NH // 2 * B + 1))

        @block.tensor
        def _(pe):
            pl = Place()

            def m_bank(u, early=False):
                if not early:
                    pe.wait_ge(m_free, pl.at("m", u - 1))
                return mb[pl.bank("m", u)]

            def three(o, a, b, first, last):
                nc.tensor.matmul(o, a[HI], b[HI], start=first, stop=False, skip_group_check=True)
                nc.tensor.matmul(o, a[HI], b[LO], start=False, stop=False, skip_group_check=True)
                return nc.tensor.matmul(o, a[LO], b[HI], start=False, stop=last, skip_group_check=True)

            def h_chunks():
                for c in range(NC):
                    ps = m_bank(c)
                    for t in range(NT):
                        mm = nc.tensor.transpose(ps[:, t * P:(t + 1) * P], xn[:, t, c * P:(c + 1) * P], idf)
                    mm.then_inc(m_full, 1)
                pl.done("hT")

            def latents():
                for m in range(NM + 1):
                    ps = m_bank(m)
                    for c in range(NC):
                        if m == 0:
                            pe.wait_ge(h_lo, pl.at("h", c + 1 - NC))
                        w = [wqd[:, hl, c, m * P:(m + 1) * P] if m < NM else wkvd[:, hl, c, :] for hl in (HI, LO)]
                        mm = three(ps[:, :], w, [hT[:, hl, c, :] for hl in (HI, LO)], c == 0, c == NC - 1)
                    mm.then_inc(m_full, 1)
                pl.done("latents")

            def kv_rows(latents_at):
                pe.wait_ge(m_free, latents_at)
                for hl in (HI, LO):
                    ps = m_bank(hl)
                    for t in range(NT):
                        mm = nc.tensor.transpose(ps[:, t * P:(t + 1) * P], kvT[:, hl, t * P:(t + 1) * P].bitcast(F32), idf)
                    mm.then_inc(m_full, 1)
                pl.done("kv_rows")

            def rotary(g, loads):
                pe.wait_ge(wr_in, loads)
                for t in range(NT):
                    tok = slice(t * P, (t + 1) * P)
                    ps = m_bank(2 * t)
                    for m in range(NM):
                        three(ps[:, 0:QW], [qcT[:, hl, m, tok] for hl in (HI, LO)], [wr[:, hl, m, :] for hl in (HI, LO)], m == 0, False)
                    nc.tensor.matmul(ps[:, 0:QW], selr[:, 0, :], brow[:, bass.ds(g * QW, QW)],
                                     start=False, stop=True, skip_group_check=True).then_inc(m_full, 1)
                    ps = m_bank(2 * t + 1)
                    three(ps[:, 0:KW], [kvT[:, hl, tok] for hl in (HI, LO)],
                          [wk[:, hl, bass.ds(g * KW, KW)] for hl in (HI, LO)], True, False)
                    nc.tensor.matmul(ps[:, 0:KW], selr[:, 1, :], brow[:, bass.ds(g * KW, KW)],
                                     start=False, stop=True, skip_group_check=True).then_inc(m_full, 1)
                pl.done("rotary")

            def queries(j, wp_loads, first=False):
                pe.wait_ge(wp_in[j % 2], wp_loads)
                ps = m_bank(0)
                for m in range(NM):
                    mm = three(ps[:, :], [wp[:, j % 2, hl, m, :] for hl in (HI, LO)], [qcT[:, hl, m, :] for hl in (HI, LO)], m == 0, m == NM - 1)
                mm.then_inc(m_full, 1)
                if first:
                    pe.wait_ge(rotated, pl.at("ab"))
                for k in range(2):
                    ps = m_bank(1 + k)
                    for t in range(NT):
                        mm = nc.tensor.transpose(ps[:, t * P:(t + 1) * P], rq[:, k, t, j * P:(j + 1) * P], idf)
                    mm.then_inc(m_full, 1)
                pl.done("queries")

            def scores(j, queries_at):
                pe.wait_ge(m_free, queries_at)
                for i in range(NT):
                    q, w = slice(i * P, (i + 1) * P), (i + 1) * P
                    pe.wait_ge(s_exp, pl.at("s", i + 1))
                    ps = sk[i][:, 0:w]
                    three(ps, [qa[:, j % 2, hl, q] for hl in (HI, LO)], [kvT[:, hl, 0:w] for hl in (HI, LO)], True, False)
                    nc.tensor.matmul(ps, q2[:, j % 2, q], kk[:, j % 2, HI, 0:w], start=False, stop=False, skip_group_check=True)
                    nc.tensor.matmul(ps, q2[:, j % 2, q], kk[:, j % 2, LO, 0:w], start=False, stop=True,
                                     skip_group_check=True).then_inc(s_full, 1)
                pl.done("scores")

            def turn(j, behind):
                for i in range(NT):
                    pe.wait_ge(p_norm, pl.at("s", i + 1 - NT * (behind + 1)))
                    pe.wait_ge(t_free, pl.at("t", i + 1))
                    o = i * (i + 1) // 2 * P
                    for k in range(i + 1):
                        mm = nc.tensor.transpose(tb[i % 2][:, k * P:(k + 1) * P],
                                                 pr[:, j % 2, o + k * P:o + (k + 1) * P], idf)
                    mm.then_inc(t_full, 1)
                pl.done("turn")

            def context():
                ps = m_bank(0)
                pe.wait_ge(t_free, pl.at("t", T0))
                for k in range(NT):
                    q = slice(k * P, S)
                    mm = three(ps[:, q], [kvr[:, hl, k, :] for hl in (HI, LO)], [pTv[:, hl, k, q] for hl in (HI, LO)], k == 0, k == NT - 1)
                mm.then_inc(m_full, 1)
                pl.done("context")

            def project(loads, context_at):
                pe.wait_ge(wvo_in, loads)
                pe.wait_ge(m_free, context_at)
                for t in range(NT):
                    ps = m_bank(t)
                    for j in range(GH):
                        mm = three(ps[:, :], [cx[:, hl, j, t * P:(t + 1) * P] for hl in (HI, LO)],
                                   [wvov[:, j, hl, :] for hl in (HI, LO)], j == 0, j == GH - 1)
                    mm.then_inc(m_full, 1)
                pl.done("project")

            def heads(queries_at, wp_loads):
                scores(0, queries_at)
                queries(2, wp_loads)
                scores(1, pl.at("m", -3))
                turn(0, 1)
                context()
                queries(3, wp_loads)
                scores(2, pl.at("m", -4))
                turn(1, 1)
                context()
                scores(3, pl.at("m", -1))
                turn(2, 1)
                context()

            pe.wait_ge(silu_done, 1)
            for k in range(6):
                ps = m_bank(k, k < 2)
                pe.wait_ge(modw_in[k % 2], 16 * (k // 2 + 1))
                for c in range(NC):
                    mm = nc.tensor.matmul(ps[0:B, :], sT[:, c * B:(c + 1) * B], modw[k % 2][:, c, :], start=(c == 0), stop=(c == NC - 1))
                mm.then_inc(m_full, 1)
            pl.done("mod", "mod", "mod")
            for r in range(2):
                ps = m_bank(r)
                if r == 0:
                    pe.wait_ge(m_free, 6)
                for k in range(2):
                    for c in range(NC):
                        o = (2 * r + k) * HID + c * P
                        mm = nc.tensor.transpose(ps[:, (k * NC + c) * B:(k * NC + c + 1) * B], modrow[:, o:o + P], idf[0:B, 0:B])
                mm.then_inc(m_full, 1)
            pl.done("modT", "normed")
            pe.wait_ge(ln_xn, 1)
            h_chunks()
            pe.wait_ge(raw_lo, EARLY)
            latents()
            latents_at = pl.at("m")
            for h in range(NH):
                pe.wait_ge(hw_in[h % 2], 16 * (h // 2 + 1))
                w = hw[h % 2]
                ku, vu, wo = w[:, QC:QC + KVC], w[:, QC + KVC + 1:QC + 2 * KVC + 1], w[:, QC + 2 * KVC + 1:HEADW]
                ps = m_bank(0)
                for m in range(NM):
                    nc.tensor.matmul(ps[:, m * 129:(m + 1) * 129], w[:, m * P:(m + 1) * P], w[:, QC:QC + KVC + 1], start=True, stop=True)
                nc.tensor.matmul(ps[:, 390:391], ku, bqu[:, 0, h:h + 1], start=True, stop=True)
                nc.tensor.matmul(ps[0:1, 391:392], bqu[:, 1, h:h + 1], bqu[:, 0, h:h + 1], start=True, stop=True).then_inc(m_full, 1)
                ps = m_bank(1)
                nc.tensor.matmul(ps[:, :], vu, wo, start=True, stop=True).then_inc(m_full, 1)
                nc.tensor.matmul(sk[0][0:1, :], bqu[:, 2, h:h + 1], wo, start=(h == 0), stop=False).then_inc(hw_used, 1)
                pl.done("absorb")
            nc.tensor.matmul(sk[0][0:1, :], idf[0:1, 0:1], bo_t[:, :], start=False, stop=True).then_inc(bias_full, 1)
            kv_rows(latents_at)
            pe.wait_ge(sel_ready, 1)
            pe.wait_ge(raw_lo, NJ)
            pe.wait_ge(brow_in, 3 * 16)
            rotary(0, 16)
            pe.wait_ge(bias_ev, 1)

            def batch(b, last):
                wp0 = pl.at("batch") * (16 * NH // 2)
                wg0 = pl.at("batch") * (16 * NG)
                queries(0, wp0 + 16, first=True)
                queries(1, wp0 + 16)
                pe.wait_ge(y_done, pl.at("y"))
                heads(pl.at("m", -3), wp0 + 32)
                if not last:
                    pl.done("normed")
                with passes(pe, pl, 1, NG, GROUP) as g:
                    wp1 = wp0 + g * 32
                    rotary(g, wg0 + g * 16 + 16)
                    turn(3, 0)
                    context()
                    queries(0, wp1 + 16, first=True)
                    project(wg0 + g * 16, pl.at("m", -3))
                    queries(1, wp1 + 16)
                    heads(pl.at("m", -7), wp1 + 32)
                if not last:
                    pe.wait_ge(ln_xn, pl.at("xn"))
                    h_chunks()
                    latents()
                turn(3, 0)
                context()
                context_at = pl.at("m")
                if not last:
                    kv_rows(pl.at("m", -1))
                project(wg0 + 16 * NG, context_at)
                pl.done("residual")
                if not last:
                    rotary(0, wg0 + 16 * NG + 16)
                pe.wait_ge(ln_xn, pl.at("xn"))
                h_chunks()
                pe.wait_ge(ff_in, pl.at("batch") * 16 + 16)
                for t in range(NT):
                    ps = m_bank(t)
                    tok = slice(t * P, (t + 1) * P)
                    for c in range(NC):
                        if t == 0:
                            pe.wait_ge(h_lo, pl.at("h", c + 1 - NC))
                        three(ps[:, 0:FW], [hT[:, hl, c, tok] for hl in (HI, LO)], [fa[:, hl, c, :] for hl in (HI, LO)], c == 0, False)
                    nc.tensor.matmul(ps[:, 0:FW], selr[:, 2, :], brow[:, HID:HID + FW], start=False, stop=True,
                                     skip_group_check=True).then_inc(m_full, 1)
                pl.done("experts")
                pe.wait_ge(base_in, pl.at("batch") * 16 + 16)
                for t in range(NT):
                    pe.wait_ge(s_exp, pl.at("s", t + 1))
                    tok = slice(t * P, (t + 1) * P)
                    for c in range(NC):
                        three(sk[t][:, :], [hT[:, hl, c, tok] for hl in (HI, LO)], [basew[:, hl, c, :] for hl in (HI, LO)], c == 0, False)
                    nc.tensor.matmul(sk[t][:, :], selr[:, 2, :], brow[:, 0:HID], start=False, stop=False, skip_group_check=True)
                pe.wait_ge(mid_gated, pl.at("batch") + 1)
                for k in range(2):
                    pe.wait_ge(t_free, pl.at("t", k + 1))
                    for t in range(2):
                        mm = nc.tensor.transpose(tb[k][:, t * P:(t + 1) * P], midg[:, 2 * k + t, :], idf)
                    mm.then_inc(t_full, 1)
                pl.done("turn_mid")
                for t in range(NT):
                    if t % 2 == 0:
                        pe.wait_ge(t_free, pl.at("t", T0 - 1 + t // 2))
                    tok = slice(t * P, (t + 1) * P)
                    three(sk[t][:, :], [midT[:, hl, tok] for hl in (HI, LO)], [fb[:, hl, :] for hl in (HI, LO)], False, True).then_inc(f_full, 1)
                pl.done("ffn_out", "batch")

            with passes(pe, pl, 0, B - 1, BATCH) as b:
                batch(b, False)
            batch(B - 1, True)

        @block.scalar
        def _(act):
            pl = Place()

            def hi_of(dst, u, bias=None):
                src = mb[pl.bank("m", u)]
                act.wait_ge(m_full, pl.at("m", u + 1))
                if bias is None:
                    nc.scalar.activation(dst, src[:, :], ACT.Copy).then_inc(m_hi, 1)
                else:
                    nc.scalar.activation(dst, src[:, :], ACT.Identity, bias=bias).then_inc(m_hi, 1)

            def h_chunks():
                for c in range(NC):
                    act.wait_ge(m_free, pl.at("m", c + 1))
                    nc.scalar.activation(hT[:, HI, c, :], hf[:, c % 2, :], ACT.Copy).then_inc(h_hi, 1)
                pl.done("hT")

            def latents():
                for m in range(NM):
                    hi_of(qcT[:, HI, m, :], m, bqd[:, m:m + 1])
                hi_of(kvT[:, HI, :], NM, bkvd)
                pl.done("latents")

            def queries(j):
                hi_of(qa[:, j % 2, HI, :], 0, qbg[:, j:j + 1])
                hi_of(q2[:, j % 2, :], 1)
                hi_of(kk[:, j % 2, HI, :], 2)
                pl.done("queries")

            def scores(j):
                for i in range(NT):
                    o, w = i * (i + 1) // 2 * P, (i + 1) * P
                    act.wait_ge(s_bias, pl.at("s", i + 1))
                    nc.scalar.activation(pr[:, j % 2, o:o + w], sk[i][:, 0:w], ACT.Exp, bias=nb[:, j % 2, i:i + 1],
                                         scale=-1.0, accum_out=sm[:, j % 2, i:i + 1]).then_inc(s_exp, 1)
                pl.done("scores")

            def turn():
                for i in range(NT):
                    w = (i + 1) * P
                    act.wait_ge(t_full, pl.at("t", i + 1))
                    nc.scalar.activation(pTv[:, HI, 0:i + 1, i * P:(i + 1) * P],
                                         tb[i % 2][:, 0:w].rearrange("p (k n) -> p k n", n=P), ACT.Copy).then_inc(t_hi, 1)
                pl.done("turn")

            def context(j):
                hi_of(cx[:, HI, j, :], 0)
                pl.done("context")

            def heads():
                scores(0)
                queries(2)
                scores(1)
                turn()
                context(0)
                queries(3)
                scores(2)
                turn()
                context(1)
                scores(3)
                turn()
                context(2)

            act.wait_ge(c_in, 4 * 16)
            nc.scalar.activation(sE[:, 0, :], sT, ACT.Exp, scale=-1.0).then_inc(silu_e, 1)
            for k in range(S0):
                nc.scalar.activation(tiny[:, k:k + 1], idf[:, k:k + 1], ACT.Copy).then_inc(s_exp, 1)

            def split(k):
                src, dst = job_parts(k)
                act.wait_ge(raw_in[k % 2], 16 * (k // 2 + 1))
                if k >= 2:
                    act.wait_ge(stg_out[k % 2], stored[k - 2])
                if ROWS <= k < ROWS + 2:
                    act.wait_ge(crow_in, k - ROWS + 1)
                nc.scalar.activation(dst[HI], src, ACT.Copy).then_inc(raw_hi, 1)

            for k in range(EARLY):
                split(k)
            pl.done("mod", "mod", "mod", "modT", "normed")
            h_chunks()
            latents()
            for h in range(NH):
                act.wait_ge(m_full, pl.at("m", 1))
                if h >= 2:
                    act.wait_ge(wps_out[h % 2], 16 * (h // 2 + 1))
                nc.scalar.activation(wps[h % 2][:, HI, :, :], mb[0][:, 0:387].rearrange("p (m n) -> p m n", m=NM)[:, :, 0:KVC],
                                     ACT.Copy).then_inc(m_hi, 1)
                act.wait_ge(m_full, pl.at("m", 2))
                if h >= 2:
                    act.wait_ge(wvs_out[h % 2], 16 * (h // 2))
                nc.scalar.activation(wvs[h % 2][:, HI, :], mb[1][:, :], ACT.Copy).then_inc(m_hi, 1)
                pl.done("absorb")
                if EARLY + h < ROWS:
                    split(EARLY + h)
            act.wait_ge(m_free, pl.at("m"))
            nc.scalar.activation(gsp[:, HI, :, :], gcol[:, :, :], ACT.Copy).then_inc(g_hi, 1)
            for k in range(ROWS, NJ):
                split(k)
            pl.done("kv_rows", "rotary")

            def batch(b, last):
                act.wait_ge(grp_ready, pl.at("grp"))
                queries(0)
                queries(1)
                heads()
                if not last:
                    pl.done("normed")
                with passes(act, pl, 1, NG, GROUP) as g:
                    pl.done("rotary")
                    turn()
                    context(3)
                    act.wait_ge(grp_ready, pl.at("grp"))
                    queries(0)
                    pl.done("project")
                    queries(1)
                    heads()
                if not last:
                    h_chunks()
                    latents()
                turn()
                context(3)
                if not last:
                    pl.done("kv_rows")
                pl.done("project", "residual")
                if not last:
                    pl.done("rotary")
                h_chunks()
                act.wait_ge(gate_max, pl.at("batch") + 1)
                nc.scalar.activation(sc[:, 1, :], sc[:, 0, :], ACT.Exp).then_inc(gate_exp, 1)
                pl.done("experts")
                for k in range(2):
                    act.wait_ge(t_full, pl.at("t", k + 1))
                    nc.scalar.activation(midT[:, HI, k * 256:(k + 1) * 256], tb[k][:, 0:256], ACT.Copy).then_inc(t_hi, 1)
                pl.done("turn_mid", "ffn_out", "batch")

            with passes(act, pl, 0, B - 1, BATCH) as b:
                batch(b, False)
            batch(B - 1, True)

        @block.vector
        def _(dve):
            pl = Place()

            def carry():
                nc.vector.tensor_copy(tiny2[:, 2:3], tiny2[:, 0:1])

            def lo_of(dst, hi, u, h, bias=None, rows=slice(0, P)):
                src = mb[pl.bank("m", u)][rows, :]
                dve.wait_ge(m_hi, pl.at("hi", h + 1))
                if bias is None:
                    nc.vector.tensor_tensor(dst, src, hi, ALU.subtract).then_inc(m_free, 1)
                else:
                    nc.vector.scalar_tensor_tensor(out=dst, in0=src, scalar=bias, in1=hi,
                                                   op0=ALU.add, op1=ALU.subtract).then_inc(m_free, 1)

            def h_chunks(half):
                for c in range(NC):
                    dve.wait_ge(m_full, pl.at("m", c + 1))
                    if not (isinstance(pl.at("h"), int) and pl.at("h") + c < 2):
                        dve.wait_ge(h_lo, pl.at("h", c - 1))
                    o = 2 * NC * half + c
                    nc.vector.tensor_scalar(hf[:, c % 2, :], mb[pl.bank("m", c)][:, :], modb[:, o + NC:o + NC + 1],
                                            modb[:, o:o + 1], ALU.mult, ALU.add).then_inc(m_free, 1)
                pl.done("hT")

            def latents():
                for m in range(NM):
                    lo_of(qcT[:, LO, m, :], qcT[:, HI, m, :], m, m, bqd[:, m:m + 1])
                lo_of(kvT[:, LO, :], kvT[:, HI, :], NM, NM, bkvd)
                pl.done("latents")

            def kv_rows():
                for hl in (HI, LO):
                    dve.wait_ge(m_full, pl.at("m", hl + 1))
                    nc.vector.tensor_copy(kvr[:, hl, :, :], mb[pl.bank("m", hl)][:, :].rearrange("p (t n) -> p t n", t=NT)).then_inc(m_free, 1)
                pl.done("kv_rows")

            def rotary(g):
                half = RD // 2
                for t in range(NT):
                    for k in range(2):
                        u = 2 * t + k
                        dve.wait_ge(m_full, pl.at("m", u + 1))
                        if not (isinstance(pl.at("ab"), int) and pl.at("ab") + u < 2):
                            dve.wait_ge(rotated, pl.at("ab", u - 1))
                        ps = mb[pl.bank("m", u)]
                        v = ps[:, 0:KW].rearrange("p (j n) -> p j n", n=RD)
                        a, r = (ab[:, u % 2, i, :].rearrange("p (j n) -> p j n", n=RD) for i in (0, 1))
                        nc.vector.tensor_tensor(a, v, cost[:, t, :].unsqueeze(1).broadcast_to([P, GH, RD]), ALU.mult)
                        nc.vector.tensor_tensor(r[:, :, 0:half], v[:, :, half:RD],
                                                sint[:, t, 0:half].unsqueeze(1).broadcast_to([P, GH, half]), ALU.mult)
                        if k == 0:
                            nc.vector.tensor_scalar(cb[:, t, :], ps[:, KW:QW], -SCALE, None, ALU.mult)
                        nc.vector.tensor_tensor(r[:, :, half:RD], v[:, :, 0:half],
                                                sint[:, t, half:RD].unsqueeze(1).broadcast_to([P, GH, half]), ALU.mult).then_inc(m_free, 1)
                nc.vector.tensor_copy(qbg[:, :], qbias[:, bass.ds(g * GH, GH)]).then_inc(grp_ready, 1)
                pl.done("rotary")

            def queries(j):
                lo_of(qa[:, j % 2, LO, :], qa[:, j % 2, HI, :], 0, 0, qbg[:, j:j + 1])
                low = slice(RD, P)
                lo_of(q2[low, j % 2, :], q2[low, j % 2, :], 1, 1, rows=low)
                lo_of(kk[:, j % 2, LO, :], kk[:, j % 2, HI, :], 2, 2)
                pl.done("queries")

            def reciprocal(j, i, since):
                dve.wait_ge(s_exp, pl.at("s", S0 + i + 1 - since))
                nc.vector.reciprocal(rsm[:, j % 2, i:i + 1], sm[:, j % 2, i:i + 1]).then_inc(s_rec, 1)

            def scores(j):
                for i in range(NT):
                    w = (i + 1) * P
                    ps = sk[i][:, 0:w]
                    dve.wait_ge(s_full, pl.at("s", i + 1))
                    carry()
                    nc.vector.tensor_tensor_reduce(ps, ps, maskt[:, S - w:S], -SCALE, 3.0e38, ALU.add, ALU.min,
                                                   nmx[:, j % 2, i:i + 1]).then_inc(s_min, 1)
                    dve.wait_ge(s_min, pl.at("s", i + 1))
                    nc.vector.tensor_scalar(nb[:, j % 2, i:i + 1], nmx[:, j % 2, i:i + 1], cb[:, i, j:j + 1],
                                            cb[:, i, j:j + 1], ALU.add, ALU.subtract).then_inc(s_bias, 1)
                    if i:
                        reciprocal(j, i - 1, 0)
                pl.done("scores")
                reciprocal(j, NT - 1, NT)

            def turn():
                for i in range(NT):
                    w = (i + 1) * P
                    dve.wait_ge(t_hi, pl.at("t", i + 1))
                    at = (slice(0, i + 1), slice(i * P, (i + 1) * P))
                    nc.vector.tensor_tensor(pTv[:, LO, at[0], at[1]], tb[i % 2][:, 0:w].rearrange("p (k n) -> p k n", n=P),
                                            pTv[:, HI, at[0], at[1]], ALU.subtract).then_inc(t_free, 1)
                pl.done("turn")

            def context(j):
                lo_of(cx[:, LO, j, :], cx[:, HI, j, :], 0, 0)
                pl.done("context")

            def heads():
                scores(0)
                queries(2)
                scores(1)
                turn()
                context(0)
                queries(3)
                scores(2)
                turn()
                context(1)
                scores(3)
                turn()
                context(2)

            steps = [0, 0]

            def step(ins):
                ins.then_inc(ln_step, 1)
                steps[0] += 1
                dve.wait_ge(ln_step, pl.at("ln", steps[0]))

            def normed(loads):
                dve.wait_ge(x_in, loads)
                steps[0] = 0
                for t in range(NT):
                    ins = nc.vector.bn_stats(stats[:, t, :], xn[:, t, :])
                step(ins)
                carry()
                for t in range(NT):
                    ins = nc.vector.bn_aggr(mv[:, t, :], stats[:, t, :])
                step(ins)
                nc.vector.tensor_scalar(ve[:, :], mv[:, :, 1], EPS, None, ALU.add).then_inc(ln_var, 1)
                dve.wait_ge(ln_rstd, pl.at("var", 1))
                for t in range(NT):
                    ins = nc.vector.tensor_scalar(xn[:, t, :], xn[:, t, :], mv[:, t, 0:1], rstd[:, t:t + 1], ALU.subtract, ALU.mult)
                ins.then_inc(ln_xn, 1)
                pl.done("normed")

            def project(first):
                dve.wait_ge(acc_in, pl.at("batch") * 16 + 16)
                dve.wait_ge(m_free, pl.at("m"))
                for t in range(NT):
                    dve.wait_ge(m_full, pl.at("m", t + 1))
                    nc.vector.tensor_tensor(acc[:, t, :], mb[pl.bank("m", t)][:, :], acc[:, t, :], ALU.add).then_inc(m_free, 1)

            def residual(b, x_loads):
                dve.wait_ge(gab_in, pl.at("batch") * 16 + 16)
                dve.wait_ge(x_in, x_loads)
                dve.wait_ge(acc_in, pl.at("batch") * 16 + 16)
                dve.wait_ge(m_free, pl.at("m"))
                steps[0] = 0

                def norm(t):
                    dve.wait_ge(ln_rstd, pl.at("var", t + 1))
                    nc.vector.tensor_scalar(xn[:, t, :], acc[:, t, :], mv[:, t, 0:1], rstd[:, t:t + 1],
                                            ALU.subtract, ALU.mult).then_inc(ln_xn, 1)

                for t in range(NT):
                    a = acc[:, t, :]
                    dve.wait_ge(m_full, pl.at("m", t + 1))
                    nc.vector.tensor_tensor(a, mb[pl.bank("m", t)][:, :], a, ALU.add).then_inc(m_free, 1)
                    dve.wait_ge(m_free, pl.at("m", t + 1))
                    step(nc.vector.tensor_tensor(a, a, gab[:, 0, :], ALU.mult))
                    step(nc.vector.tensor_tensor(a, a, xn[:, t, :], ALU.add))
                    step(nc.vector.bn_stats(stats[:, t, :], a))
                    carry()
                    step(nc.vector.bn_aggr(mv[:, t, :], stats[:, t, :]))
                    nc.vector.tensor_scalar(ve[:, t:t + 1], mv[:, t, 1:2], EPS, None, ALU.add).then_inc(ln_var, 1)
                    if t:
                        norm(t - 1)
                norm(NT - 1)
                assert steps[0] == 4 * NT
                pl.done("project", "residual")

            def experts():
                for t in range(NT):
                    dve.wait_ge(m_full, pl.at("m", t + 1))
                    nc.vector.tensor_copy(mid[:, t, :], mb[pl.bank("m", t)][:, 0:FW]).then_inc(m_free, 1)
                dve.wait_ge(m_free, pl.at("m", NT))
                steps[1] = 0

                def gstep(ins):
                    ins.then_inc(gate_step, 1)
                    steps[1] += 1
                    dve.wait_ge(gate_step, pl.at("gate", steps[1]))

                def tile(i):
                    return sc[:, i, :].rearrange("p (t e) -> p t e", t=NT)

                def per_row(i):
                    return sc[:, i, 0:NT]

                def spread(ap, n=NE):
                    return ap.unsqueeze(2).broadcast_to([P, NT, n])

                logits = mid[:, :, NE * R:FW]
                gstep(nc.vector.tensor_reduce(per_row(2), logits, AX.X, ALU.max))
                nc.vector.tensor_tensor(tile(0), logits, spread(per_row(2)), ALU.subtract).then_inc(gate_max, 1)
                dve.wait_ge(gate_exp, pl.at("batch") + 1)
                gstep(nc.vector.tensor_reduce(per_row(3), tile(1), AX.X, ALU.add))
                gstep(nc.vector.reciprocal(per_row(4), per_row(3)))
                gstep(nc.vector.tensor_tensor(tile(5), tile(1), spread(per_row(4)), ALU.mult))
                carry()
                for t in range(NT):
                    ins = nc.vector.max(v8[:, t, :], tile(5)[:, t, :])
                gstep(ins)
                carry()
                for t in range(NT):
                    ins = nc.vector.max_index(i8[:, t, :], v8[:, t, :], tile(5)[:, t, :])
                gstep(ins)
                gstep(nc.vector.tensor_tensor(per_row(2), v8[:, :, 0], v8[:, :, 1], ALU.add))
                gstep(nc.vector.reciprocal(per_row(3), per_row(2)))
                w = sc[:, 4, 0:2 * NT].rearrange("p (t e) -> p t e", e=2)
                ix = sc[:, 6, 0:2 * NT].rearrange("p (t e) -> p t e", e=2)
                gstep(nc.vector.scalar_tensor_tensor(out=w, in0=v8[:, :, 0:2], scalar=LORA_SCALING, in1=spread(per_row(3), 2),
                                                     op0=ALU.mult, op1=ALU.mult))
                gstep(nc.vector.tensor_copy(ix, i8[:, :, 0:2]))
                io = iotat.unsqueeze(1).broadcast_to([P, NT, NE])
                gstep(nc.vector.tensor_tensor(tile(0), io, spread(ix[:, :, 0]), ALU.is_equal))
                gstep(nc.vector.tensor_tensor(tile(1), tile(0), spread(w[:, :, 0]), ALU.mult))
                gstep(nc.vector.tensor_tensor(tile(5), io, spread(ix[:, :, 1]), ALU.is_equal))
                gstep(nc.vector.tensor_tensor(tile(7), tile(5), spread(w[:, :, 1]), ALU.mult))
                gstep(nc.vector.tensor_tensor(tile(0), tile(1), tile(7), ALU.add))
                assert steps[1] == Place.STAGES["experts"]["gate"], steps[1]
                pl.done("experts")

            nc.vector.memset(nhalf[:, :], -0.5)
            nc.vector.memset(brow[:, :].bitcast(F32), 0.0).then_inc(zeroed, 1)
            for k in range(T0):
                nc.vector.memset(tiny2[:, k:k + 1], 0.0).then_inc(t_free, 1)

            def link(ins, n):
                ins.then_inc(set_step, 1)
                dve.wait_ge(set_step, n)

            dve.wait_ge(silu_e, 1)
            link(nc.vector.tensor_scalar(sE[:, 1, :], sE[:, 0, :], 1.0, None, ALU.add), 1)
            link(nc.vector.reciprocal(sE[:, 0, :], sE[:, 1, :]), 2)
            nc.vector.tensor_tensor(sT, sT, sE[:, 0, :], ALU.mult).then_inc(silu_done, 1)
            dve.wait_ge(c_in, 4 * 16)
            nc.vector.tensor_copy(selr[:, :, :], selt.rearrange("p (k n) -> p k n", k=3)).then_inc(sel_ready, 1)

            def split(k):
                src, dst = job_parts(k)
                dve.wait_ge(raw_hi, k + 1)
                nc.vector.tensor_tensor(dst[LO], src, dst[HI], ALU.subtract).then_inc(raw_lo, 1)

            for k in range(EARLY):
                split(k)
            dve.wait_ge(zeroed, 1)
            dve.wait_ge(raw_lo, EARLY)
            g1, g2 = mrow[:, 0:HID], mrow[:, HID:2 * HID]
            for k in range(6):
                dve.wait_ge(m_full, k + 1)
                ps = mb[k % 2][0:B, :]
                if k in (2, 5):
                    n = 3 + 3 * (k // 3)
                    link(nc.vector.tensor_scalar(g1, ps, -1.0, 0.25, ALU.mult, ALU.max), n)
                    link(nc.vector.scalar_tensor_tensor(out=g1, in0=ps, scalar=0.25, in1=g1, op0=ALU.max, op1=ALU.max), n + 1)
                    nc.vector.tensor_scalar(g2, ps, 0.0, 2.0, ALU.is_ge, ALU.mult).then_inc(m_free, 1)
                    dve.wait_ge(m_free, k + 1)
                    nc.vector.scalar_tensor_tensor(out=gab[0:B, k // 3, :], in0=g2, scalar=1.0, in1=g1,
                                                   op0=ALU.subtract, op1=ALU.mult).then_inc(set_step, 1)
                    dve.wait_ge(set_step, n + 2)
                else:
                    r = (0, 1, None, 2, 3)[k]
                    nc.vector.tensor_scalar(modrow[:, r * HID:(r + 1) * HID], ps, float(k in (1, 4)), None, ALU.add).then_inc(m_free, 1)
            pl.done("mod", "mod", "mod")
            for r in range(2):
                dve.wait_ge(m_full, pl.at("m", r + 1))
                nc.vector.tensor_copy(modT[:, 2 * NC * r:2 * NC * (r + 1), :],
                                      mb[pl.bank("m", r)][:, 0:2 * NC * B].rearrange("p (k b) -> p k b", b=B)).then_inc(m_free, 1)
            pl.done("modT")
            dve.wait_ge(m_free, pl.at("m"))
            nc.vector.tensor_copy(modb[:, :], modT[:, :, 0]).then_inc(mod_b, 1)
            normed(16)
            dve.wait_ge(mod_b, 1)
            h_chunks(0)
            latents()
            for h in range(NH):
                dve.wait_ge(m_hi, pl.at("hi", 1))
                pv = mb[0][:, 0:387].rearrange("p (m n) -> p m n", m=NM)
                nc.vector.tensor_tensor(wps[h % 2][:, LO, :, :], pv[:, :, 0:KVC], wps[h % 2][:, HI, :, :], ALU.subtract)
                nc.vector.tensor_copy(gcol[:, :, h:h + 1], pv[:, :, KVC:KVC + 1])
                nc.vector.tensor_copy(crow[0:1, h:h + 1], mb[0][0:1, 391:392])
                nc.vector.tensor_copy(qbias[:, h:h + 1], mb[0][:, 390:391]).then_inc(m_free, 1)
                dve.wait_ge(m_hi, pl.at("hi", 2))
                nc.vector.tensor_tensor(wvs[h % 2][:, LO, :], mb[1][:, :], wvs[h % 2][:, HI, :], ALU.subtract).then_inc(m_free, 1)
                pl.done("absorb")
                if EARLY + h < ROWS:
                    split(EARLY + h)
            dve.wait_ge(bias_full, 1)
            nc.vector.tensor_copy(bias_s[:, :], sk[0][0:1, :]).then_inc(bias_ev, 1)
            dve.wait_ge(m_free, pl.at("m"))
            dve.wait_ge(g_hi, 1)
            nc.vector.tensor_tensor(gsp[:, LO, :, :], gcol[:, :, :], gsp[:, HI, :, :], ALU.subtract).then_inc(g_lo, 1)
            for k in range(ROWS, ROWS + 2):
                dve.wait_ge(raw_in[k % 2], 16 * (k // 2 + 1))
                h0 = 2 * GH * (k - ROWS)
                nc.vector.tensor_copy(raw[k % 2][0:1, 0:2 * QW].rearrange("p (g n) -> p g n", g=2)[:, :, KW:QW],
                                      crow[0:1, h0:h0 + 2 * GH].rearrange("p (g n) -> p g n", g=2)).then_inc(crow_in, 1)
            for k in range(ROWS, NJ):
                split(k)
            kv_rows()
            rotary(0)

            def batch(b, last):
                dve.wait_ge(grp_ready, pl.at("grp"))
                queries(0)
                queries(1)
                heads()
                if not last:
                    normed(pl.at("batch") * 32 + 32)
                with passes(dve, pl, 1, NG, GROUP) as g:
                    rotary(g)
                    turn()
                    context(3)
                    dve.wait_ge(grp_ready, pl.at("grp"))
                    queries(0)
                    project(False)
                    pl.done("project")
                    queries(1)
                    heads()
                if not last:
                    nc.vector.tensor_copy(modb[:, 0:2 * NC], modT[:, 0:2 * NC, b + 1])
                nc.vector.tensor_copy(modb[:, 2 * NC:4 * NC], modT[:, 2 * NC:4 * NC, b]).then_inc(mod_b, 1)
                dve.wait_ge(mod_b, pl.at("batch") + 2)
                if not last:
                    h_chunks(0)
                    latents()
                turn()
                context(3)
                if not last:
                    kv_rows()
                residual(b, pl.at("batch") * 32 + (32 if last else 48))
                if not last:
                    rotary(0)
                h_chunks(1)
                experts()
                for k in range(2):
                    dve.wait_ge(t_hi, pl.at("t", k + 1))
                    at = slice(k * 256, (k + 1) * 256)
                    nc.vector.tensor_tensor(midT[:, LO, at], tb[k][:, 0:256], midT[:, HI, at], ALU.subtract).then_inc(t_free, 1)
                pl.done("turn_mid")
                for t in range(NT):
                    dve.wait_ge(f_full, pl.at("y", t + 1))
                    nc.vector.tensor_tensor(xn[:, t, :], sk[t][:, :], gab[:, 1, :], ALU.mult).then_inc(y_mul, 1)
                    dve.wait_ge(y_mul, pl.at("y", t + 1))
                    nc.vector.tensor_tensor(xn[:, t, :], xn[:, t, :], acc[:, t, :], ALU.add).then_inc(y_done, 1)
                pl.done("ffn_out", "batch")

            with passes(dve, pl, 0, B - 1, BATCH) as b:
                batch(b, False)
            batch(B - 1, True)

        @block.gpsimd
        def _(pool):
            pl = Place()

            def h_chunks():
                for c in range(NC):
                    pool.wait_ge(h_hi, pl.at("h", c + 1))
                    nc.gpsimd.tensor_tensor(hT[:, LO, c, :], hf[:, c % 2, :], hT[:, HI, c, :], ALU.subtract).then_inc(h_lo, 1)
                pl.done("hT")

            def rotary():
                for u in range(2 * NT):
                    pool.wait_ge(m_free, pl.at("m", u + 1))
                    a, r = (ab[:, u % 2, i, :].rearrange("p (j n) -> p j n", n=RD) for i in (0, 1))
                    o = rq[:, u % 2, u // 2, :].rearrange("p (j d n) -> p j d n", d=2, n=RD)
                    for d in range(2):
                        ins = nc.gpsimd.tensor_tensor(o[:, :, d, :], a, r, ALU.add)
                    ins.then_inc(rotated, 1)
                pl.done("rotary")

            def scores(j):
                for i in range(NT):
                    o, w = i * (i + 1) // 2 * P, (i + 1) * P
                    pool.wait_ge(s_rec, pl.at("s", i + 1))
                    nc.gpsimd.tensor_tensor(pr[:, j % 2, o:o + w], pr[:, j % 2, o:o + w],
                                            rsm[:, j % 2, i:i + 1].broadcast_to([P, w]), ALU.mult).then_inc(p_norm, 1)
                pl.done("scores")

            def heads():
                scores(0)
                pl.done("queries")
                scores(1)
                pl.done("turn", "context", "queries")
                scores(2)
                pl.done("turn", "context")
                scores(3)
                pl.done("turn", "context")

            def rstd_of(k, n, at):
                pool.wait_ge(ln_var, at)
                nc.gpsimd.tensor_tensor(rstd[:, k:k + n], ve[:, k:k + n], nhalf[:, k:k + n], ALU.pow).then_inc(ln_rstd, 1)

            def load(k):
                src, rows, n, a, _, _ = JOBS[k]
                dst = raw[k % 2][0:rows, 0:n]
                pool.dma_start(v3(dst, a) if a > 1 else dst, src).then_inc(raw_in[k % 2], 16)

            def store(k):
                pool.wait_ge(raw_lo, k + 1)
                for dst, hl, a, n in JOBS[k][5]:
                    pool.dma_start(dst, v3(stg[k % 2][0:JOBS[k][1], hl, 0:n].bitcast(F32), a)).then_inc(stg_out[k % 2], 16)

            load(0)
            load(1)
            pool.wait_ge(raw_lo, 1)
            load(2)
            pool.wait_ge(zeroed, 1)
            for k in range(2):
                pool.wait_ge(set_step, 5 + 3 * k)
                pool.dma_start(gate_d[:, k, :], gab[0:B, k, :]).then_inc(gate_out, 16)
            rstd_of(0, NT, 1)
            pool.wait_ge(m_full, 8)
            load(3)
            pl.done("mod", "mod", "mod", "modT", "normed")
            h_chunks()
            pool.wait_ge(h_lo, NC)
            load(4)
            pl.done("latents")
            for h in range(NH):
                pool.wait_ge(m_free, pl.at("m", 1))
                src = wps[h % 2].bitcast(F32).rearrange("p k m n -> p (k m n)")
                pool.dma_start(wp_d[h], src).then_inc(wps_out[h % 2], 16)
                if h < 2:
                    pool.dma_start(wp_d[NH + h], src).then_inc(wps_out[h % 2], 16)
                pool.wait_ge(m_free, pl.at("m", 2))
                pool.dma_start(wvo_d[h], wvs[h % 2].bitcast(F32).rearrange("p k n -> p (k n)")).then_inc(wvs_out[h % 2], 16)
                pl.done("absorb")
                k = EARLY + h
                if k < ROWS:
                    store(k)
                    load(k + 2)
            pool.wait_ge(g_lo, 1)
            for hl in (HI, LO):
                for m in range(NM):
                    src = gsp[:, hl, m, :].bitcast(F32)
                    pool.dma_start(wr_d[0:NG, :, hl, m, KW:QW].rearrange("g p n -> p g n"), v3(src, NG)).then_inc(gcol_out, 16)
                    pool.dma_start(wr_d[NG, :, hl, m, KW:QW], src[:, 0:GH]).then_inc(gcol_out, 16)
            for k in range(ROWS, NJ):
                store(k)
                if k + 2 < NJ:
                    load(k + 2)
            pl.done("kv_rows")
            rotary()

            def batch(b, last):
                pl.done("queries", "queries")
                heads()
                if not last:
                    rstd_of(0, NT, pl.at("var", 1))
                    pl.done("normed")
                with passes(pool, pl, 1, NG, GROUP) as g:
                    rotary()
                    pl.done("turn", "context", "queries", "project", "queries")
                    heads()
                if not last:
                    h_chunks()
                    pl.done("latents")
                pl.done("turn", "context")
                if not last:
                    pl.done("kv_rows")
                for t in range(NT):
                    rstd_of(t, 1, pl.at("var", t + 1))
                pl.done("project", "residual")
                if not last:
                    rotary()
                h_chunks()
                pool.wait_ge(gate_step, pl.at("gate", Place.STAGES["experts"]["gate"]))
                gate = sc[:, 0, :].rearrange("p (t e) -> p t e", t=NT).unsqueeze(3).broadcast_to([P, NT, NE, R])
                nc.gpsimd.tensor_tensor(midg.rearrange("p t (e r) -> p t e r", r=R), mid[:, :, 0:NE * R].rearrange("p t (e r) -> p t e r", r=R),
                                        gate, ALU.mult).then_inc(mid_gated, 1)
                pl.done("experts", "turn_mid", "ffn_out", "batch")

            with passes(pool, pl, 0, B - 1, BATCH) as b:
                batch(b, False)
            batch(B - 1, True)


def constants():
    ident = np.eye(P, dtype=np.float32)
    mask = np.zeros((P, S), np.float32)
    mask[:, S - P:] = np.where(np.arange(P)[None, :] > np.arange(P)[:, None], np.float32(-1e30), np.float32(0))
    power = np.power(10000.0, (np.arange(0, RD, 2, dtype=np.float32) / np.float32(RD)).astype(np.float64)).astype(np.float32)
    inv_freq = np.float32(1) / power
    ang = (np.arange(S, dtype=np.float32)[:, None] * inv_freq[None, :]).astype(np.float64)
    c, s = np.cos(ang).astype(np.float32), np.sin(ang).astype(np.float32)
    tiles = [np.concatenate(h, 1).reshape(NT, P, RD).transpose(1, 0, 2).reshape(P, NT * RD) for h in ((c, c), (-s, s))]
    iota = np.tile(np.arange(NE, dtype=np.float32), (P, 1))
    sel = np.zeros((P, 3, P), np.float32)
    for k in range(3):
        sel[2 * k:2 * k + 2, k, :] = 1
    return np.concatenate([ident, mask, *tiles, iota, sel.reshape(P, 3 * P)], 1)


def kernel(**inputs):
    import concourse.bacc as bacc
    from concourse.bass_utils import run_bass_kernel_spmd

    a = {n: np.asarray(v) for n, v in inputs.items()}
    at, ff = "L0_attn_", "L0_ffn_"

    def by_head(b):
        return b.reshape(NH, HD).T

    laid = {
        "x": a[at + "x"],
        "inputs": np.concatenate([a["L0_c"].T.reshape(NC, P, B).transpose(1, 0, 2).reshape(P, NC * B),
                                  a[at + "b_qd"].reshape(NM, P).T, a[at + "b_kvd"].reshape(P, 1),
                                  by_head(a[at + "b_qu"]), by_head(a[at + "b_ku"]), by_head(a[at + "b_vu"])], 1),
        "consts": constants(),
        "b_o": a[at + "b_o"].reshape(1, HID),
        "wmod": a["L0_wmod"],
        "w_qd": a[at + "W_qd"],
        "w_kvd": a[at + "W_kvd"],
        "heads_w": np.concatenate([a[at + "W_qu"].T, a[at + "W_ku"].T, a[at + "b_ku"].reshape(NH * HD, 1),
                                   a[at + "W_vu"].T, a[at + "W_o"]], 1),
        "w_qr": a[at + "W_qr"],
        "w_kr": a[at + "W_kr"],
        "base_wT": a[ff + "base_w"].T,
        "ffn_a": np.concatenate([a[ff + "lora_A"].transpose(1, 0, 2).reshape(HID, NE * R), a[ff + "router_w"].T], 1),
        "ffn_b": a[ff + "lora_B"].reshape(NE * R, HID),
        "q_row": np.concatenate([a[at + "b_qr"].reshape(NG, KW), np.zeros((NG, GH), np.float32)], 1).reshape(1, NG * QW),
        "k_row": a[at + "b_kr"].reshape(1, NG * KW),
        "f_row": np.concatenate([a[ff + "base_b"], np.zeros(NE * R, np.float32), a[ff + "router_b"]]).reshape(1, HID + FW),
    }
    nc = bacc.Bacc("TRN2", target_bir_lowering=False, num_devices=1)
    arrays, args = {}, []
    for name, v in laid.items():
        v = np.ascontiguousarray(v)
        arrays[f"in_{name}"] = v
        args.append(nc.dram_tensor(f"in_{name}", v.shape, mybir.dt.from_np(v.dtype), kind="ExternalInput").ap())
    args.append(nc.dram_tensor("out_y", (B, S, HID), F32, kind="ExternalOutput").ap())
    build(nc, *args)
    r = run_bass_kernel_spmd(nc, [arrays], core_ids=[0])
    return r.results[0]["out_y"]
```

```python
from contextlib import ExitStack, contextmanager

import numpy as np
import concourse.bass as bass
from concourse import mybir

ALU = mybir.AluOpType
ACT = mybir.ActivationFunctionType
AX = mybir.AxisListType
F32 = mybir.dt.float32
F32R = mybir.dt.float32r
U32 = mybir.dt.uint32

P = 128
B, S, HID = 8, 512, 512
NH, HD, RD = 16, 128, 64
KVC, QC = 128, 384
NE, R = 8, 16
LORA_SCALING = 2.0
EPS = 1e-5
NT = S // P
NC = HID // P
NM = QC // P
GH = 4
NG = NH // GH
QW = GH * RD + GH
KW = GH * RD
FW = NE * R + NE
SCALE = 1.0 / float(np.sqrt(HD + RD))
HI, LO = 0, 1


class Count:

    def __init__(self):
        self.base, self.off = 0, 0
        self.seen = 0

    def at(self, more=0):
        return self.base + (self.off + more)

    def add(self, n=1):
        self.off += n
        self.seen += n


class Place:

    STAGES = {
        "one": dict(m=1),
        "hi": dict(hi=2),
        "mod": dict(m=2),
        "modT": dict(m=2),
        "absorb": dict(m=2, hi=2),
        "normed": dict(var=1, xn=1),
        "feature": dict(m=1, hi=1, h=1),
        "latent": dict(m=1, hi=1),
        "kv_row": dict(m=1),
        "rotate": dict(m=1, ab=1),
        "group": dict(grp=1),
        "query": dict(m=1, hi=1, qm=1),
        "rope": dict(m=1, hi=1),
        "score": dict(s=1),
        "turn": dict(t=1),
        "context": dict(m=1, hi=1),
        "project": dict(m=1),
        "projected": dict(pg=1),
        "residual": dict(var=1, xn=1),
        "step": dict(ln=1),
        "expert": dict(m=1),
        "gate_step": dict(gate=1),
        "turn_mid": dict(t=1),
        "ffn_out": dict(y=1),
        "batch": dict(batch=1),
    }
    NAMES = ("m", "hi", "h", "ab", "grp", "qm", "pg", "s", "t", "var", "xn", "ln", "gate", "y", "batch")

    def __init__(self):
        self.c = {n: Count() for n in self.NAMES}
        self.marks = {}
        self.open = []

    def at(self, name, more=0):
        return self.c[name].at(more)

    def bank(self, name, more=0):
        return (self.c[name].seen + more) % 2

    def mark(self, key, name):
        self.marks[key] = (name, self.c[name].seen)
        for own, _ in self.open:
            own.add(key)

    def since(self, key, more=0):
        name, seen = self.marks[key]
        for own, read in self.open:
            if key not in own:
                read.add(key)
        return self.at(name, seen - self.c[name].seen + more)

    def done(self, *stages):
        for stage in stages:
            for name, n in self.STAGES[stage].items():
                self.c[name].add(n)


GATE_STEPS = 15
GROUP = dict(turn=GH * NT, score=GH * NT, context=GH, query=GH, rope=2 * GH, rotate=2 * NT, group=1, project=NT, projected=1)
BATCH = dict(turn=NH * NT, score=NH * NT, context=NH, query=NH, rope=2 * NH, rotate=NG * 2 * NT, group=NG, project=NG * NT,
             projected=NG, normed=1, feature=2 * NC, latent=NM + 1, kv_row=2, residual=NT, step=4 * NT + 2, expert=NT,
             gate_step=GATE_STEPS, turn_mid=2, ffn_out=NT, batch=1)


@contextmanager
def passes(eng, place, lo, hi, stages):
    per = {n: sum(k * Place.STAGES[stage].get(n, 0) for stage, k in stages.items()) for n in Place.NAMES}
    assert per["m"] % 2 == 0 and per["t"] % 2 == 0 and per["ab"] % 2 == 0
    before = {n: c.at() for n, c in place.c.items()}
    seen = {n: c.seen for n, c in place.c.items()}
    ago = {key: seen[n] - at for key, (n, at) in place.marks.items()}
    place.open.append((set(), set()))
    with eng.Fori(lo, hi) as i:
        for n, c in place.c.items():
            c.base, c.off = (before[n] + (i - lo) * per[n] if per[n] else before[n]), 0
        yield i
        short = {n: (c.seen - seen[n], per[n]) for n, c in place.c.items() if c.seen - seen[n] not in (0, per[n])}
        assert not short, short
        skipped = {n for n, c in place.c.items() if c.seen == seen[n]}
    own, read = place.open.pop()
    for key in read:
        n, at = place.marks[key]
        assert place.c[n].seen - at == ago[key], key
    for n, c in place.c.items():
        n_all = 0 if n in skipped else (hi - lo) * per[n]
        c.base, c.off, c.seen = before[n] + n_all, 0, seen[n] + n_all
    for key in own:
        n, at = place.marks[key]
        place.marks[key] = (n, at + (hi - lo - 1) * per[n])


def build(nc, x, inputs, consts, b_o, wmod, w_qd, w_kvd, heads_w, w_qr, w_kr, base_wT, ffn_a, ffn_b,
          q_row, k_row, f_row, out):
    with ExitStack() as ctx:
        def sb(name, shape, dt=F32):
            return ctx.enter_context(nc.sbuf_tensor(name, shape, dt))

        def sem(name):
            return ctx.enter_context(nc.semaphore(name))

        wqd = sb("wqd", [P, 2, NC, QC], F32R)
        wkvd = sb("wkvd", [P, 2, NC, KVC], F32R)
        wk = sb("wk", [P, 2, NG * KW], F32R)
        wp = sb("wp", [P, 2, 2, NM, KVC], F32R)
        wvo = sb("wvo", [P, 2 * GH * HID], F32R)
        wr = sb("wr", [P, 2, NM, QW], F32R)
        brow = sb("brow", [P, NG * QW], F32R)
        selr = sb("selr", [P, 3, P], F32R)
        cst = sb("cst", [P, P + S + 2 * NT * RD + NE])
        idf = cst[:, 0:P]
        maskt = cst[:, P:P + S]
        cost = cst[:, P + S:P + S + NT * RD].rearrange("p (t n) -> p t n", t=NT)
        sint = cst[:, P + S + NT * RD:P + S + 2 * NT * RD].rearrange("p (t n) -> p t n", t=NT)
        iotat = cst[:, P + S + 2 * NT * RD:]
        inp = sb("inp", [P, NC * B + NM + 1 + 3 * NH])
        sT = inp[:, 0:NC * B]
        bqd = inp[:, NC * B:NC * B + NM]
        bkvd = inp[:, NC * B + NM:NC * B + NM + 1]
        bqu = inp[:, NC * B + NM + 1:].rearrange("p (k h) -> p k h", k=3)
        qbias = sb("qbias", [P, NH])
        qbg = sb("qbg", [P, GH])
        modT = sb("modT", [P, 4 * NC, B])
        modb = sb("modb", [P, 4 * NC])
        nhalf = sb("nhalf", [P, NT])
        tiny = sb("tiny", [P, 4])
        tiny2 = sb("tiny2", [P, 7])
        xn = sb("xn", [P, NT, HID])
        acc = sb("acc", [P, NT, HID])
        gab = sb("gab", [P, 2, HID])
        hT = sb("hT", [P, 2, NC, S], F32R)
        qcT = sb("qcT", [P, 2, NM, S], F32R)
        kvT = sb("kvT", [P, 2, S], F32R)
        kvr = sb("kvr", [P, 2, NT, KVC], F32R)
        NR = 2 * NT * GH * 2 * RD
        rr = sb("rr", [P, NR + 4 * KW])
        rq = rr[:, 0:NR].rearrange("p (k t n) -> p k t n", k=2, t=NT)
        ab = rr[:, NR:NR + 4 * KW].rearrange("p (s k n) -> p s k n", s=2, k=2)
        cb = sb("cb", [P, NT, GH])
        cbn = sb("cbn", [P, NT, GH])
        qa = sb("qa", [P, 2, 2, S], F32R)
        q2 = sb("q2", [P, 2, S], F32R)
        kk = sb("kk", [P, 2, 2, S], F32R)
        NP_ = NT * (NT + 1) // 2 * P
        pr = sb("pr", [P, 2, NP_])
        pT = sb("pT", [P, 2 * NT * S], F32R)
        cxT = sb("cxT", [P, 2 * GH * S], F32R)
        nmx = sb("nmx", [P, 2, NT])
        nb = sb("nb", [P, 2, NT])
        sm = sb("sm", [P, 2, NT])
        rsm = sb("rsm", [P, 2, NT])
        stats = sb("stats", [P, NT, 6])
        mv = sb("mv", [P, NT, 2])
        ve = sb("ve", [P, NT])
        rstd = sb("rstd", [P, NT])
        sc = sb("sc", [P, 8, NT * NE])
        v8 = sb("v8", [P, NT, NE])
        i8 = sb("i8", [P, NT, NE], U32)
        gcol = sb("gcol", [P, NM, NH])
        gsp = sb("gsp", [P, 2, NM, NH], F32R)
        crow = sb("crow", [1, NH])
        sE = sb("sE", [P, 2, NC * B])
        bo_t = sb("bo_t", [1, HID])
        bias_s = sb("bias_s", [1, HID])

        pTv = pT[:, :].rearrange("p (k j s) -> p k j s", k=2, j=NT)
        cx = cxT[:, :].rearrange("p (k j s) -> p k j s", k=2, j=GH)
        wvov = wvo[:, :].rearrange("p (j k n) -> p j k n", j=GH, k=2)
        basew = pT[:, :].rearrange("p (k c n) -> p k c n", k=2, c=NC)
        NF = NC * FW + HID
        ffw = cxT[:, 0:2 * NF].rearrange("p (k n) -> p k n", k=2)
        fa = ffw[:, :, 0:NC * FW].rearrange("p k (c n) -> p k c n", c=NC)
        fb = ffw[:, :, NC * FW:NF]
        midT = cxT[:, 2 * NF:2 * NF + 2 * S].rearrange("p (k n) -> p k n", k=2)
        mid = pr[:, 1, 0:NT * FW].rearrange("p (t n) -> p t n", t=NT)
        midg = pr[:, 1, 640:640 + NT * P].rearrange("p (t n) -> p t n", t=NT)
        HEADW = QC + KVC + 1 + KVC + HID
        hw = [rr[:, k * 1160:k * 1160 + HEADW] for k in range(2)]
        modw = [acc[:, :, :], rr[:, 2320:2320 + NC * HID].rearrange("p (c n) -> p c n", c=NC)]
        selt = rr[:, 4400:4400 + 3 * P]
        modrow = pr[0:B, :, :].rearrange("p k n -> p (k n)")
        raw = [pr[:, k, :] for k in range(2)]
        wps = [pT[:, k * 768:(k + 1) * 768].rearrange("p (k m n) -> p k m n", k=2, m=NM) for k in range(2)]
        wvs = [cxT[:, k * 1024:(k + 1) * 1024].rearrange("p (k n) -> p k n", k=2) for k in range(2)]
        stg = [wvo[:, k * 2048:(k + 1) * 2048].rearrange("p (k n) -> p k n", k=2) for k in range(2)]
        mrow = rr[0:B, 0:2 * HID]

        mb = [ctx.enter_context(nc.psum_tensor(f"mb{i}", [P, 512], F32)) for i in range(2)]
        tb = [ctx.enter_context(nc.psum_tensor(f"tb{i}", [P, 512], F32)) for i in range(2)]
        sk = [ctx.enter_context(nc.psum_tensor(f"sk{i}", [P, 512], F32)) for i in range(NT)]

        def scratch(name, shape):
            return nc.dram_tensor(name, shape, F32, kind="Internal").ap()

        wp_d = scratch("wp_d", [NH + 2, P, 2 * NM * KVC])
        wvo_d = scratch("wvo_d", [NH, P, 2 * HID])
        wr_d = scratch("wr_d", [NG + 1, P, 2, NM, QW])
        base_d = scratch("base_d", [P, 2, NC * HID])
        ff_d = scratch("ff_d", [P, 2, NF])
        gate_d = scratch("gate_d", [B, 2, HID])
        bias_d = scratch("bias_d", [1, HID])
        row_d = scratch("row_d", [6, NG * QW])

        names = ("c_in x_in wvo_in wr_in base_in ff_in gab_in acc_in brow_in "
                 "gcol_out gate_out bias_out y_out "
                 "m_full m_hi m_free t_full t_hi t_free s_full s_min s_bias s_exp s_rec p_norm "
                 "h_mod rotated grp_ready ln_var ln_rstd ln_xn ln_step mod_b "
                 "gate_step gate_max gate_exp mid_gated f_full y_mul y_done "
                 "raw_hi raw_lo g_hi g_lo set_step silu_e silu_done sel_ready bias_full bias_ev zeroed "
                 "crow_in hw_used brow_ok").split()
        (c_in, x_in, wvo_in, wr_in, base_in, ff_in, gab_in, acc_in, brow_in,
         gcol_out, gate_out, bias_out, y_out,
         m_full, m_hi, m_free, t_full, t_hi, t_free, s_full, s_min, s_bias, s_exp, s_rec, p_norm,
         h_mod, rotated, grp_ready, ln_var, ln_rstd, ln_xn, ln_step, mod_b,
         gate_step, gate_max, gate_exp, mid_gated, f_full, y_mul, y_done,
         raw_hi, raw_lo, g_hi, g_lo, set_step, silu_e, silu_done, sel_ready, bias_full, bias_ev, zeroed,
         crow_in, hw_used, brow_ok) = [sem(n) for n in names]
        modw_in = [sem(f"modw_in{i}") for i in range(2)]
        hw_in = [sem(f"hw_in{i}") for i in range(2)]
        raw_in = [sem(f"raw_in{i}") for i in range(2)]
        wp_in = [sem(f"wp_in{i}") for i in range(2)]
        wps_out = [sem(f"wps_out{i}") for i in range(2)]
        wvs_out = [sem(f"wvs_out{i}") for i in range(2)]
        stg_out = [sem(f"stg_out{i}") for i in range(2)]
        T0, S0, Y0 = 2, NT, NT

        block = ctx.enter_context(nc.Block())

        def v3(ap, a):
            return ap.rearrange("p (a n) -> p a n", a=a)

        wqd_v = w_qd.rearrange("(c p) n -> p c n", p=P)
        wqr_v = w_qr.rearrange("(m p) n -> m p n", p=P)
        base_v = base_wT.rearrange("(c p) n -> p c n", p=P)
        JOBS = []
        for k in range(2):
            JOBS.append((wqd_v[:, 2 * k:2 * k + 2, :], P, 2 * QC, 2, [wqd[:, hl, 2 * k:2 * k + 2, :] for hl in (HI, LO)], []))
        JOBS.append((w_kvd.rearrange("(c p) n -> p c n", p=P), P, NC * KVC, NC, [wkvd[:, hl, :, :] for hl in (HI, LO)], []))
        EARLY = len(JOBS)
        JOBS.append((w_kr, P, NG * KW, 1, [wk[:, hl, :] for hl in (HI, LO)], []))
        for m in range(NM):
            st = []
            for hl in (HI, LO):
                st.append((wr_d[0:NG, :, hl, m, 0:KW].rearrange("g p n -> p g n"), hl, NG, NG * KW))
                st.append((wr_d[NG:NG + 1, :, hl, m, 0:KW].rearrange("g p n -> p g n"), hl, 1, KW))
            JOBS.append((wqr_v[m], P, NG * KW, 1, None, st))
        for k in range(2):
            JOBS.append((base_v[:, 2 * k:2 * k + 2, :], P, 2 * HID, 2, None,
                         [(base_d[:, hl:hl + 1, 2 * k * HID:(2 * k + 2) * HID], hl, 1, 2 * HID) for hl in (HI, LO)]))
        JOBS.append((ffn_a.rearrange("(c p) n -> p c n", p=P), P, NC * FW, NC, None,
                     [(ff_d[:, hl:hl + 1, 0:NC * FW], hl, 1, NC * FW) for hl in (HI, LO)]))
        JOBS.append((ffn_b, P, HID, 1, None, [(ff_d[:, hl:hl + 1, NC * FW:NF], hl, 1, HID) for hl in (HI, LO)]))
        ROWS = len(JOBS)
        for src, n, r0, c0 in ((q_row[:, 0:2 * QW], 2 * QW, 0, 0), (q_row[:, 2 * QW:4 * QW], 2 * QW, 0, 2 * QW),
                               (k_row, NG * KW, 2, 0), (f_row, HID + FW, 4, 0)):
            JOBS.append((src, 1, n, 1, None, [(row_d[r0 + hl:r0 + hl + 1, c0:c0 + n].unsqueeze(1), hl, 1, n) for hl in (HI, LO)]))
        NJ = len(JOBS)
        stored, total = [], [0, 0]
        for k, job in enumerate(JOBS):
            total[k % 2] += 16 * len(job[5])
            stored.append(total[k % 2])

        def job_parts(k):
            _, rows, n, a, dst, _ = JOBS[k]
            src = raw[k % 2][0:rows, 0:n]
            if dst is None:
                return src, [stg[k % 2][0:rows, hl, 0:n] for hl in (HI, LO)]
            return (v3(src, a) if a > 1 else src), dst

        @block.sync
        def _(sp):
            pl = Place()
            sp.dma_start(inp[:, :], inputs).then_inc(c_in, 16)
            sp.dma_start(cst[:, :], consts[:, 0:P + S + 2 * NT * RD + NE]).then_inc(c_in, 16)
            sp.dma_start(selt, consts[:, P + S + 2 * NT * RD + NE:]).then_inc(c_in, 16)
            sp.dma_start(bo_t[:, :], b_o).then_inc(c_in, 16)
            sp.dma_start(xn[:, :, :], x[0].rearrange("(t p) n -> p t n", p=P)).then_inc(x_in, 16)
            wmod_v = wmod.rearrange("(c p) (k n) -> k p c n", p=P, n=HID)
            for k in range(6):
                if k >= 2:
                    sp.wait_ge(m_full, k - 1)
                sp.dma_start(modw[k % 2], wmod_v[k]).then_inc(modw_in[k % 2], 16)
            for h in range(NH):
                if h >= 2:
                    sp.wait_ge(hw_used, h - 1)
                else:
                    sp.wait_ge(sel_ready, 1)
                    sp.wait_ge(set_step, 8)
                sp.dma_start(hw[h % 2], heads_w[h * HD:(h + 1) * HD, :]).then_inc(hw_in[h % 2], 16)
            sp.wait_ge(bias_ev, 1)
            sp.dma_start(bias_d, bias_s[:, :]).then_inc(bias_out, 16)
            for k in (0, 1):
                sp.wait_ge(stg_out[k], total[k])
                sp.wait_ge(wps_out[k], 16 * (NH // 2 + 1))
                sp.wait_ge(wvs_out[k], 16 * (NH // 2))
            sp.wait_ge(gcol_out, 16 * 4 * NM)
            sp.wait_ge(zeroed, 1)
            for r0, n in ((0, NG * QW), (2, NG * KW), (4, HID + FW)):
                sp.dma_start(brow[r0:r0 + 2, 0:n].bitcast(F32), row_d[r0:r0 + 2, 0:n]).then_inc(brow_in, 16)
            sp.dma_start(wr[:, :, :, :].bitcast(F32), wr_d[0]).then_inc(wr_in, 16)

            def wp_load(k, h):
                sp.dma_start(wp[:, k, :, :, :].bitcast(F32).rearrange("p k m n -> p (k m n)"), wp_d[h]).then_inc(wp_in[k], 16)

            def wvo_load(h0):
                sp.dma_start(wvo[:, :].bitcast(F32).rearrange("p (j n) -> p j n", j=GH),
                             wvo_d[bass.ds(h0, GH)].rearrange("j p n -> p j n")).then_inc(wvo_in, 16)

            wp_load(0, 0)
            wp_load(1, 1)
            wvo_load(0)
            sp.wait_ge(bias_out, 16)
            sp.wait_ge(gate_out, 32)
            pl.done("mod", "mod", "mod", "modT", "normed", *["feature"] * NC, *["latent"] * (NM + 1), *["absorb"] * NH,
                    "kv_row", "kv_row")

            def rotated_group(g, n):
                pl.done(*["rotate"] * n, "group")
                sp.wait_ge(m_full, pl.at("m"))
                sp.dma_start(wr[:, :, :, :].bitcast(F32), wr_d[g]).then_inc(wr_in, 16)

            def query(j, h):
                pl.done("query")
                sp.wait_ge(m_full, pl.at("m"))
                wp_load(j % 2, h)

            def projected(h0):
                pl.done("project", "projected")
                sp.wait_ge(m_full, pl.at("m"))
                wvo_load(h0)

            def acc_load():
                sp.dma_start(acc[:, :, :], bias_d.unsqueeze(1).broadcast_to([P, NT, HID])).then_inc(acc_in, 16)

            acc_load()
            rotated_group(1, 2 * NT)
            query(0, 2)
            pl.done("rope", "rope")
            query(1, 3)
            pl.done("rope", "rope")

            def group(b, g, first, last, more):
                if first:
                    pl.done("rope", "rope")
                else:
                    pl.done("project", "project", "project", "rope")
                    projected(GH * g)
                    pl.done("rope")
                query(2, GH * g + 4)
                pl.done("context", "rope", "rope")
                if not last:
                    pl.done("rotate", "rotate")
                elif more:
                    pl.done("feature", "feature")
                query(3, GH * g + 5)
                if not last:
                    pl.done("rotate", "context", "rotate")
                    rotated_group(g + 2, NT)
                    query(0, GH * g + 6)
                    pl.done("context", "rope", "rope")
                    query(1, GH * g + 7)
                    pl.done("rope", "rope", "context")
                else:
                    if more:
                        pl.done("feature", "context", "feature")
                        sp.wait_ge(m_full, pl.at("m"))
                        sp.dma_start(xn[:, :, :], x[b].rearrange("(t p) n -> p t n", p=P)).then_inc(x_in, 16)
                        pl.done("latent", "latent", "context", "latent", "latent", "rotate")
                    else:
                        pl.done("context", "context")
                    pl.done("context")

            def batch(b, more):
                sp.dma_start(gab[:, :, :], gate_d[bass.ds(b, 1)].broadcast_to([P, 2, HID])).then_inc(gab_in, 16)
                sp.dma_start(xn[:, :, :], x[b + 1 if more else b].rearrange("(t p) n -> p t n", p=P)).then_inc(x_in, 16)
                group(b, 0, True, False, more)
                if more:
                    pl.done("normed")
                with passes(sp, pl, 1, NG - 1, GROUP) as g:
                    group(b, g, False, False, more)
                group(b, NG - 1, False, True, more)
                sp.wait_ge(m_full, pl.at("m"))
                sp.dma_start(pT[:, :].bitcast(F32), base_d.rearrange("p k n -> p (k n)")).then_inc(base_in, 16)
                if more:
                    pl.done("rotate", "rotate", "rotate", "kv_row", "kv_row", "rotate", "rotate")
                pl.done("project", "project", "project")
                projected(0)
                sp.dma_start(cxT[:, 0:2 * NF].bitcast(F32), ff_d.rearrange("p k n -> p (k n)")).then_inc(ff_in, 16)
                pl.done(*["residual"] * NT)
                if more:
                    rotated_group(1, 2)
                    query(0, 2)
                    pl.done("rope", "rope", "feature")
                    query(1, 3)
                    pl.done("rope", "rope", *["feature"] * 3)
                else:
                    pl.done(*["feature"] * NC)
                pl.done(*["expert"] * NT)
                for t in range(NT):
                    sp.wait_ge(y_done, pl.at("y", 1))
                    sp.dma_start(out[b, t * P:(t + 1) * P, :], xn[:, t, :]).then_inc(y_out, 16)
                    pl.done("ffn_out")
                sp.wait_ge(y_out, pl.at("y") * 16)
                if more:
                    acc_load()
                pl.done(*["gate_step"] * GATE_STEPS, *["step"] * (4 * NT + 2 * more), "batch")

            with passes(sp, pl, 0, B - 1, BATCH) as b:
                batch(b, True)
            batch(B - 1, False)
            sp.wait_ge(wvo_in, 16 * (NG * B + 1))
            for k in (0, 1):
                sp.wait_ge(wp_in[k], 16 * (NH // 2 * B + 1))

        @block.tensor
        def _(pe):
            pl = Place()

            def m_bank(early=False):
                if not early:
                    pe.wait_ge(m_free, pl.at("m", -1))
                return mb[pl.bank("m")]

            def three(o, a, b, first, last):
                nc.tensor.matmul(o, a[HI], b[HI], start=first, stop=False, skip_group_check=True)
                nc.tensor.matmul(o, a[HI], b[LO], start=False, stop=False, skip_group_check=True)
                return nc.tensor.matmul(o, a[LO], b[HI], start=False, stop=last, skip_group_check=True)

            def feature(c):
                ps = m_bank()
                for t in range(NT):
                    mm = nc.tensor.transpose(ps[:, t * P:(t + 1) * P], xn[:, t, c * P:(c + 1) * P], idf)
                mm.then_inc(m_full, 1)
                pl.done("feature")
                pl.mark(("h", c), "m")

            def latent(m):
                ps = m_bank()
                for c in range(NC):
                    if m == 0:
                        pe.wait_ge(m_free, pl.since(("h", c)))
                    w = [wqd[:, hl, c, m * P:(m + 1) * P] if m < NM else wkvd[:, hl, c, :] for hl in (HI, LO)]
                    mm = three(ps[:, :], w, [hT[:, hl, c, :] for hl in (HI, LO)], c == 0, c == NC - 1)
                mm.then_inc(m_full, 1)
                pl.done("latent")
                pl.mark(("latent", m), "m")

            def kv_row(hl):
                ps = m_bank()
                pe.wait_ge(m_free, pl.since(("latent", NM)))
                for t in range(NT):
                    mm = nc.tensor.transpose(ps[:, t * P:(t + 1) * P], kvT[:, hl, t * P:(t + 1) * P].bitcast(F32), idf)
                mm.then_inc(m_full, 1)
                pl.done("kv_row")

            def rotate(g, t, k, new=False):
                tok = slice(t * P, (t + 1) * P)
                ps = m_bank()
                if k == 0:
                    if t == 0:
                        pe.wait_ge(wr_in, pl.at("grp") * 16 + 16)
                        if new:
                            pe.wait_ge(m_free, pl.since(("latent", NM - 1)))
                    for m in range(NM):
                        three(ps[:, 0:QW], [qcT[:, hl, m, tok] for hl in (HI, LO)], [wr[:, hl, m, :] for hl in (HI, LO)], m == 0, False)
                    nc.tensor.matmul(ps[:, 0:QW], selr[:, 0, :], brow[:, bass.ds(g * QW, QW)],
                                     start=False, stop=True, skip_group_check=True).then_inc(m_full, 1)
                else:
                    if t == 0 and new:
                        pe.wait_ge(m_free, pl.since(("latent", NM)))
                    three(ps[:, 0:KW], [kvT[:, hl, tok] for hl in (HI, LO)],
                          [wk[:, hl, bass.ds(g * KW, KW)] for hl in (HI, LO)], True, False)
                    nc.tensor.matmul(ps[:, 0:KW], selr[:, 1, :], brow[:, bass.ds(g * KW, KW)],
                                     start=False, stop=True, skip_group_check=True).then_inc(m_full, 1)
                pl.done("rotate")

            def query(j):
                pe.wait_ge(wp_in[j % 2], pl.at("qm") * 8 + (8 if j % 2 else 16))
                ps = m_bank()
                for m in range(NM):
                    mm = three(ps[:, :], [wp[:, j % 2, hl, m, :] for hl in (HI, LO)], [qcT[:, hl, m, :] for hl in (HI, LO)], m == 0, m == NM - 1)
                mm.then_inc(m_full, 1)
                pl.done("query")
                pl.mark(("q", j % 2), "m")

            def rope(j, k):
                ps = m_bank()
                if j == 0 and k == 0:
                    pe.wait_ge(rotated, pl.at("ab"))
                for t in range(NT):
                    mm = nc.tensor.transpose(ps[:, t * P:(t + 1) * P], rq[:, k, t, j * P:(j + 1) * P], idf)
                mm.then_inc(m_full, 1)
                pl.done("rope")
                pl.mark(("q", j % 2), "m")

            def score(j, i, after_y=False):
                if i == 0:
                    pe.wait_ge(m_free, pl.since(("q", j % 2)))
                q, w = slice(i * P, (i + 1) * P), (i + 1) * P
                if after_y:
                    pe.wait_ge(y_mul, pl.at("y", i + 1))
                pe.wait_ge(s_exp, pl.at("s", 1))
                ps = sk[i][:, 0:w]
                three(ps, [qa[:, j % 2, hl, q] for hl in (HI, LO)], [kvT[:, hl, 0:w] for hl in (HI, LO)], True, False)
                nc.tensor.matmul(ps, q2[:, j % 2, q], kk[:, j % 2, HI, 0:w], start=False, stop=False, skip_group_check=True)
                nc.tensor.matmul(ps, q2[:, j % 2, q], kk[:, j % 2, LO, 0:w], start=False, stop=True,
                                 skip_group_check=True).then_inc(s_full, 1)
                pl.done("score")
                pl.mark(("s", j % 2, i), "s")

            def turn(j, i):
                pe.wait_ge(p_norm, pl.since(("s", j % 2, i)))
                pe.wait_ge(t_free, pl.at("t", 1))
                o = i * (i + 1) // 2 * P
                for k in range(i + 1):
                    mm = nc.tensor.transpose(tb[pl.bank("t")][:, k * P:(k + 1) * P],
                                             pr[:, j % 2, o + k * P:o + (k + 1) * P], idf)
                mm.then_inc(t_full, 1)
                pl.done("turn")

            def context(j):
                ps = m_bank()
                pe.wait_ge(t_free, pl.at("t", T0))
                for k in range(NT):
                    q = slice(k * P, S)
                    mm = three(ps[:, q], [kvr[:, hl, k, :] for hl in (HI, LO)], [pTv[:, hl, k, q] for hl in (HI, LO)], k == 0, k == NT - 1)
                mm.then_inc(m_full, 1)
                pl.done("context")
                pl.mark("cx", "m")

            def project(t):
                ps = m_bank()
                if t == 0:
                    pe.wait_ge(wvo_in, pl.at("pg") * 16 + 16)
                    pe.wait_ge(m_free, pl.since("cx"))
                for j in range(GH):
                    mm = three(ps[:, :], [cx[:, hl, j, t * P:(t + 1) * P] for hl in (HI, LO)],
                               [wvov[:, j, hl, :] for hl in (HI, LO)], j == 0, j == GH - 1)
                mm.then_inc(m_full, 1)
                pl.done("project")
                if t == NT - 1:
                    pl.done("projected")

            pe.wait_ge(silu_done, 1)
            for k in range(6):
                ps = m_bank(k < 2)
                pe.wait_ge(modw_in[k % 2], 16 * (k // 2 + 1))
                for c in range(NC):
                    mm = nc.tensor.matmul(ps[0:B, :], sT[:, c * B:(c + 1) * B], modw[k % 2][:, c, :], start=(c == 0), stop=(c == NC - 1))
                mm.then_inc(m_full, 1)
                pl.done("one")
            for r in range(2):
                ps = m_bank()
                if r == 0:
                    pe.wait_ge(m_free, 6)
                for k in range(2):
                    for c in range(NC):
                        o = (2 * r + k) * HID + c * P
                        mm = nc.tensor.transpose(ps[:, (k * NC + c) * B:(k * NC + c + 1) * B], modrow[:, o:o + P], idf[0:B, 0:B])
                mm.then_inc(m_full, 1)
                pl.done("one")
            pl.done("normed")
            pe.wait_ge(ln_xn, 1)
            for c in range(NC):
                feature(c)
            pe.wait_ge(raw_lo, EARLY)
            for m in range(NM + 1):
                latent(m)
            for h in range(NH):
                pe.wait_ge(hw_in[h % 2], 16 * (h // 2 + 1))
                w = hw[h % 2]
                ku, vu, wo = w[:, QC:QC + KVC], w[:, QC + KVC + 1:QC + 2 * KVC + 1], w[:, QC + 2 * KVC + 1:HEADW]
                ps = m_bank()
                for m in range(NM):
                    nc.tensor.matmul(ps[:, m * 129:(m + 1) * 129], w[:, m * P:(m + 1) * P], w[:, QC:QC + KVC + 1], start=True, stop=True)
                nc.tensor.matmul(ps[:, 390:391], ku, bqu[:, 0, h:h + 1], start=True, stop=True)
                nc.tensor.matmul(ps[0:1, 391:392], bqu[:, 1, h:h + 1], bqu[:, 0, h:h + 1], start=True, stop=True).then_inc(m_full, 1)
                pl.done("one")
                ps = m_bank()
                nc.tensor.matmul(ps[:, :], vu, wo, start=True, stop=True).then_inc(m_full, 1)
                nc.tensor.matmul(sk[0][0:1, :], bqu[:, 2, h:h + 1], wo, start=(h == 0), stop=False).then_inc(hw_used, 1)
                pl.done("one", "hi")
            nc.tensor.matmul(sk[0][0:1, :], idf[0:1, 0:1], bo_t[:, :], start=False, stop=True).then_inc(bias_full, 1)
            kv_row(HI)
            kv_row(LO)
            pe.wait_ge(sel_ready, 1)
            pe.wait_ge(raw_lo, NJ)
            pe.wait_ge(brow_in, 3 * 16)
            for t in range(NT):
                rotate(0, t, 0)
                rotate(0, t, 1)
            pl.done("group")
            for j in range(2):
                query(j)
                rope(j, 0)
                rope(j, 1)
            pe.wait_ge(bias_ev, 1)
            for i in range(NT):
                score(0, i)

            def group(g, first, last, more):
                turn(0, 0)
                turn(0, 1)
                if first:
                    rope(2, 0)
                    turn(0, 2)
                    rope(2, 1)
                    turn(0, 3)
                    query(2)
                    for i in range(NT):
                        score(1, i, after_y=True)
                else:
                    score(1, 0)
                    score(1, 1)
                    score(1, 2)
                    project(0)
                    turn(0, 2)
                    project(1)
                    score(1, 3)
                    project(2)
                    turn(0, 3)
                    rope(2, 0)
                    project(3)
                    rope(2, 1)
                    query(2)
                context(0)

                turn(1, 0)
                turn(1, 1)
                rope(3, 0)
                score(2, 0)
                score(2, 1)
                turn(1, 2)
                rope(3, 1)
                score(2, 2)
                if not last:
                    rotate(g + 1, 0, 0)
                elif more:
                    pe.wait_ge(ln_xn, pl.at("xn"))
                    feature(0)
                turn(1, 3)
                score(2, 3)
                if not last:
                    rotate(g + 1, 0, 1)
                elif more:
                    feature(1)
                query(3)
                if not last:
                    rotate(g + 1, 1, 0)
                elif more:
                    feature(2)
                context(1)
                if not last:
                    rotate(g + 1, 1, 1)
                elif more:
                    feature(3)

                turn(2, 0)
                turn(2, 1)
                score(3, 0)
                score(3, 1)
                if not last:
                    rotate(g + 1, 2, 0)
                turn(2, 2)
                score(3, 2)
                if not last:
                    rotate(g + 1, 2, 1)
                elif more:
                    latent(0)
                turn(2, 3)
                score(3, 3)
                if not last:
                    rotate(g + 1, 3, 0)
                    rotate(g + 1, 3, 1)
                    pl.done("group")
                    query(0)
                elif more:
                    latent(1)
                context(2)
                if not last:
                    rope(0, 0)

                turn(3, 0)
                if not last:
                    rope(0, 1)
                    turn(3, 1)
                    query(1)
                    score(0, 0)
                    score(0, 1)
                    turn(3, 2)
                    rope(1, 0)
                    score(0, 2)
                    turn(3, 3)
                    rope(1, 1)
                    score(0, 3)
                else:
                    turn(3, 1)
                    if more:
                        latent(2)
                    turn(3, 2)
                    if more:
                        latent(3)
                    turn(3, 3)
                    if more:
                        rotate(0, 0, 0, new=True)
                context(3)

            def batch(b, more):
                pl.mark(("q", 1), "m")
                group(0, True, False, more)
                if more:
                    pl.done("normed")
                with passes(pe, pl, 1, NG - 1, GROUP) as g:
                    group(g, False, False, more)
                group(NG - 1, False, True, more)
                if more:
                    rotate(0, 0, 1, new=True)
                    rotate(0, 1, 0)
                    rotate(0, 1, 1)
                for t in range(NT):
                    project(t)
                    pl.done("residual")
                    if more and t < 2:
                        kv_row(t)
                    if more and t >= 2:
                        rotate(0, t, 0)
                        rotate(0, t, 1)
                if more:
                    pl.done("group")
                    query(0)
                    rope(0, 0)
                    rope(0, 1)
                pe.wait_ge(ln_xn, pl.at("xn"))
                feature(0)
                if more:
                    query(1)
                feature(1)
                if more:
                    rope(1, 0)
                feature(2)
                if more:
                    rope(1, 1)
                feature(3)
                if more:
                    for i in range(NT):
                        score(0, i)
                pe.wait_ge(ff_in, pl.at("batch") * 16 + 16)
                for t in range(NT):
                    ps = m_bank()
                    tok = slice(t * P, (t + 1) * P)
                    for c in range(NC):
                        if t == 0:
                            pe.wait_ge(m_free, pl.since(("h", c)))
                        three(ps[:, 0:FW], [hT[:, hl, c, tok] for hl in (HI, LO)], [fa[:, hl, c, :] for hl in (HI, LO)], c == 0, False)
                    nc.tensor.matmul(ps[:, 0:FW], selr[:, 2, :], brow[:, HID:HID + FW], start=False, stop=True,
                                     skip_group_check=True).then_inc(m_full, 1)
                    pl.done("expert")
                pe.wait_ge(base_in, pl.at("batch") * 16 + 16)
                for t in range(NT):
                    pe.wait_ge(s_exp, pl.at("s", t + 1))
                    tok = slice(t * P, (t + 1) * P)
                    for c in range(NC):
                        three(sk[t][:, :], [hT[:, hl, c, tok] for hl in (HI, LO)], [basew[:, hl, c, :] for hl in (HI, LO)], c == 0, False)
                    nc.tensor.matmul(sk[t][:, :], selr[:, 2, :], brow[:, 0:HID], start=False, stop=False, skip_group_check=True)
                pe.wait_ge(mid_gated, pl.at("batch") + 1)
                for k in range(2):
                    pe.wait_ge(t_free, pl.at("t", 1))
                    for t in range(2):
                        mm = nc.tensor.transpose(tb[pl.bank("t")][:, t * P:(t + 1) * P], midg[:, 2 * k + t, :], idf)
                    mm.then_inc(t_full, 1)
                    pl.done("turn_mid")
                for t in range(NT):
                    if t % 2 == 0:
                        pe.wait_ge(t_free, pl.at("t", T0 - 1 + t // 2))
                    tok = slice(t * P, (t + 1) * P)
                    three(sk[t][:, :], [midT[:, hl, tok] for hl in (HI, LO)], [fb[:, hl, :] for hl in (HI, LO)], False, True).then_inc(f_full, 1)
                    pl.done("ffn_out")
                pl.done(*["gate_step"] * GATE_STEPS, *["step"] * (4 * NT + 2 * more), "batch")

            with passes(pe, pl, 0, B - 1, BATCH) as b:
                batch(b, True)
            batch(B - 1, False)

        @block.scalar
        def _(act):
            pl = Place()

            def hi_of(dst, bias=None):
                src = mb[pl.bank("m")]
                act.wait_ge(m_full, pl.at("m", 1))
                if bias is None:
                    nc.scalar.activation(dst, src[:, :], ACT.Copy).then_inc(m_hi, 1)
                else:
                    nc.scalar.activation(dst, src[:, :], ACT.Identity, bias=bias).then_inc(m_hi, 1)

            def feature(c, half):
                ps = mb[pl.bank("m")]
                o = 2 * NC * half + c
                act.wait_ge(m_full, pl.at("m", 1))
                nc.scalar.activation(ps[:, :], ps[:, :], ACT.Identity, bias=modb[:, o:o + 1],
                                     scale=modb[:, o + NC:o + NC + 1]).then_inc(h_mod, 1)
                act.wait_ge(h_mod, pl.at("h", 1))
                nc.scalar.activation(hT[:, HI, c, :], ps[:, :], ACT.Copy).then_inc(m_hi, 1)
                pl.done("feature")

            def latent(m):
                if m < NM:
                    hi_of(qcT[:, HI, m, :], bqd[:, m:m + 1])
                else:
                    hi_of(kvT[:, HI, :], bkvd)
                pl.done("latent")

            def query(j):
                if j == 0:
                    act.wait_ge(grp_ready, pl.at("grp"))
                hi_of(qa[:, j % 2, HI, :], qbg[:, j:j + 1])
                pl.done("query")

            def rope(j, k):
                hi_of(kk[:, j % 2, HI, :] if k else q2[:, j % 2, :])
                pl.done("rope")

            def score(j, i):
                o, w = i * (i + 1) // 2 * P, (i + 1) * P
                act.wait_ge(s_bias, pl.at("s", 1))
                nc.scalar.activation(pr[:, j % 2, o:o + w], sk[i][:, 0:w], ACT.Exp, bias=nb[:, j % 2, i:i + 1],
                                     scale=-1.0, accum_out=sm[:, j % 2, i:i + 1]).then_inc(s_exp, 1)
                pl.done("score")

            def turn(i):
                w = (i + 1) * P
                act.wait_ge(t_full, pl.at("t", 1))
                nc.scalar.activation(pTv[:, HI, 0:i + 1, i * P:(i + 1) * P],
                                     tb[pl.bank("t")][:, 0:w].rearrange("p (k n) -> p k n", n=P), ACT.Copy).then_inc(t_hi, 1)
                pl.done("turn")

            def context(j):
                hi_of(cx[:, HI, j, :])
                pl.done("context")

            act.wait_ge(c_in, 4 * 16)
            nc.scalar.activation(sE[:, 0, :], sT, ACT.Exp, scale=-1.0).then_inc(silu_e, 1)
            for k in range(S0):
                nc.scalar.activation(tiny[:, k:k + 1], idf[:, k:k + 1], ACT.Copy).then_inc(s_exp, 1)

            def split(k):
                src, dst = job_parts(k)
                act.wait_ge(raw_in[k % 2], 16 * (k // 2 + 1))
                if k >= 2:
                    act.wait_ge(stg_out[k % 2], stored[k - 2])
                if ROWS <= k < ROWS + 2:
                    act.wait_ge(crow_in, k - ROWS + 1)
                nc.scalar.activation(dst[HI], src, ACT.Copy).then_inc(raw_hi, 1)

            for k in range(EARLY):
                split(k)
            pl.done("mod", "mod", "mod", "modT", "normed")
            act.wait_ge(mod_b, 1)
            for c in range(NC):
                feature(c, 0)
            for m in range(NM + 1):
                latent(m)
            for h in range(NH):
                act.wait_ge(m_full, pl.at("m", 1))
                if h >= 2:
                    act.wait_ge(wps_out[h % 2], 16 * (h // 2 + 1))
                nc.scalar.activation(wps[h % 2][:, HI, :, :], mb[0][:, 0:387].rearrange("p (m n) -> p m n", m=NM)[:, :, 0:KVC],
                                     ACT.Copy).then_inc(m_hi, 1)
                act.wait_ge(m_full, pl.at("m", 2))
                if h >= 2:
                    act.wait_ge(wvs_out[h % 2], 16 * (h // 2))
                nc.scalar.activation(wvs[h % 2][:, HI, :], mb[1][:, :], ACT.Copy).then_inc(m_hi, 1)
                pl.done("absorb")
                if EARLY + h < ROWS:
                    split(EARLY + h)
            act.wait_ge(m_free, pl.at("m"))
            nc.scalar.activation(gsp[:, HI, :, :], gcol[:, :, :], ACT.Copy).then_inc(g_hi, 1)
            for k in range(ROWS, NJ):
                split(k)
            pl.done("kv_row", "kv_row", *["rotate"] * (2 * NT), "group")
            for j in range(2):
                query(j)
                rope(j, 0)
                rope(j, 1)
            for i in range(NT):
                score(0, i)

            def group(first, last, more):
                turn(0)
                turn(1)
                if first:
                    rope(2, 0)
                    turn(2)
                    rope(2, 1)
                    turn(3)
                    query(2)
                    for i in range(NT):
                        score(1, i)
                else:
                    score(1, 0)
                    score(1, 1)
                    score(1, 2)
                    turn(2)
                    score(1, 3)
                    turn(3)
                    pl.done(*["project"] * 3)
                    rope(2, 0)
                    pl.done("project")
                    rope(2, 1)
                    query(2)
                context(0)

                turn(0)
                turn(1)
                rope(3, 0)
                score(2, 0)
                score(2, 1)
                turn(2)
                rope(3, 1)
                score(2, 2)
                if not last:
                    pl.done("rotate")
                elif more:
                    feature(0, 0)
                turn(3)
                score(2, 3)
                if not last:
                    pl.done("rotate")
                elif more:
                    feature(1, 0)
                query(3)
                if not last:
                    pl.done("rotate")
                elif more:
                    feature(2, 0)
                context(1)
                if not last:
                    pl.done("rotate")
                elif more:
                    feature(3, 0)

                turn(0)
                turn(1)
                score(3, 0)
                score(3, 1)
                turn(2)
                score(3, 2)
                if not last:
                    pl.done("rotate", "rotate")
                elif more:
                    latent(0)
                turn(3)
                score(3, 3)
                if not last:
                    pl.done("rotate", "rotate", "group")
                    query(0)
                elif more:
                    latent(1)
                context(2)
                if not last:
                    rope(0, 0)

                turn(0)
                if not last:
                    rope(0, 1)
                    turn(1)
                    query(1)
                    score(0, 0)
                    score(0, 1)
                    turn(2)
                    rope(1, 0)
                    score(0, 2)
                    turn(3)
                    rope(1, 1)
                    score(0, 3)
                else:
                    turn(1)
                    if more:
                        latent(2)
                    turn(2)
                    if more:
                        latent(3)
                    turn(3)
                    if more:
                        pl.done("rotate")
                context(3)

            def batch(b, more):
                group(True, False, more)
                if more:
                    pl.done("normed")
                with passes(act, pl, 1, NG - 1, GROUP):
                    group(False, False, more)
                act.wait_ge(mod_b, pl.at("batch") + 2)
                group(False, True, more)
                pl.done(*["project", "residual"] * NT)
                if more:
                    pl.done(*["rotate"] * (2 * NT - 1), "kv_row", "kv_row", "group")
                    query(0)
                    rope(0, 0)
                    rope(0, 1)
                    feature(0, 1)
                    query(1)
                    feature(1, 1)
                    rope(1, 0)
                    feature(2, 1)
                    rope(1, 1)
                    feature(3, 1)
                    for i in range(NT):
                        score(0, i)
                else:
                    for c in range(NC):
                        feature(c, 1)
                pl.done(*["expert"] * NT)
                act.wait_ge(gate_max, pl.at("batch") + 1)
                nc.scalar.activation(sc[:, 1, :], sc[:, 0, :], ACT.Exp).then_inc(gate_exp, 1)
                pl.done(*["gate_step"] * GATE_STEPS)
                for k in range(2):
                    act.wait_ge(t_full, pl.at("t", 1))
                    nc.scalar.activation(midT[:, HI, k * 256:(k + 1) * 256], tb[pl.bank("t")][:, 0:256], ACT.Copy).then_inc(t_hi, 1)
                    pl.done("turn_mid")
                pl.done(*["ffn_out"] * NT, *["step"] * (4 * NT + 2 * more), "batch")

            with passes(act, pl, 0, B - 1, BATCH) as b:
                batch(b, True)
            batch(B - 1, False)

        @block.vector
        def _(dve):
            pl = Place()

            def carry():
                nc.vector.tensor_copy(tiny2[:, T0 + Y0:], tiny2[:, 0:1])

            def lo_of(dst, hi, bias=None, rows=slice(0, P)):
                src = mb[pl.bank("m")][rows, :]
                dve.wait_ge(m_hi, pl.at("hi", 1))
                if bias is None:
                    nc.vector.tensor_tensor(dst, src, hi, ALU.subtract).then_inc(m_free, 1)
                else:
                    nc.vector.scalar_tensor_tensor(out=dst, in0=src, scalar=bias, in1=hi,
                                                   op0=ALU.add, op1=ALU.subtract).then_inc(m_free, 1)

            def feature(c):
                lo_of(hT[:, LO, c, :], hT[:, HI, c, :])
                pl.done("feature")

            def latent(m):
                if m < NM:
                    lo_of(qcT[:, LO, m, :], qcT[:, HI, m, :], bqd[:, m:m + 1])
                else:
                    lo_of(kvT[:, LO, :], kvT[:, HI, :], bkvd)
                pl.done("latent")

            def kv_row(hl):
                dve.wait_ge(m_full, pl.at("m", 1))
                nc.vector.tensor_copy(kvr[:, hl, :, :], mb[pl.bank("m")][:, :].rearrange("p (t n) -> p t n", t=NT)).then_inc(m_free, 1)
                pl.done("kv_row")

            def rotate(t, k):
                half = RD // 2
                u = pl.bank("ab")
                dve.wait_ge(m_full, pl.at("m", 1))
                if not (isinstance(pl.at("ab"), int) and pl.at("ab") < 2):
                    dve.wait_ge(rotated, pl.at("ab", -1))
                ps = mb[pl.bank("m")]
                v = ps[:, 0:KW].rearrange("p (j n) -> p j n", n=RD)
                a, r = (ab[:, u, i, :].rearrange("p (j n) -> p j n", n=RD) for i in (0, 1))
                nc.vector.tensor_tensor(a, v, cost[:, t, :].unsqueeze(1).broadcast_to([P, GH, RD]), ALU.mult)
                nc.vector.tensor_tensor(r[:, :, 0:half], v[:, :, half:RD],
                                        sint[:, t, 0:half].unsqueeze(1).broadcast_to([P, GH, half]), ALU.mult)
                if k == 0:
                    nc.vector.tensor_scalar(cbn[:, t, :], ps[:, KW:QW], -SCALE, None, ALU.mult)
                nc.vector.tensor_tensor(r[:, :, half:RD], v[:, :, 0:half],
                                        sint[:, t, half:RD].unsqueeze(1).broadcast_to([P, GH, half]), ALU.mult).then_inc(m_free, 1)
                pl.done("rotate")

            def ready(g, scored=True):
                dve.wait_ge(m_free, pl.at("m"))
                if scored:
                    dve.wait_ge(s_bias, pl.at("s"))
                nc.vector.tensor_copy(cb[:, :, :], cbn[:, :, :])
                nc.vector.tensor_copy(qbg[:, :], qbias[:, bass.ds(g * GH, GH)]).then_inc(grp_ready, 1)
                pl.done("group")

            def query(j):
                if j == 0:
                    dve.wait_ge(grp_ready, pl.at("grp"))
                lo_of(qa[:, j % 2, LO, :], qa[:, j % 2, HI, :], qbg[:, j:j + 1])
                pl.done("query")

            def rope(j, k):
                if k == 0:
                    low = slice(RD, P)
                    lo_of(q2[low, j % 2, :], q2[low, j % 2, :], rows=low)
                else:
                    lo_of(kk[:, j % 2, LO, :], kk[:, j % 2, HI, :])
                pl.done("rope")

            def score(j, i):
                w = (i + 1) * P
                ps = sk[i][:, 0:w]
                dve.wait_ge(s_full, pl.at("s", 1))
                carry()
                nc.vector.tensor_tensor_reduce(ps, ps, maskt[:, S - w:S], -SCALE, 3.0e38, ALU.add, ALU.min,
                                               nmx[:, j % 2, i:i + 1]).then_inc(s_min, 1)
                dve.wait_ge(s_min, pl.at("s", 1))
                nc.vector.scalar_tensor_tensor(out=nb[:, j % 2, i:i + 1], in0=nmx[:, j % 2, i:i + 1], scalar=cb[:, i, j:j + 1],
                                               in1=cb[:, i, j:j + 1], op0=ALU.add, op1=ALU.subtract).then_inc(s_bias, 1)
                pl.done("score")
                pl.mark(("s", i), "s")

            def reciprocal(j, i):
                dve.wait_ge(s_exp, pl.since(("s", i), S0))
                nc.vector.reciprocal(rsm[:, j % 2, i:i + 1], sm[:, j % 2, i:i + 1]).then_inc(s_rec, 1)

            def turn(i):
                w = (i + 1) * P
                dve.wait_ge(t_hi, pl.at("t", 1))
                at = (slice(0, i + 1), slice(i * P, (i + 1) * P))
                nc.vector.tensor_tensor(pTv[:, LO, at[0], at[1]], tb[pl.bank("t")][:, 0:w].rearrange("p (k n) -> p k n", n=P),
                                        pTv[:, HI, at[0], at[1]], ALU.subtract).then_inc(t_free, 1)
                pl.done("turn")

            def context(j):
                lo_of(cx[:, LO, j, :], cx[:, HI, j, :])
                pl.done("context")

            def project(t):
                if t == 0:
                    dve.wait_ge(acc_in, pl.at("batch") * 16 + 16)
                dve.wait_ge(m_free, pl.at("m", -1))
                dve.wait_ge(m_full, pl.at("m", 1))
                nc.vector.tensor_tensor(acc[:, t, :], mb[pl.bank("m")][:, :], acc[:, t, :], ALU.add).then_inc(m_free, 1)
                pl.done("project")

            def step(ins):
                ins.then_inc(ln_step, 1)
                pl.done("step")
                dve.wait_ge(ln_step, pl.at("ln"))

            def row_stats(t):
                return nc.vector.bn_stats(stats[:, t, :], xn[:, t, :])

            def row_vars(ins):
                step(ins)
                carry()
                for t in range(NT):
                    ins = nc.vector.bn_aggr(mv[:, t, :], stats[:, t, :])
                step(ins)
                nc.vector.tensor_scalar(ve[:, :], mv[:, :, 1], EPS, None, ALU.add).then_inc(ln_var, 1)

            def rows_normed():
                dve.wait_ge(ln_rstd, pl.at("var", 1))
                for t in range(NT):
                    ins = nc.vector.tensor_scalar(xn[:, t, :], xn[:, t, :], mv[:, t, 0:1], rstd[:, t:t + 1], ALU.subtract, ALU.mult)
                ins.then_inc(ln_xn, 1)
                pl.done("normed")

            def residual(t, x_loads):
                if t == 0:
                    dve.wait_ge(gab_in, pl.at("batch") * 16 + 16)
                    dve.wait_ge(x_in, x_loads)
                project(t)
                a = acc[:, t, :]
                dve.wait_ge(m_free, pl.at("m"))
                step(nc.vector.tensor_tensor(a, a, gab[:, 0, :], ALU.mult))
                step(nc.vector.tensor_tensor(a, a, xn[:, t, :], ALU.add))
                step(nc.vector.bn_stats(stats[:, t, :], a))
                carry()
                step(nc.vector.bn_aggr(mv[:, t, :], stats[:, t, :]))
                nc.vector.tensor_scalar(ve[:, t:t + 1], mv[:, t, 1:2], EPS, None, ALU.add).then_inc(ln_var, 1)

            def normed(t):
                dve.wait_ge(ln_rstd, pl.at("var", 1))
                nc.vector.tensor_scalar(xn[:, t, :], acc[:, t, :], mv[:, t, 0:1], rstd[:, t:t + 1],
                                        ALU.subtract, ALU.mult).then_inc(ln_xn, 1)
                pl.done("residual")

            def experts():
                for t in range(NT):
                    dve.wait_ge(m_full, pl.at("m", 1))
                    nc.vector.tensor_copy(mid[:, t, :], mb[pl.bank("m")][:, 0:FW]).then_inc(m_free, 1)
                    pl.done("expert")
                dve.wait_ge(m_free, pl.at("m"))

                def gstep(ins):
                    ins.then_inc(gate_step, 1)
                    pl.done("gate_step")
                    dve.wait_ge(gate_step, pl.at("gate"))

                def tile(i):
                    return sc[:, i, :].rearrange("p (t e) -> p t e", t=NT)

                def per_row(i):
                    return sc[:, i, 0:NT]

                def spread(ap, n=NE):
                    return ap.unsqueeze(2).broadcast_to([P, NT, n])

                logits = mid[:, :, NE * R:FW]
                gstep(nc.vector.tensor_reduce(per_row(2), logits, AX.X, ALU.max))
                nc.vector.tensor_tensor(tile(0), logits, spread(per_row(2)), ALU.subtract).then_inc(gate_max, 1)
                dve.wait_ge(gate_exp, pl.at("batch") + 1)
                gstep(nc.vector.tensor_reduce(per_row(3), tile(1), AX.X, ALU.add))
                gstep(nc.vector.reciprocal(per_row(4), per_row(3)))
                gstep(nc.vector.tensor_tensor(tile(5), tile(1), spread(per_row(4)), ALU.mult))
                carry()
                for t in range(NT):
                    ins = nc.vector.max(v8[:, t, :], tile(5)[:, t, :])
                gstep(ins)
                carry()
                for t in range(NT):
                    ins = nc.vector.max_index(i8[:, t, :], v8[:, t, :], tile(5)[:, t, :])
                gstep(ins)
                gstep(nc.vector.tensor_tensor(per_row(2), v8[:, :, 0], v8[:, :, 1], ALU.add))
                gstep(nc.vector.reciprocal(per_row(3), per_row(2)))
                w = sc[:, 4, 0:2 * NT].rearrange("p (t e) -> p t e", e=2)
                ix = sc[:, 6, 0:2 * NT].rearrange("p (t e) -> p t e", e=2)
                gstep(nc.vector.scalar_tensor_tensor(out=w, in0=v8[:, :, 0:2], scalar=LORA_SCALING, in1=spread(per_row(3), 2),
                                                     op0=ALU.mult, op1=ALU.mult))
                gstep(nc.vector.tensor_copy(ix, i8[:, :, 0:2]))
                io = iotat.unsqueeze(1).broadcast_to([P, NT, NE])
                gstep(nc.vector.tensor_tensor(tile(0), io, spread(ix[:, :, 0]), ALU.is_equal))
                gstep(nc.vector.tensor_tensor(tile(1), tile(0), spread(w[:, :, 0]), ALU.mult))
                gstep(nc.vector.tensor_tensor(tile(5), io, spread(ix[:, :, 1]), ALU.is_equal))
                gstep(nc.vector.tensor_tensor(tile(7), tile(5), spread(w[:, :, 1]), ALU.mult))
                gstep(nc.vector.tensor_tensor(tile(0), tile(1), tile(7), ALU.add))
            nc.vector.memset(nhalf[:, :], -0.5)
            nc.vector.memset(brow[:, :].bitcast(F32), 0.0).then_inc(zeroed, 1)
            for k in range(T0):
                nc.vector.memset(tiny2[:, k:k + 1], 0.0).then_inc(t_free, 1)
            for k in range(Y0):
                nc.vector.memset(tiny2[:, T0 + k:T0 + k + 1], 0.0).then_inc(y_mul, 1)

            def link(ins, n):
                ins.then_inc(set_step, 1)
                dve.wait_ge(set_step, n)

            dve.wait_ge(silu_e, 1)
            link(nc.vector.tensor_scalar(sE[:, 1, :], sE[:, 0, :], 1.0, None, ALU.add), 1)
            link(nc.vector.reciprocal(sE[:, 0, :], sE[:, 1, :]), 2)
            nc.vector.tensor_tensor(sT, sT, sE[:, 0, :], ALU.mult).then_inc(silu_done, 1)
            dve.wait_ge(c_in, 4 * 16)
            nc.vector.tensor_copy(selr[:, :, :], selt.rearrange("p (k n) -> p k n", k=3)).then_inc(sel_ready, 1)

            def split(k):
                src, dst = job_parts(k)
                dve.wait_ge(raw_hi, k + 1)
                nc.vector.tensor_tensor(dst[LO], src, dst[HI], ALU.subtract).then_inc(raw_lo, 1)

            for k in range(EARLY):
                split(k)
            dve.wait_ge(zeroed, 1)
            dve.wait_ge(raw_lo, EARLY)
            g1, g2 = mrow[:, 0:HID], mrow[:, HID:2 * HID]
            for k in range(6):
                dve.wait_ge(m_full, k + 1)
                ps = mb[k % 2][0:B, :]
                if k in (2, 5):
                    n = 3 + 3 * (k // 3)
                    link(nc.vector.tensor_scalar(g1, ps, -1.0, 0.25, ALU.mult, ALU.max), n)
                    link(nc.vector.scalar_tensor_tensor(out=g1, in0=ps, scalar=0.25, in1=g1, op0=ALU.max, op1=ALU.max), n + 1)
                    nc.vector.tensor_scalar(g2, ps, 0.0, 2.0, ALU.is_ge, ALU.mult).then_inc(m_free, 1)
                    dve.wait_ge(m_free, k + 1)
                    nc.vector.scalar_tensor_tensor(out=gab[0:B, k // 3, :], in0=g2, scalar=1.0, in1=g1,
                                                   op0=ALU.subtract, op1=ALU.mult).then_inc(set_step, 1)
                    dve.wait_ge(set_step, n + 2)
                else:
                    r = (0, 1, None, 2, 3)[k]
                    nc.vector.tensor_scalar(modrow[:, r * HID:(r + 1) * HID], ps, float(k in (1, 4)), None, ALU.add).then_inc(m_free, 1)
            pl.done("mod", "mod", "mod")
            for r in range(2):
                dve.wait_ge(m_full, pl.at("m", r + 1))
                nc.vector.tensor_copy(modT[:, 2 * NC * r:2 * NC * (r + 1), :],
                                      mb[pl.bank("m", r)][:, 0:2 * NC * B].rearrange("p (k b) -> p k b", b=B)).then_inc(m_free, 1)
            pl.done("modT")
            dve.wait_ge(m_free, pl.at("m"))
            nc.vector.tensor_copy(modb[:, :], modT[:, :, 0]).then_inc(mod_b, 1)
            dve.wait_ge(x_in, 16)
            for t in range(NT):
                ins = row_stats(t)
            row_vars(ins)
            rows_normed()
            for c in range(NC):
                feature(c)
            for m in range(NM + 1):
                latent(m)
            for h in range(NH):
                dve.wait_ge(m_hi, pl.at("hi", 1))
                pv = mb[0][:, 0:387].rearrange("p (m n) -> p m n", m=NM)
                nc.vector.tensor_tensor(wps[h % 2][:, LO, :, :], pv[:, :, 0:KVC], wps[h % 2][:, HI, :, :], ALU.subtract)
                nc.vector.tensor_copy(gcol[:, :, h:h + 1], pv[:, :, KVC:KVC + 1])
                nc.vector.tensor_copy(crow[0:1, h:h + 1], mb[0][0:1, 391:392])
                nc.vector.tensor_copy(qbias[:, h:h + 1], mb[0][:, 390:391]).then_inc(m_free, 1)
                dve.wait_ge(m_hi, pl.at("hi", 2))
                nc.vector.tensor_tensor(wvs[h % 2][:, LO, :], mb[1][:, :], wvs[h % 2][:, HI, :], ALU.subtract).then_inc(m_free, 1)
                pl.done("absorb")
                if EARLY + h < ROWS:
                    split(EARLY + h)
            dve.wait_ge(bias_full, 1)
            nc.vector.tensor_copy(bias_s[:, :], sk[0][0:1, :]).then_inc(bias_ev, 1)
            dve.wait_ge(m_free, pl.at("m"))
            dve.wait_ge(g_hi, 1)
            nc.vector.tensor_tensor(gsp[:, LO, :, :], gcol[:, :, :], gsp[:, HI, :, :], ALU.subtract).then_inc(g_lo, 1)
            for k in range(ROWS, ROWS + 2):
                dve.wait_ge(raw_in[k % 2], 16 * (k // 2 + 1))
                h0 = 2 * GH * (k - ROWS)
                nc.vector.tensor_copy(raw[k % 2][0:1, 0:2 * QW].rearrange("p (g n) -> p g n", g=2)[:, :, KW:QW],
                                      crow[0:1, h0:h0 + 2 * GH].rearrange("p (g n) -> p g n", g=2)).then_inc(crow_in, 1)
            for k in range(ROWS, NJ):
                split(k)
            for hl in (HI, LO):
                kv_row(hl)
            for t in range(NT):
                rotate(t, 0)
                rotate(t, 1)
            ready(0, scored=False)
            for j in range(2):
                query(j)
                rope(j, 0)
                rope(j, 1)
            for i in range(NT):
                score(0, i)
                if i:
                    reciprocal(0, i - 1)
            reciprocal(0, NT - 1)

            def group(g, first, last, more):
                if first:
                    for i in range(2):
                        turn(i)
                    if more:
                        ins = row_stats(0)
                    rope(2, 0)
                    turn(2)
                    rope(2, 1)
                    turn(3)
                    query(2)
                    for i in range(NT):
                        score(1, i)
                        if i:
                            reciprocal(1, i - 1)
                    reciprocal(1, NT - 1)
                else:
                    turn(0)
                    turn(1)
                    score(1, 0)
                    score(1, 1)
                    reciprocal(1, 0)
                    score(1, 2)
                    reciprocal(1, 1)
                    reciprocal(1, 2)
                    project(0)
                    turn(2)
                    project(1)
                    score(1, 3)
                    reciprocal(1, 3)
                    project(2)
                    turn(3)
                    rope(2, 0)
                    project(3)
                    rope(2, 1)
                    query(2)
                    if last and more:
                        rows_normed()
                context(0)

                turn(0)
                turn(1)
                if first and more:
                    ins = row_stats(1)
                rope(3, 0)
                score(2, 0)
                score(2, 1)
                reciprocal(2, 0)
                turn(2)
                reciprocal(2, 1)
                rope(3, 1)
                score(2, 2)
                reciprocal(2, 2)
                if not last:
                    rotate(0, 0)
                elif more:
                    feature(0)
                turn(3)
                score(2, 3)
                reciprocal(2, 3)
                if not last:
                    rotate(0, 1)
                elif more:
                    feature(1)
                query(3)
                if not last:
                    rotate(1, 0)
                elif more:
                    feature(2)
                context(1)
                if not last:
                    rotate(1, 1)
                elif more:
                    feature(3)

                turn(0)
                turn(1)
                if first and more:
                    ins = row_stats(2)
                score(3, 0)
                score(3, 1)
                reciprocal(3, 0)
                reciprocal(3, 1)
                if not last:
                    rotate(2, 0)
                turn(2)
                score(3, 2)
                reciprocal(3, 2)
                if not last:
                    rotate(2, 1)
                elif more:
                    latent(0)
                turn(3)
                score(3, 3)
                reciprocal(3, 3)
                if not last:
                    rotate(3, 0)
                    rotate(3, 1)
                    ready(g + 1)
                    query(0)
                elif more:
                    latent(1)
                context(2)
                if not last:
                    rope(0, 0)

                turn(0)
                if not last:
                    rope(0, 1)
                    turn(1)
                    query(1)
                    if first and more:
                        row_vars(row_stats(3))
                    score(0, 0)
                    score(0, 1)
                    reciprocal(0, 0)
                    turn(2)
                    reciprocal(0, 1)
                    rope(1, 0)
                    score(0, 2)
                    reciprocal(0, 2)
                    turn(3)
                    rope(1, 1)
                    score(0, 3)
                    reciprocal(0, 3)
                else:
                    turn(1)
                    if more:
                        latent(2)
                    turn(2)
                    if more:
                        latent(3)
                    turn(3)
                    if more:
                        rotate(0, 0)
                context(3)

            def batch(b, more):
                if more:
                    dve.wait_ge(x_in, pl.at("batch") * 32 + 32)
                group(0, True, False, more)
                with passes(dve, pl, 1, NG - 1, GROUP) as g:
                    group(g, False, False, more)
                if more:
                    nc.vector.tensor_copy(modb[:, 0:2 * NC], modT[:, 0:2 * NC, b + 1])
                nc.vector.tensor_copy(modb[:, 2 * NC:4 * NC], modT[:, 2 * NC:4 * NC, b]).then_inc(mod_b, 1)
                group(NG - 1, False, True, more)
                if more:
                    rotate(0, 1)
                    rotate(1, 0)
                    rotate(1, 1)
                for t in range(NT):
                    residual(t, pl.at("batch") * 32 + (48 if more else 32))
                    if more and t < 2:
                        kv_row(t)
                    if more and t >= 2:
                        rotate(t, 0)
                        rotate(t, 1)
                    normed(t)
                if more:
                    ready(0)
                    query(0)
                    rope(0, 0)
                    rope(0, 1)
                    feature(0)
                    query(1)
                    feature(1)
                    rope(1, 0)
                    feature(2)
                    rope(1, 1)
                    feature(3)
                    for i in range(NT):
                        score(0, i)
                        if i:
                            reciprocal(0, i - 1)
                    reciprocal(0, NT - 1)
                else:
                    for c in range(NC):
                        feature(c)
                experts()
                for k in range(2):
                    dve.wait_ge(t_hi, pl.at("t", 1))
                    at = slice(k * 256, (k + 1) * 256)
                    nc.vector.tensor_tensor(midT[:, LO, at], tb[pl.bank("t")][:, 0:256], midT[:, HI, at], ALU.subtract).then_inc(t_free, 1)
                    pl.done("turn_mid")
                for t in range(NT):
                    dve.wait_ge(f_full, pl.at("y", 1))
                    nc.vector.tensor_tensor(xn[:, t, :], sk[t][:, :], gab[:, 1, :], ALU.mult).then_inc(y_mul, 1)
                    pl.done("ffn_out")
                pl.done("batch")

            with passes(dve, pl, 0, B - 1, BATCH) as b:
                batch(b, True)
            batch(B - 1, False)

        @block.gpsimd
        def _(pool):
            pl = Place()

            def rotate(t, k):
                pool.wait_ge(m_free, pl.at("m", 1))
                u = pl.bank("ab")
                a, r = (ab[:, u, i, :].rearrange("p (j n) -> p j n", n=RD) for i in (0, 1))
                o = rq[:, k, t, :].rearrange("p (j d n) -> p j d n", d=2, n=RD)
                nc.gpsimd.tensor_tensor(o[:, :, 0, :], a, r, ALU.add)
                nc.gpsimd.tensor_tensor(o[:, :, 1, :], a, r, ALU.add).then_inc(rotated, 1)
                pl.done("rotate")

            def normalise(j, i):
                o, w = i * (i + 1) // 2 * P, (i + 1) * P
                pool.wait_ge(s_rec, pl.at("s", 1))
                nc.gpsimd.tensor_tensor(pr[:, j % 2, o:o + w], pr[:, j % 2, o:o + w],
                                        rsm[:, j % 2, i:i + 1].broadcast_to([P, w]), ALU.mult).then_inc(p_norm, 1)
                pl.done("score")

            def rstd_of(k, n):
                pool.wait_ge(ln_var, pl.at("var", 1))
                nc.gpsimd.tensor_tensor(rstd[:, k:k + n], ve[:, k:k + n], nhalf[:, k:k + n], ALU.pow).then_inc(ln_rstd, 1)

            def load(k):
                src, rows, n, a, _, _ = JOBS[k]
                dst = raw[k % 2][0:rows, 0:n]
                pool.dma_start(v3(dst, a) if a > 1 else dst, src).then_inc(raw_in[k % 2], 16)

            def store(k):
                pool.wait_ge(raw_lo, k + 1)
                for dst, hl, a, n in JOBS[k][5]:
                    pool.dma_start(dst, v3(stg[k % 2][0:JOBS[k][1], hl, 0:n].bitcast(F32), a)).then_inc(stg_out[k % 2], 16)

            load(0)
            load(1)
            pool.wait_ge(raw_lo, 1)
            load(2)
            pool.wait_ge(zeroed, 1)
            for k in range(2):
                pool.wait_ge(set_step, 5 + 3 * k)
                pool.dma_start(gate_d[:, k, :], gab[0:B, k, :]).then_inc(gate_out, 16)
            rstd_of(0, NT)
            pool.wait_ge(m_full, 8)
            load(3)
            load(4)
            pl.done("mod", "mod", "mod", "modT", "normed", *["feature"] * NC, *["latent"] * (NM + 1))
            for h in range(NH):
                pool.wait_ge(m_free, pl.at("m", 1))
                src = wps[h % 2].bitcast(F32).rearrange("p k m n -> p (k m n)")
                pool.dma_start(wp_d[h], src).then_inc(wps_out[h % 2], 16)
                if h < 2:
                    pool.dma_start(wp_d[NH + h], src).then_inc(wps_out[h % 2], 16)
                pool.wait_ge(m_free, pl.at("m", 2))
                pool.dma_start(wvo_d[h], wvs[h % 2].bitcast(F32).rearrange("p k n -> p (k n)")).then_inc(wvs_out[h % 2], 16)
                pl.done("absorb")
                k = EARLY + h
                if k < ROWS:
                    store(k)
                    load(k + 2)
            pool.wait_ge(g_lo, 1)
            for hl in (HI, LO):
                for m in range(NM):
                    src = gsp[:, hl, m, :].bitcast(F32)
                    pool.dma_start(wr_d[0:NG, :, hl, m, KW:QW].rearrange("g p n -> p g n"), v3(src, NG)).then_inc(gcol_out, 16)
                    pool.dma_start(wr_d[NG, :, hl, m, KW:QW], src[:, 0:GH]).then_inc(gcol_out, 16)
            for k in range(ROWS, NJ):
                store(k)
                if k + 2 < NJ:
                    load(k + 2)
            pl.done("kv_row", "kv_row")
            for t in range(NT):
                rotate(t, 0)
                rotate(t, 1)
            pl.done("group", "query", "rope", "rope", "query", "rope", "rope")
            for i in range(NT):
                normalise(0, i)

            def group(first, last, more):
                if not first:
                    pl.done(*["project"] * NT)
                pl.done("rope", "rope", "query", "context")
                for i in range(NT):
                    normalise(1, i)

                pl.done("rope", "rope")
                normalise(2, 0)
                normalise(2, 1)
                normalise(2, 2)
                if not last:
                    rotate(0, 0)
                    normalise(2, 3)
                    rotate(0, 1)
                    pl.done("query")
                    rotate(1, 0)
                    pl.done("context")
                    rotate(1, 1)
                else:
                    normalise(2, 3)
                    pl.done("query", "context")
                    if more:
                        pl.done(*["feature"] * NC)

                normalise(3, 0)
                normalise(3, 1)
                if not last:
                    rotate(2, 0)
                    normalise(3, 2)
                    rotate(2, 1)
                    normalise(3, 3)
                    rotate(3, 0)
                    rotate(3, 1)
                    pl.done("group", "query", "context", "rope")

                    pl.done("rope", "query", "rope", "rope", "context")
                    for i in range(NT):
                        normalise(0, i)
                else:
                    normalise(3, 2)
                    normalise(3, 3)
                    if more:
                        pl.done("latent", "latent", "context", "latent", "latent")
                        rotate(0, 0)
                    else:
                        pl.done("context")
                    pl.done("context")

            def batch(b, more):
                group(True, False, more)
                if more:
                    rstd_of(0, NT)
                    pl.done("normed")
                with passes(pool, pl, 1, NG - 1, GROUP):
                    group(False, False, more)
                group(False, True, more)
                if more:
                    rotate(0, 1)
                    rotate(1, 0)
                    rotate(1, 1)
                for t in range(NT):
                    rstd_of(t, 1)
                    pl.done("project", "residual")
                    if more and t < 2:
                        pl.done("kv_row")
                    if more and t >= 2:
                        rotate(t, 0)
                        rotate(t, 1)
                if more:
                    pl.done("group", "query", "rope", "rope", "query", "rope", "rope")
                pl.done(*["feature"] * NC)
                if more:
                    for i in range(NT):
                        normalise(0, i)
                pl.done(*["expert"] * NT)
                pool.wait_ge(gate_step, pl.at("gate", GATE_STEPS))
                gate = sc[:, 0, :].rearrange("p (t e) -> p t e", t=NT).unsqueeze(3).broadcast_to([P, NT, NE, R])
                nc.gpsimd.tensor_tensor(midg.rearrange("p t (e r) -> p t e r", r=R), mid[:, :, 0:NE * R].rearrange("p t (e r) -> p t e r", r=R),
                                        gate, ALU.mult).then_inc(mid_gated, 1)
                pl.done(*["gate_step"] * GATE_STEPS)
                for t in range(NT):
                    pool.wait_ge(y_mul, pl.at("y", Y0 + 1))
                    nc.gpsimd.tensor_tensor(xn[:, t, :], xn[:, t, :], acc[:, t, :], ALU.add).then_inc(y_done, 1)
                    pl.done("ffn_out")
                pl.done(*["step"] * (4 * NT + 2 * more), "batch")

            with passes(pool, pl, 0, B - 1, BATCH) as b:
                batch(b, True)
            batch(B - 1, False)


def constants():
    ident = np.eye(P, dtype=np.float32)
    mask = np.zeros((P, S), np.float32)
    mask[:, S - P:] = np.where(np.arange(P)[None, :] > np.arange(P)[:, None], np.float32(-1e30), np.float32(0))
    power = np.power(10000.0, (np.arange(0, RD, 2, dtype=np.float32) / np.float32(RD)).astype(np.float64)).astype(np.float32)
    inv_freq = np.float32(1) / power
    ang = (np.arange(S, dtype=np.float32)[:, None] * inv_freq[None, :]).astype(np.float64)
    c, s = np.cos(ang).astype(np.float32), np.sin(ang).astype(np.float32)
    tiles = [np.concatenate(h, 1).reshape(NT, P, RD).transpose(1, 0, 2).reshape(P, NT * RD) for h in ((c, c), (-s, s))]
    iota = np.tile(np.arange(NE, dtype=np.float32), (P, 1))
    sel = np.zeros((P, 3, P), np.float32)
    for k in range(3):
        sel[2 * k:2 * k + 2, k, :] = 1
    return np.concatenate([ident, mask, *tiles, iota, sel.reshape(P, 3 * P)], 1)


def kernel(**inputs):
    import concourse.bacc as bacc
    from concourse.bass_utils import run_bass_kernel_spmd

    a = {n: np.asarray(v) for n, v in inputs.items()}
    at, ff = "L0_attn_", "L0_ffn_"

    def by_head(b):
        return b.reshape(NH, HD).T

    laid = {
        "x": a[at + "x"],
        "inputs": np.concatenate([a["L0_c"].T.reshape(NC, P, B).transpose(1, 0, 2).reshape(P, NC * B),
                                  a[at + "b_qd"].reshape(NM, P).T, a[at + "b_kvd"].reshape(P, 1),
                                  by_head(a[at + "b_qu"]), by_head(a[at + "b_ku"]), by_head(a[at + "b_vu"])], 1),
        "consts": constants(),
        "b_o": a[at + "b_o"].reshape(1, HID),
        "wmod": a["L0_wmod"],
        "w_qd": a[at + "W_qd"],
        "w_kvd": a[at + "W_kvd"],
        "heads_w": np.concatenate([a[at + "W_qu"].T, a[at + "W_ku"].T, a[at + "b_ku"].reshape(NH * HD, 1),
                                   a[at + "W_vu"].T, a[at + "W_o"]], 1),
        "w_qr": a[at + "W_qr"],
        "w_kr": a[at + "W_kr"],
        "base_wT": a[ff + "base_w"].T,
        "ffn_a": np.concatenate([a[ff + "lora_A"].transpose(1, 0, 2).reshape(HID, NE * R), a[ff + "router_w"].T], 1),
        "ffn_b": a[ff + "lora_B"].reshape(NE * R, HID),
        "q_row": np.concatenate([a[at + "b_qr"].reshape(NG, KW), np.zeros((NG, GH), np.float32)], 1).reshape(1, NG * QW),
        "k_row": a[at + "b_kr"].reshape(1, NG * KW),
        "f_row": np.concatenate([a[ff + "base_b"], np.zeros(NE * R, np.float32), a[ff + "router_b"]]).reshape(1, HID + FW),
    }
    nc = bacc.Bacc("TRN2", target_bir_lowering=False, num_devices=1)
    arrays, args = {}, []
    for name, v in laid.items():
        v = np.ascontiguousarray(v)
        arrays[f"in_{name}"] = v
        args.append(nc.dram_tensor(f"in_{name}", v.shape, mybir.dt.from_np(v.dtype), kind="ExternalInput").ap())
    args.append(nc.dram_tensor("out_y", (B, S, HID), F32, kind="ExternalOutput").ap())
    build(nc, *args)
    r = run_bass_kernel_spmd(nc, [arrays], core_ids=[0])
    return r.results[0]["out_y"]
```

```python
from contextlib import ExitStack, contextmanager

import numpy as np
import concourse.bass as bass
from concourse import mybir

ALU = mybir.AluOpType
ACT = mybir.ActivationFunctionType
AX = mybir.AxisListType
F32 = mybir.dt.float32
F32R = mybir.dt.float32r
U32 = mybir.dt.uint32

P = 128
B, S, HID = 8, 512, 512
NH, HD, RD = 16, 128, 64
KVC, QC = 128, 384
NE, R = 8, 16
LORA_SCALING = 2.0
EPS = 1e-5
NT = S // P
NC = HID // P
NM = QC // P
GH = 4
NG = NH // GH
QW = GH * RD + GH
KW = GH * RD
FW = NE * R + NE
SCALE = 1.0 / float(np.sqrt(HD + RD))
HI, LO = 0, 1


class Count:

    def __init__(self):
        self.base, self.off = 0, 0
        self.seen = 0

    def at(self, more=0):
        return self.base + (self.off + more)

    def add(self, n=1):
        self.off += n
        self.seen += n


class Place:

    STAGES = {
        "one": dict(m=1),
        "hi": dict(hi=2),
        "mod": dict(m=2),
        "modT": dict(m=2),
        "absorb": dict(m=2, hi=2),
        "normed": dict(var=1, xn=1),
        "feature": dict(m=1, hi=1, h=1),
        "latent": dict(m=1, hi=1),
        "kv_row": dict(m=1),
        "rotate": dict(m=1, ab=1),
        "group": dict(grp=1),
        "query": dict(m=1, hi=1, qm=1),
        "rope": dict(m=1, hi=1),
        "score": dict(s=1),
        "turn": dict(m=1, hi=1),
        "context": dict(m=1, hi=1),
        "project": dict(m=1),
        "projected": dict(pg=1),
        "residual": dict(var=1, xn=1),
        "summed": dict(res=1),
        "step": dict(ln=1),
        "expert": dict(m=1),
        "gate_step": dict(gate=1),
        "turn_mid": dict(m=1, hi=1),
        "ffn_out": dict(y=1),
        "batch": dict(batch=1),
    }
    NAMES = ("m", "hi", "h", "ab", "grp", "qm", "pg", "s", "var", "xn", "res", "ln", "gate", "y", "batch")

    def __init__(self):
        self.c = {n: Count() for n in self.NAMES}
        self.marks = {}
        self.open = []

    def at(self, name, more=0):
        return self.c[name].at(more)

    def slot(self, name, more=0):
        return (self.c[name].seen + more) % RINGS[name]

    def mark(self, key, name):
        self.marks[key] = (name, self.c[name].seen)
        for own, _ in self.open:
            own.add(key)

    def since(self, key, more=0):
        name, seen = self.marks[key]
        for own, read in self.open:
            if key not in own:
                read.add(key)
        return self.at(name, seen - self.c[name].seen + more)

    def done(self, *stages):
        for stage in stages:
            for name, n in self.STAGES[stage].items():
                self.c[name].add(n)


GATE_STEPS = 15
RINGS = dict(m=4, ab=4)
GROUP = dict(turn=GH * NT, score=GH * NT, context=GH, query=GH, rope=2 * GH, rotate=2 * NT, group=1, project=NT, projected=1)
BATCH = dict(turn=NH * NT, score=NH * NT, context=NH, query=NH, rope=2 * NH, rotate=NG * 2 * NT, group=NG, project=NG * NT,
             projected=NG, normed=1, feature=2 * NC, latent=NM + 1, kv_row=2, residual=NT, summed=NT, step=2 * NT + 2, expert=NT,
             gate_step=GATE_STEPS, turn_mid=2, ffn_out=NT, batch=1)


@contextmanager
def passes(eng, place, lo, hi, stages):
    per = {n: sum(k * Place.STAGES[stage].get(n, 0) for stage, k in stages.items()) for n in Place.NAMES}
    assert all(per[n] % k == 0 for n, k in RINGS.items())
    before = {n: c.at() for n, c in place.c.items()}
    seen = {n: c.seen for n, c in place.c.items()}
    ago = {key: seen[n] - at for key, (n, at) in place.marks.items()}
    place.open.append((set(), set()))
    with eng.Fori(lo, hi) as i:
        for n, c in place.c.items():
            c.base, c.off = (before[n] + (i - lo) * per[n] if per[n] else before[n]), 0
        yield i
        short = {n: (c.seen - seen[n], per[n]) for n, c in place.c.items() if c.seen - seen[n] not in (0, per[n])}
        assert not short, short
        skipped = {n for n, c in place.c.items() if c.seen == seen[n]}
    own, read = place.open.pop()
    for key in read:
        n, at = place.marks[key]
        assert place.c[n].seen - at == ago[key], key
    for n, c in place.c.items():
        n_all = 0 if n in skipped else (hi - lo) * per[n]
        c.base, c.off, c.seen = before[n] + n_all, 0, seen[n] + n_all
    for key in own:
        n, at = place.marks[key]
        place.marks[key] = (n, at + (hi - lo - 1) * per[n])


def build(nc, x, inputs, consts, b_o, wmod, w_qd, w_kvd, heads_w, w_qr, w_kr, base_wT, ffn_a, ffn_b,
          q_row, k_row, f_row, out):
    with ExitStack() as ctx:
        def sb(name, shape, dt=F32):
            return ctx.enter_context(nc.sbuf_tensor(name, shape, dt))

        def sem(name):
            return ctx.enter_context(nc.semaphore(name))

        wqd = sb("wqd", [P, 2, NC, QC], F32R)
        wkvd = sb("wkvd", [P, 2, NC, KVC], F32R)
        wk = sb("wk", [P, 2, NG * KW], F32R)
        wp = sb("wp", [P, 2, 2, NM, KVC], F32R)
        wvo = sb("wvo", [P, 2 * GH * HID], F32R)
        wr = sb("wr", [P, 2, NM, QW], F32R)
        brow = sb("brow", [P, NG * QW], F32R)
        selr = sb("selr", [P, 3, P], F32R)
        cst = sb("cst", [P, P + S + 2 * NT * RD + NE])
        idf = cst[:, 0:P]
        maskt = cst[:, P:P + S]
        cost = cst[:, P + S:P + S + NT * RD].rearrange("p (t n) -> p t n", t=NT)
        sint = cst[:, P + S + NT * RD:P + S + 2 * NT * RD].rearrange("p (t n) -> p t n", t=NT)
        iotat = cst[:, P + S + 2 * NT * RD:]
        inp = sb("inp", [P, NC * B + NM + 1 + 3 * NH])
        sT = inp[:, 0:NC * B]
        bqd = inp[:, NC * B:NC * B + NM]
        bkvd = inp[:, NC * B + NM:NC * B + NM + 1]
        bqu = inp[:, NC * B + NM + 1:].rearrange("p (k h) -> p k h", k=3)
        qbias = sb("qbias", [P, NH])
        qbg = sb("qbg", [P, GH])
        modT = sb("modT", [P, 4 * NC, B])
        modb = sb("modb", [P, 4 * NC])
        nhalf = sb("nhalf", [P, NT])
        tiny = sb("tiny", [P, 4])
        tiny2 = sb("tiny2", [P, NT + 1])
        xn = sb("xn", [P, NT, HID])
        acc = sb("acc", [P, NT, HID])
        gab = sb("gab", [P, 2, HID])
        hT = sb("hT", [P, 2, NC, S], F32R)
        qcT = sb("qcT", [P, 2, NM, S], F32R)
        kvT = sb("kvT", [P, 2, S], F32R)
        kvr = sb("kvr", [P, 2, NT, KVC], F32R)
        NR = 2 * NT * GH * 2 * RD
        rr = sb("rr", [P, NR + 2 * RINGS["ab"] * KW])
        rq = rr[:, 0:NR].rearrange("p (k t n) -> p k t n", k=2, t=NT)
        ab = rr[:, NR:].rearrange("p (s k n) -> p s k n", k=2, n=KW)
        cb = sb("cb", [P, NT, GH])
        cbn = sb("cbn", [P, NT, GH])
        qa = sb("qa", [P, 2, 2, S], F32R)
        q2 = sb("q2", [P, 2, S], F32R)
        kk = sb("kk", [P, 2, 2, S], F32R)
        NP_ = NT * (NT + 1) // 2 * P
        pr = sb("pr", [P, 2, NP_])
        pT = sb("pT", [P, 2 * NT * S], F32R)
        cxT = sb("cxT", [P, 2 * GH * S], F32R)
        nmx = sb("nmx", [P, 2, NT])
        nb = sb("nb", [P, 2, NT])
        sm = sb("sm", [P, 2, NT])
        rsm = sb("rsm", [P, 2, NT])
        stats = sb("stats", [P, NT, 6])
        mv = sb("mv", [P, NT, 2])
        ve = sb("ve", [P, NT])
        rstd = sb("rstd", [P, NT])
        sc = sb("sc", [P, 8, NT * NE])
        v8 = sb("v8", [P, NT, NE])
        i8 = sb("i8", [P, NT, NE], U32)
        gcol = sb("gcol", [P, NM, NH])
        gsp = sb("gsp", [P, 2, NM, NH], F32R)
        crow = sb("crow", [1, NH])
        sE = sb("sE", [P, 2, NC * B])

        pTv = pT[:, :].rearrange("p (k j s) -> p k j s", k=2, j=NT)
        cx = cxT[:, :].rearrange("p (k j s) -> p k j s", k=2, j=GH)
        wvov = wvo[:, :].rearrange("p (j k n) -> p j k n", j=GH, k=2)
        basew = pT[:, :].rearrange("p (k c n) -> p k c n", k=2, c=NC)
        NF = NC * FW + HID
        ffw = cxT[:, 0:2 * NF].rearrange("p (k n) -> p k n", k=2)
        fa = ffw[:, :, 0:NC * FW].rearrange("p k (c n) -> p k c n", c=NC)
        fb = ffw[:, :, NC * FW:NF]
        midT = cxT[:, 2 * NF:2 * NF + 2 * S].rearrange("p (k n) -> p k n", k=2)
        mid = pr[:, 1, 0:NT * FW].rearrange("p (t n) -> p t n", t=NT)
        midg = pr[:, 1, 640:640 + NT * P].rearrange("p (t n) -> p t n", t=NT)
        HEADW = QC + KVC + 1 + KVC + HID
        hw = [rr[:, k * 1160:k * 1160 + HEADW] for k in range(2)]
        modw = acc[:, :, :]
        selt = rr[:, 4400:4400 + 3 * P]
        modrow = rr[0:B, 2320:2320 + 4 * HID]
        raw = [pr[:, k, :] for k in range(2)]
        wps = [pT[:, k * 768:(k + 1) * 768].rearrange("p (k m n) -> p k m n", k=2, m=NM) for k in range(2)]
        wvs = [cxT[:, k * 1024:(k + 1) * 1024].rearrange("p (k n) -> p k n", k=2) for k in range(2)]
        stg = [wvo[:, k * 2048:(k + 1) * 2048].rearrange("p (k n) -> p k n", k=2) for k in range(2)]
        bo_t = rr[0:1, 4880:4880 + HID]
        bias_s = rr[0:1, 4880 + HID:4880 + 2 * HID]
        grow = rr[0:B, 4368:4368 + HID]

        mb = [ctx.enter_context(nc.psum_tensor(f"mb{i}", [P, 512], F32)) for i in range(RINGS["m"])]
        sk = [ctx.enter_context(nc.psum_tensor(f"sk{i}", [P, 512], F32)) for i in range(NT)]

        def scratch(name, shape):
            return nc.dram_tensor(name, shape, F32, kind="Internal").ap()

        wp_d = scratch("wp_d", [NH + 2, P, 2 * NM * KVC])
        wvo_d = scratch("wvo_d", [NH, P, 2 * HID])
        wr_d = scratch("wr_d", [NG + 1, P, 2, NM, QW])
        base_d = scratch("base_d", [P, 2, NC * HID])
        ff_d = scratch("ff_d", [P, 2, NF])
        gate_d = scratch("gate_d", [B, 2, HID])
        bias_d = scratch("bias_d", [1, HID])
        row_d = scratch("row_d", [6, NG * QW])

        names = ("c_in x_in wvo_in wr_in base_in ff_in gab_in acc_in brow_in "
                 "gcol_out gate_out bias_out y_out "
                 "m_full m_hi m_free s_full s_min s_bias s_exp s_rec p_norm "
                 "h_mod rotated grp_ready ln_var ln_rstd ln_xn ln_step res_step res_sum mod_b "
                 "gate_step gate_max gate_exp mid_gated f_full y_mul y_done "
                 "raw_hi raw_lo g_hi g_lo set_step silu_e silu_done sel_ready bias_full bias_ev zeroed "
                 "crow_in hw_used").split()
        (c_in, x_in, wvo_in, wr_in, base_in, ff_in, gab_in, acc_in, brow_in,
         gcol_out, gate_out, bias_out, y_out,
         m_full, m_hi, m_free, s_full, s_min, s_bias, s_exp, s_rec, p_norm,
         h_mod, rotated, grp_ready, ln_var, ln_rstd, ln_xn, ln_step, res_step, res_sum, mod_b,
         gate_step, gate_max, gate_exp, mid_gated, f_full, y_mul, y_done,
         raw_hi, raw_lo, g_hi, g_lo, set_step, silu_e, silu_done, sel_ready, bias_full, bias_ev, zeroed,
         crow_in, hw_used) = [sem(n) for n in names]
        modw_in = sem("modw_in")
        hw_in = [sem(f"hw_in{i}") for i in range(2)]
        raw_in = [sem(f"raw_in{i}") for i in range(2)]
        wp_in = [sem(f"wp_in{i}") for i in range(2)]
        wps_out = [sem(f"wps_out{i}") for i in range(2)]
        wvs_out = [sem(f"wvs_out{i}") for i in range(2)]
        stg_out = [sem(f"stg_out{i}") for i in range(2)]
        S0, Y0 = NT, NT

        block = ctx.enter_context(nc.Block())

        def v3(ap, a):
            return ap.rearrange("p (a n) -> p a n", a=a)

        wqd_v = w_qd.rearrange("(c p) n -> p c n", p=P)
        wqr_v = w_qr.rearrange("(m p) n -> m p n", p=P)
        base_v = base_wT.rearrange("(c p) n -> p c n", p=P)
        JOBS = []
        for k in range(2):
            JOBS.append((wqd_v[:, 2 * k:2 * k + 2, :], P, 2 * QC, 2, [wqd[:, hl, 2 * k:2 * k + 2, :] for hl in (HI, LO)], []))
        JOBS.append((w_kvd.rearrange("(c p) n -> p c n", p=P), P, NC * KVC, NC, [wkvd[:, hl, :, :] for hl in (HI, LO)], []))
        EARLY = len(JOBS)
        JOBS.append((w_kr, P, NG * KW, 1, [wk[:, hl, :] for hl in (HI, LO)], []))
        for m in range(NM):
            JOBS.append((wqr_v[m], P, NG * KW, 1, None,
                         [(wr_d[0:NG, :, hl, m, 0:KW].rearrange("g p n -> p g n"), hl, NG * KW, NG) for hl in (HI, LO)]
                         + [(wr_d[NG, :, :, m, 0:KW], None, KW, 1)]))
        for k in range(2):
            JOBS.append((base_v[:, 2 * k:2 * k + 2, :], P, 2 * HID, 2, None,
                         [(base_d[:, :, 2 * k * HID:(2 * k + 2) * HID], None, 2 * HID, 1)]))
        JOBS.append((ffn_a.rearrange("(c p) n -> p c n", p=P), P, NC * FW, NC, None, [(ff_d[:, :, 0:NC * FW], None, NC * FW, 1)]))
        JOBS.append((ffn_b, P, HID, 1, None, [(ff_d[:, :, NC * FW:NF], None, HID, 1)]))

        def row_job(src, n, r0, c0):
            JOBS.append((src, 1, n, 1, None, [(row_d[r0:r0 + 2, c0:c0 + n].unsqueeze(0), None, n, 1)]))

        row_job(k_row, NG * KW, 2, 0)
        row_job(f_row, HID + FW, 4, 0)
        ROWS = len(JOBS)
        for k in range(2):
            row_job(q_row[:, 2 * k * QW:(2 * k + 2) * QW], 2 * QW, 0, 2 * k * QW)
        NJ = len(JOBS)
        stored, total = [], [0, 0]
        for k, job in enumerate(JOBS):
            total[k % 2] += 16 * len(job[5])
            stored.append(total[k % 2])

        def job_parts(k):
            _, rows, n, a, dst, _ = JOBS[k]
            src = raw[k % 2][0:rows, 0:n]
            if dst is None:
                return src, [stg[k % 2][0:rows, hl, 0:n] for hl in (HI, LO)]
            return (v3(src, a) if a > 1 else src), dst

        MODS = 6

        def mod_after(h):
            return h % 2 == 1 and h < 2 * MODS

        @block.sync
        def _(sp):
            pl = Place()
            sp.dma_start(inp[:, :], inputs).then_inc(c_in, 16)
            sp.dma_start(cst[:, :], consts[:, 0:P + S + 2 * NT * RD + NE]).then_inc(c_in, 16)
            sp.dma_start(selt, consts[:, P + S + 2 * NT * RD + NE:]).then_inc(c_in, 16)
            sp.dma_start(bo_t[:, :], b_o).then_inc(c_in, 16)
            wmod_v = wmod.rearrange("(c p) (k n) -> k p c n", p=P, n=HID)
            def head_load(h):
                sp.dma_start(hw[h % 2], heads_w[h * HD:(h + 1) * HD, :]).then_inc(hw_in[h % 2], 16)

            head_load(0)
            sp.dma_start(xn[:, :, :], x[0].rearrange("(t p) n -> p t n", p=P)).then_inc(x_in, 16)
            head_load(1)
            sp.dma_start(modw, wmod_v[0]).then_inc(modw_in, 16)

            def wp_load(k, h):
                sp.dma_start(wp[:, k, :, :, :].bitcast(F32).rearrange("p k m n -> p (k m n)"), wp_d[h]).then_inc(wp_in[k], 16)

            def wvo_load(h0):
                sp.dma_start(wvo[:, :].bitcast(F32).rearrange("p (j n) -> p j n", j=GH),
                             wvo_d[bass.ds(h0, GH)].rearrange("j p n -> p j n")).then_inc(wvo_in, 16)

            for h in range(NH):
                sp.wait_ge(m_free, pl.at("m", 1))
                src = wps[h % 2].bitcast(F32).rearrange("p k m n -> p (k m n)")
                sp.dma_start(wp_d[h], src).then_inc(wps_out[h % 2], 16)
                if h < 2:
                    sp.dma_start(wp_d[NH + h], src).then_inc(wps_out[h % 2], 16)
                if h + 2 < NH:
                    sp.wait_ge(hw_used, h + 1)
                    head_load(h + 2)
                sp.wait_ge(m_free, pl.at("m", 2))
                sp.dma_start(wvo_d[h], wvs[h % 2].bitcast(F32).rearrange("p k n -> p (k n)")).then_inc(wvs_out[h % 2], 16)
                pl.done("absorb")
                if mod_after(h):
                    pl.done("one")
                    if h // 2 + 1 < MODS:
                        sp.wait_ge(m_full, pl.at("m"))
                        sp.dma_start(modw, wmod_v[h // 2 + 1]).then_inc(modw_in, 16)
                if h in (2, 3):
                    sp.wait_ge(wps_out[h % 2], 16 * (2 + 1))
                    wp_load(h % 2, h % 2)
            sp.wait_ge(g_lo, 1)
            for g in range(NG + 1):
                h0 = GH * (g % NG)
                sp.dma_start(wr_d[g, :, :, :, KW:QW].rearrange("p k m n -> p (k m) n"),
                             gsp[:, :, :, h0:h0 + GH].bitcast(F32).rearrange("p k m n -> p (k m) n")).then_inc(gcol_out, 16)
            sp.wait_ge(bias_ev, 1)
            sp.dma_start(bias_d, bias_s[:, :]).then_inc(bias_out, 16)
            for k in (0, 1):
                sp.wait_ge(stg_out[k], total[k])
            sp.wait_ge(zeroed, 1)
            for r0, n in ((0, NG * QW), (2, NG * KW), (4, HID + FW)):
                sp.dma_start(brow[r0:r0 + 2, 0:n].bitcast(F32), row_d[r0:r0 + 2, 0:n]).then_inc(brow_in, 16)
            sp.wait_ge(gcol_out, 16 * (NG + 1))
            sp.dma_start(wr[:, :, :, :].bitcast(F32), wr_d[0]).then_inc(wr_in, 16)
            for k in (0, 1):
                sp.wait_ge(wps_out[k], 16 * (NH // 2 + 1))
                sp.wait_ge(wvs_out[k], 16 * (NH // 2))
            wvo_load(0)
            sp.wait_ge(bias_out, 16)
            sp.wait_ge(gate_out, 32)
            pl.done("modT", "normed", *["feature"] * NC, *["latent"] * (NM + 1), "kv_row", "kv_row")

            def rotated_group(g, n):
                pl.done(*["rotate"] * n, "group")
                sp.wait_ge(m_full, pl.at("m"))
                sp.dma_start(wr[:, :, :, :].bitcast(F32), wr_d[g]).then_inc(wr_in, 16)

            def query(j, h):
                pl.done("query")
                sp.wait_ge(m_full, pl.at("m"))
                wp_load(j % 2, h)

            def projected(h0):
                pl.done("project", "projected")
                sp.wait_ge(m_full, pl.at("m"))
                wvo_load(h0)

            def acc_load():
                sp.dma_start(acc[:, :, :], bias_d.unsqueeze(1).broadcast_to([P, NT, HID])).then_inc(acc_in, 16)

            acc_load()
            query(0, 2)
            query(1, 3)
            rotated_group(1, 2 * NT)
            pl.done(*["rope"] * 4)

            def group(b, g, first, last, more):
                pl.done("turn", "turn")
                if first:
                    pl.done("rope", "turn", "rope", "turn")
                    query(2, GH * g + 4)
                    pl.done("rope", "rope", "context")
                else:
                    pl.done("rope", "turn", "project", "rope", "project", "turn", "project", "rope")
                    query(2, GH * g + 4)
                    pl.done("rope")
                    projected(GH * g)
                if not last:
                    query(3, GH * g + 5)
                if not first:
                    pl.done("context")

                pl.done("turn", "turn", "turn")
                if not last:
                    pl.done("rotate", "rotate", "rotate", "turn", "rotate", "rotate", "context", "rotate", "turn", "turn",
                            "rotate", "turn")
                    rotated_group(g + 2, 1)
                    pl.done("turn")
                    query(0, GH * g + 6)
                    pl.done("rope", "rope", "context", "turn", "turn")
                    query(1, GH * g + 7)
                    pl.done("turn", "turn", "rope", "rope", "context")
                else:
                    pl.done("turn")
                    if more:
                        pl.done("feature", "feature")
                    query(3, GH * g + 5)
                    pl.done("context")
                    if more:
                        pl.done("feature", "feature")
                        sp.wait_ge(m_full, pl.at("m"))
                        sp.dma_start(xn[:, :, :], x[b].rearrange("(t p) n -> p t n", p=P)).then_inc(x_in, 16)
                        pl.done(*["latent"] * (NM + 1), "rotate")
                    pl.done(*["turn"] * (2 * NT), "context", "context")

            def batch(b, more):
                sp.dma_start(gab[:, :, :], gate_d[bass.ds(b, 1)].broadcast_to([P, 2, HID])).then_inc(gab_in, 16)
                sp.dma_start(xn[:, :, :], x[b + 1 if more else b].rearrange("(t p) n -> p t n", p=P)).then_inc(x_in, 16)
                group(b, 0, True, False, more)
                if more:
                    pl.done("normed")
                with passes(sp, pl, 1, NG - 1, GROUP) as g:
                    group(b, g, False, False, more)
                group(b, NG - 1, False, True, more)
                sp.wait_ge(m_full, pl.at("m"))
                sp.dma_start(pT[:, :].bitcast(F32), base_d.rearrange("p k n -> p (k n)")).then_inc(base_in, 16)
                pl.done("project", "project", "project")
                if more:
                    pl.done(*["rotate"] * (2 * NT - 2), "kv_row", "kv_row")
                    rotated_group(1, 1)
                projected(0)
                sp.dma_start(cxT[:, 0:2 * NF].bitcast(F32), ff_d.rearrange("p k n -> p (k n)")).then_inc(ff_in, 16)
                pl.done(*["residual"] * NT)
                if more:
                    query(0, 2)
                    pl.done("rope", "rope")
                    query(1, 3)
                    pl.done("rope", "rope", *["feature"] * NC)
                else:
                    pl.done(*["feature"] * NC)
                pl.done(*["expert"] * NT, "turn_mid", "turn_mid")
                for t in range(NT):
                    sp.wait_ge(y_done, pl.at("y", 1))
                    sp.dma_start(out[b, t * P:(t + 1) * P, :], xn[:, t, :]).then_inc(y_out, 16)
                    pl.done("ffn_out")
                sp.wait_ge(y_out, pl.at("y") * 16)
                if more:
                    acc_load()
                pl.done(*["gate_step"] * GATE_STEPS, *["summed"] * NT, *["step"] * (2 * NT + 2 * more), "batch")

            with passes(sp, pl, 0, B - 1, BATCH) as b:
                batch(b, True)
            batch(B - 1, False)
            sp.wait_ge(wvo_in, 16 * (NG * B + 1))
            for k in (0, 1):
                sp.wait_ge(wp_in[k], 16 * (NH // 2 * B + 1))

        @block.tensor
        def _(pe):
            pl = Place()

            def m_bank():
                free = pl.at("m", 1 - RINGS["m"])
                if not (isinstance(free, int) and free < 1):
                    pe.wait_ge(m_free, free)
                return mb[pl.slot("m")]

            def three(o, a, b, first, last):
                nc.tensor.matmul(o, a[HI], b[HI], start=first, stop=False, skip_group_check=True)
                nc.tensor.matmul(o, a[HI], b[LO], start=False, stop=False, skip_group_check=True)
                return nc.tensor.matmul(o, a[LO], b[HI], start=False, stop=last, skip_group_check=True)

            def feature(c):
                ps = m_bank()
                for t in range(NT):
                    mm = nc.tensor.transpose(ps[:, t * P:(t + 1) * P], xn[:, t, c * P:(c + 1) * P], idf)
                mm.then_inc(m_full, 1)
                pl.done("feature")
                pl.mark(("h", c), "m")

            def latent(m):
                ps = m_bank()
                for c in range(NC):
                    if m == 0:
                        pe.wait_ge(m_free, pl.since(("h", c)))
                    w = [wqd[:, hl, c, m * P:(m + 1) * P] if m < NM else wkvd[:, hl, c, :] for hl in (HI, LO)]
                    mm = three(ps[:, :], w, [hT[:, hl, c, :] for hl in (HI, LO)], c == 0, c == NC - 1)
                mm.then_inc(m_full, 1)
                pl.done("latent")
                pl.mark(("latent", m), "m")

            def kv_row(hl):
                ps = m_bank()
                pe.wait_ge(m_free, pl.since(("latent", NM)))
                for t in range(NT):
                    mm = nc.tensor.transpose(ps[:, t * P:(t + 1) * P], kvT[:, hl, t * P:(t + 1) * P].bitcast(F32), idf)
                mm.then_inc(m_full, 1)
                pl.done("kv_row")

            def rotate(g, t, k, new=False):
                tok = slice(t * P, (t + 1) * P)
                ps = m_bank()
                if k == 0:
                    if t == 0:
                        pe.wait_ge(wr_in, pl.at("grp") * 16 + 16)
                        if new:
                            pe.wait_ge(m_free, pl.since(("latent", NM - 1)))
                    for m in range(NM):
                        three(ps[:, 0:QW], [qcT[:, hl, m, tok] for hl in (HI, LO)], [wr[:, hl, m, :] for hl in (HI, LO)], m == 0, False)
                    nc.tensor.matmul(ps[:, 0:QW], selr[:, 0, :], brow[:, bass.ds(g * QW, QW)],
                                     start=False, stop=True, skip_group_check=True).then_inc(m_full, 1)
                else:
                    if t == 0 and new:
                        pe.wait_ge(m_free, pl.since(("latent", NM)))
                    three(ps[:, 0:KW], [kvT[:, hl, tok] for hl in (HI, LO)],
                          [wk[:, hl, bass.ds(g * KW, KW)] for hl in (HI, LO)], True, False)
                    nc.tensor.matmul(ps[:, 0:KW], selr[:, 1, :], brow[:, bass.ds(g * KW, KW)],
                                     start=False, stop=True, skip_group_check=True).then_inc(m_full, 1)
                pl.done("rotate")

            def query(j):
                pe.wait_ge(wp_in[j % 2], pl.at("qm") * 8 + (8 if j % 2 else 16))
                ps = m_bank()
                for m in range(NM):
                    mm = three(ps[:, :], [wp[:, j % 2, hl, m, :] for hl in (HI, LO)], [qcT[:, hl, m, :] for hl in (HI, LO)], m == 0, m == NM - 1)
                mm.then_inc(m_full, 1)
                pl.done("query")
                pl.mark(("q", j % 2), "m")

            def rope(j, k):
                ps = m_bank()
                if j == 0 and k == 0:
                    pe.wait_ge(rotated, pl.at("ab"))
                for t in range(NT):
                    mm = nc.tensor.transpose(ps[:, t * P:(t + 1) * P], rq[:, k, t, j * P:(j + 1) * P], idf)
                mm.then_inc(m_full, 1)
                pl.done("rope")
                pl.mark(("q", j % 2), "m")

            def score(j, i, after_y=False):
                if i == 0:
                    pe.wait_ge(m_free, pl.since(("q", j % 2)))
                q, w = slice(i * P, (i + 1) * P), (i + 1) * P
                if after_y:
                    pe.wait_ge(y_mul, pl.at("y", i + 1))
                pe.wait_ge(s_exp, pl.at("s", 1))
                ps = sk[i][:, 0:w]
                three(ps, [qa[:, j % 2, hl, q] for hl in (HI, LO)], [kvT[:, hl, 0:w] for hl in (HI, LO)], True, False)
                nc.tensor.matmul(ps, q2[:, j % 2, q], kk[:, j % 2, HI, 0:w], start=False, stop=False, skip_group_check=True)
                nc.tensor.matmul(ps, q2[:, j % 2, q], kk[:, j % 2, LO, 0:w], start=False, stop=True,
                                 skip_group_check=True).then_inc(s_full, 1)
                pl.done("score")
                pl.mark(("s", j % 2, i), "s")

            def turn(j, i):
                ps = m_bank()
                pe.wait_ge(p_norm, pl.since(("s", j % 2, i)))
                o = i * (i + 1) // 2 * P
                for k in range(i + 1):
                    mm = nc.tensor.transpose(ps[:, k * P:(k + 1) * P], pr[:, j % 2, o + k * P:o + (k + 1) * P], idf)
                mm.then_inc(m_full, 1)
                pl.done("turn")
                pl.mark("turned", "m")

            def context(j):
                ps = m_bank()
                pe.wait_ge(m_free, pl.since("turned"))
                for k in range(NT):
                    q = slice(k * P, S)
                    mm = three(ps[:, q], [kvr[:, hl, k, :] for hl in (HI, LO)], [pTv[:, hl, k, q] for hl in (HI, LO)], k == 0, k == NT - 1)
                mm.then_inc(m_full, 1)
                pl.done("context")
                pl.mark("cx", "m")

            def project(t):
                ps = m_bank()
                if t == 0:
                    pe.wait_ge(wvo_in, pl.at("pg") * 16 + 16)
                    pe.wait_ge(m_free, pl.since("cx"))
                for j in range(GH):
                    mm = three(ps[:, :], [cx[:, hl, j, t * P:(t + 1) * P] for hl in (HI, LO)],
                               [wvov[:, j, hl, :] for hl in (HI, LO)], j == 0, j == GH - 1)
                mm.then_inc(m_full, 1)
                pl.done("project")
                if t == NT - 1:
                    pl.done("projected")

            pe.wait_ge(silu_done, 1)
            for h in range(NH):
                pe.wait_ge(hw_in[h % 2], 16 * (h // 2 + 1))
                w = hw[h % 2]
                ku, vu, wo = w[:, QC:QC + KVC], w[:, QC + KVC + 1:QC + 2 * KVC + 1], w[:, QC + 2 * KVC + 1:HEADW]
                ps = m_bank()
                for m in range(NM):
                    nc.tensor.matmul(ps[:, m * 129:(m + 1) * 129], w[:, m * P:(m + 1) * P], w[:, QC:QC + KVC + 1], start=True, stop=True)
                nc.tensor.matmul(ps[:, 390:391], ku, bqu[:, 0, h:h + 1], start=True, stop=True)
                nc.tensor.matmul(ps[0:1, 391:392], bqu[:, 1, h:h + 1], bqu[:, 0, h:h + 1], start=True, stop=True).then_inc(m_full, 1)
                pl.done("one")
                ps = m_bank()
                nc.tensor.matmul(ps[:, :], vu, wo, start=True, stop=True).then_inc(m_full, 1)
                nc.tensor.matmul(sk[0][0:1, :], bqu[:, 2, h:h + 1], wo, start=(h == 0), stop=False, skip_group_check=True).then_inc(hw_used, 1)
                pl.done("one", "hi")
                if mod_after(h):
                    ps = m_bank()
                    pe.wait_ge(modw_in, 16 * (h // 2 + 1))
                    for c in range(NC):
                        mm = nc.tensor.matmul(ps[0:B, :], sT[:, c * B:(c + 1) * B], modw[:, c, :], start=(c == 0), stop=(c == NC - 1))
                    mm.then_inc(m_full, 1)
                    pl.done("one")
            nc.tensor.matmul(sk[0][0:1, :], idf[0:1, 0:1], bo_t[:, :], start=False, stop=True, skip_group_check=True).then_inc(bias_full, 1)
            for r in range(2):
                ps = m_bank()
                if r == 0:
                    pe.wait_ge(m_free, pl.at("m"))
                for k in range(2):
                    for c in range(NC):
                        o = (2 * r + k) * HID + c * P
                        mm = nc.tensor.transpose(ps[:, (k * NC + c) * B:(k * NC + c + 1) * B], modrow[:, o:o + P], idf[0:B, 0:B])
                mm.then_inc(m_full, 1)
                pl.done("one")
            pl.done("normed")
            pe.wait_ge(ln_xn, 1)
            for c in range(NC):
                feature(c)
            pe.wait_ge(raw_lo, EARLY)
            for m in range(NM + 1):
                latent(m)
            kv_row(HI)
            kv_row(LO)
            query(0)
            query(1)
            pe.wait_ge(sel_ready, 1)
            pe.wait_ge(raw_lo, NJ)
            pe.wait_ge(brow_in, 3 * 16)
            for t in range(NT):
                rotate(0, t, 0)
                rotate(0, t, 1)
            pl.done("group")
            for j in range(2):
                rope(j, 0)
                rope(j, 1)
            pe.wait_ge(bias_ev, 1)
            for i in range(NT):
                score(0, i)

            def group(g, first, last, more):
                turn(0, 0)
                turn(0, 1)
                if first:
                    rope(2, 0)
                    turn(0, 2)
                    rope(2, 1)
                    turn(0, 3)
                    query(2)
                    for i in range(NT):
                        score(1, i, after_y=True)
                    rope(3, 0)
                    rope(3, 1)
                    context(0)
                    query(3)
                else:
                    rope(2, 0)
                    score(1, 0)
                    score(1, 1)
                    score(1, 2)
                    turn(0, 2)
                    project(0)
                    rope(2, 1)
                    project(1)
                    score(1, 3)
                    turn(0, 3)
                    project(2)
                    rope(3, 0)
                    query(2)
                    rope(3, 1)
                    project(3)
                    if not last:
                        query(3)
                    context(0)

                turn(1, 0)
                turn(1, 1)
                score(2, 0)
                score(2, 1)
                if not last:
                    rotate(g + 1, 0, 0)
                turn(1, 2)
                score(2, 2)
                if not last:
                    rotate(g + 1, 0, 1)
                    rotate(g + 1, 1, 0)
                turn(1, 3)
                score(2, 3)
                if not last:
                    rotate(g + 1, 1, 1)
                    rotate(g + 1, 2, 0)
                else:
                    if more:
                        pe.wait_ge(ln_xn, pl.at("xn"))
                        feature(0)
                        feature(1)
                    query(3)
                context(1)
                if not last:
                    rotate(g + 1, 2, 1)
                elif more:
                    feature(2)
                    feature(3)

                turn(2, 0)
                turn(2, 1)
                score(3, 0)
                score(3, 1)
                if not last:
                    rotate(g + 1, 3, 0)
                elif more:
                    latent(0)
                turn(2, 2)
                score(3, 2)
                if not last:
                    rotate(g + 1, 3, 1)
                    pl.done("group")
                turn(2, 3)
                score(3, 3)
                if not last:
                    query(0)
                    rope(0, 0)
                    rope(0, 1)
                elif more:
                    latent(1)
                context(2)

                turn(3, 0)
                turn(3, 1)
                if not last:
                    query(1)
                    turn(3, 2)
                    score(0, 0)
                    score(0, 1)
                    turn(3, 3)
                    rope(1, 0)
                    score(0, 2)
                    rope(1, 1)
                    score(0, 3)
                else:
                    if more:
                        latent(2)
                    turn(3, 2)
                    if more:
                        latent(3)
                    turn(3, 3)
                    if more:
                        rotate(0, 0, 0, new=True)
                context(3)

            def batch(b, more):
                pl.mark(("q", 1), "m")
                group(0, True, False, more)
                if more:
                    pl.done("normed")
                with passes(pe, pl, 1, NG - 1, GROUP) as g:
                    group(g, False, False, more)
                group(NG - 1, False, True, more)
                if more:
                    rotate(0, 0, 1, new=True)
                    rotate(0, 1, 0)
                    rotate(0, 1, 1)
                for t in range(NT):
                    if more and t >= 2:
                        rotate(0, t, 0)
                        rotate(0, t, 1)
                    project(t)
                    pl.done("residual")
                    if more and t < 2:
                        kv_row(t)
                if more:
                    pl.done("group")
                    query(0)
                    rope(0, 0)
                    rope(0, 1)
                    query(1)
                    rope(1, 0)
                    rope(1, 1)
                pe.wait_ge(ln_xn, pl.at("xn"))
                feature(0)
                feature(1)
                feature(2)
                if more:
                    score(0, 0)
                feature(3)
                if more:
                    score(0, 1)
                    score(0, 2)
                    score(0, 3)
                pe.wait_ge(ff_in, pl.at("batch") * 16 + 16)
                for t in range(NT):
                    ps = m_bank()
                    tok = slice(t * P, (t + 1) * P)
                    for c in range(NC):
                        if t == 0:
                            pe.wait_ge(m_free, pl.since(("h", c)))
                        three(ps[:, 0:FW], [hT[:, hl, c, tok] for hl in (HI, LO)], [fa[:, hl, c, :] for hl in (HI, LO)], c == 0, False)
                    nc.tensor.matmul(ps[:, 0:FW], selr[:, 2, :], brow[:, HID:HID + FW], start=False, stop=True,
                                     skip_group_check=True).then_inc(m_full, 1)
                    pl.done("expert")
                pe.wait_ge(base_in, pl.at("batch") * 16 + 16)
                for t in range(NT):
                    pe.wait_ge(s_exp, pl.at("s", t + 1))
                    tok = slice(t * P, (t + 1) * P)
                    for c in range(NC):
                        three(sk[t][:, :], [hT[:, hl, c, tok] for hl in (HI, LO)], [basew[:, hl, c, :] for hl in (HI, LO)], c == 0, False)
                    nc.tensor.matmul(sk[t][:, :], selr[:, 2, :], brow[:, 0:HID], start=False, stop=False, skip_group_check=True)
                pe.wait_ge(mid_gated, pl.at("batch") + 1)
                for k in range(2):
                    ps = m_bank()
                    for t in range(2):
                        mm = nc.tensor.transpose(ps[:, t * P:(t + 1) * P], midg[:, 2 * k + t, :], idf)
                    mm.then_inc(m_full, 1)
                    pl.done("turn_mid")
                for t in range(NT):
                    if t % 2 == 0:
                        pe.wait_ge(m_free, pl.at("m", t // 2 - 1))
                    tok = slice(t * P, (t + 1) * P)
                    three(sk[t][:, :], [midT[:, hl, tok] for hl in (HI, LO)], [fb[:, hl, :] for hl in (HI, LO)], False, True).then_inc(f_full, 1)
                    pl.done("ffn_out")
                pl.done(*["gate_step"] * GATE_STEPS, *["summed"] * NT, *["step"] * (2 * NT + 2 * more), "batch")

            with passes(pe, pl, 0, B - 1, BATCH) as b:
                batch(b, True)
            batch(B - 1, False)

        @block.scalar
        def _(act):
            pl = Place()

            def hi_of(dst, bias=None):
                src = mb[pl.slot("m")]
                act.wait_ge(m_full, pl.at("m", 1))
                if bias is None:
                    nc.scalar.activation(dst, src[:, :], ACT.Copy).then_inc(m_hi, 1)
                else:
                    nc.scalar.activation(dst, src[:, :], ACT.Identity, bias=bias).then_inc(m_hi, 1)

            def feature(c, half):
                ps = mb[pl.slot("m")]
                o = 2 * NC * half + c
                act.wait_ge(m_full, pl.at("m", 1))
                nc.scalar.activation(ps[:, :], ps[:, :], ACT.Identity, bias=modb[:, o:o + 1],
                                     scale=modb[:, o + NC:o + NC + 1]).then_inc(h_mod, 1)
                act.wait_ge(h_mod, pl.at("h", 1))
                nc.scalar.activation(hT[:, HI, c, :], ps[:, :], ACT.Copy).then_inc(m_hi, 1)
                pl.done("feature")

            def latent(m):
                if m < NM:
                    hi_of(qcT[:, HI, m, :], bqd[:, m:m + 1])
                else:
                    hi_of(kvT[:, HI, :], bkvd)
                pl.done("latent")

            def query(j):
                if j == 0:
                    act.wait_ge(grp_ready, pl.at("grp"))
                hi_of(qa[:, j % 2, HI, :], qbg[:, j:j + 1])
                pl.done("query")

            def rope(j, k):
                hi_of(kk[:, j % 2, HI, :] if k else q2[:, j % 2, :])
                pl.done("rope")

            def score(j, i):
                o, w = i * (i + 1) // 2 * P, (i + 1) * P
                act.wait_ge(s_bias, pl.at("s", 1))
                nc.scalar.activation(pr[:, j % 2, o:o + w], sk[i][:, 0:w], ACT.Exp, bias=nb[:, j % 2, i:i + 1],
                                     scale=-1.0, accum_out=sm[:, j % 2, i:i + 1]).then_inc(s_exp, 1)
                pl.done("score")

            def turn(i):
                w = (i + 1) * P
                act.wait_ge(m_full, pl.at("m", 1))
                nc.scalar.activation(pTv[:, HI, 0:i + 1, i * P:(i + 1) * P],
                                     mb[pl.slot("m")][:, 0:w].rearrange("p (k n) -> p k n", n=P), ACT.Copy).then_inc(m_hi, 1)
                pl.done("turn")

            def context(j):
                hi_of(cx[:, HI, j, :])
                pl.done("context")

            act.wait_ge(c_in, 4 * 16)
            nc.scalar.activation(sE[:, 0, :], sT, ACT.Exp, scale=-1.0).then_inc(silu_e, 1)
            for k in range(S0):
                nc.scalar.activation(tiny[:, k:k + 1], idf[:, k:k + 1], ACT.Copy).then_inc(s_exp, 1)

            def split(k):
                src, dst = job_parts(k)
                act.wait_ge(raw_in[k % 2], 16 * (k // 2 + 1))
                if k >= 2 and stored[k - 2]:
                    act.wait_ge(stg_out[k % 2], stored[k - 2])
                if ROWS <= k < ROWS + 2:
                    act.wait_ge(crow_in, k - ROWS + 1)
                nc.scalar.activation(dst[HI], src, ACT.Copy).then_inc(raw_hi, 1)

            for k in range(EARLY):
                split(k)
            for h in range(NH):
                act.wait_ge(m_full, pl.at("m", 1))
                if h >= 2:
                    act.wait_ge(wps_out[h % 2], 16 * (h // 2 + 1))
                nc.scalar.activation(wps[h % 2][:, HI, :, :], mb[pl.slot("m")][:, 0:387].rearrange("p (m n) -> p m n", m=NM)[:, :, 0:KVC],
                                     ACT.Copy).then_inc(m_hi, 1)
                act.wait_ge(m_full, pl.at("m", 2))
                if h >= 2:
                    act.wait_ge(wvs_out[h % 2], 16 * (h // 2))
                nc.scalar.activation(wvs[h % 2][:, HI, :], mb[pl.slot("m", 1)][:, :], ACT.Copy).then_inc(m_hi, 1)
                pl.done("absorb")
                if mod_after(h):
                    pl.done("one")
                if EARLY + h < ROWS:
                    split(EARLY + h)
            act.wait_ge(m_free, pl.at("m"))
            nc.scalar.activation(gsp[:, HI, :, :], gcol[:, :, :], ACT.Copy).then_inc(g_hi, 1)
            for k in range(ROWS, NJ):
                split(k)
            pl.done("modT", "normed")
            act.wait_ge(mod_b, 1)
            for c in range(NC):
                feature(c, 0)
            for m in range(NM + 1):
                latent(m)
            pl.done("kv_row", "kv_row", "group")
            query(0)
            query(1)
            pl.done(*["rotate"] * (2 * NT))
            for j in range(2):
                rope(j, 0)
                rope(j, 1)
            for i in range(NT):
                score(0, i)

            def group(first, last, more):
                turn(0)
                turn(1)
                if first:
                    rope(2, 0)
                    turn(2)
                    rope(2, 1)
                    turn(3)
                    query(2)
                    for i in range(NT):
                        score(1, i)
                    rope(3, 0)
                    rope(3, 1)
                    context(0)
                    query(3)
                else:
                    rope(2, 0)
                    score(1, 0)
                    score(1, 1)
                    turn(2)
                    score(1, 2)
                    pl.done("project")
                    rope(2, 1)
                    pl.done("project")
                    turn(3)
                    score(1, 3)
                    pl.done("project")
                    rope(3, 0)
                    query(2)
                    rope(3, 1)
                    pl.done("project")
                    if not last:
                        query(3)
                    context(0)

                turn(0)
                turn(1)
                score(2, 0)
                if not last:
                    score(2, 1)
                    pl.done("rotate")
                    turn(2)
                    score(2, 2)
                    pl.done("rotate", "rotate")
                    turn(3)
                    score(2, 3)
                    pl.done("rotate", "rotate")
                else:
                    turn(2)
                    score(2, 1)
                    turn(3)
                    score(2, 2)
                    score(2, 3)
                    if more:
                        feature(0, 0)
                        feature(1, 0)
                    query(3)
                context(1)
                if not last:
                    pl.done("rotate")
                elif more:
                    feature(2, 0)
                    feature(3, 0)

                turn(0)
                turn(1)
                score(3, 0)
                score(3, 1)
                if not last:
                    pl.done("rotate")
                elif more:
                    latent(0)
                turn(2)
                score(3, 2)
                if not last:
                    pl.done("rotate", "group")
                turn(3)
                score(3, 3)
                if not last:
                    query(0)
                    rope(0, 0)
                    rope(0, 1)
                elif more:
                    latent(1)
                context(2)

                turn(0)
                turn(1)
                if not last:
                    query(1)
                    turn(2)
                    turn(3)
                    score(0, 0)
                    rope(1, 0)
                    score(0, 1)
                    rope(1, 1)
                    score(0, 2)
                    score(0, 3)
                else:
                    if more:
                        latent(2)
                    turn(2)
                    if more:
                        latent(3)
                    turn(3)
                    if more:
                        pl.done("rotate")
                context(3)

            def batch(b, more):
                group(True, False, more)
                if more:
                    pl.done("normed")
                with passes(act, pl, 1, NG - 1, GROUP):
                    group(False, False, more)
                act.wait_ge(mod_b, pl.at("batch") + 2)
                group(False, True, more)
                pl.done(*["project", "residual"] * NT)
                if more:
                    pl.done(*["rotate"] * (2 * NT - 1), "kv_row", "kv_row", "group")
                    query(0)
                    rope(0, 0)
                    rope(0, 1)
                    query(1)
                    rope(1, 0)
                    rope(1, 1)
                    feature(0, 1)
                    feature(1, 1)
                    feature(2, 1)
                    feature(3, 1)
                    for i in range(NT):
                        score(0, i)
                else:
                    for c in range(NC):
                        feature(c, 1)
                pl.done(*["expert"] * NT)
                act.wait_ge(gate_max, pl.at("batch") + 1)
                nc.scalar.activation(sc[:, 1, :], sc[:, 0, :], ACT.Exp).then_inc(gate_exp, 1)
                pl.done(*["gate_step"] * GATE_STEPS)
                for k in range(2):
                    act.wait_ge(m_full, pl.at("m", 1))
                    nc.scalar.activation(midT[:, HI, k * 256:(k + 1) * 256], mb[pl.slot("m")][:, 0:256], ACT.Copy).then_inc(m_hi, 1)
                    pl.done("turn_mid")
                pl.done(*["ffn_out"] * NT, *["summed"] * NT, *["step"] * (2 * NT + 2 * more), "batch")

            with passes(act, pl, 0, B - 1, BATCH) as b:
                batch(b, True)
            batch(B - 1, False)

        @block.vector
        def _(dve):
            pl = Place()

            def carry():
                nc.vector.tensor_copy(tiny2[:, Y0:], tiny2[:, 0:1])

            def lo_of(dst, hi, bias=None, rows=slice(0, P)):
                src = mb[pl.slot("m")][rows, :]
                dve.wait_ge(m_hi, pl.at("hi", 1))
                if bias is None:
                    nc.vector.tensor_tensor(dst, src, hi, ALU.subtract).then_inc(m_free, 1)
                else:
                    nc.vector.scalar_tensor_tensor(out=dst, in0=src, scalar=bias, in1=hi,
                                                   op0=ALU.add, op1=ALU.subtract).then_inc(m_free, 1)

            def feature(c):
                lo_of(hT[:, LO, c, :], hT[:, HI, c, :])
                pl.done("feature")

            def latent(m):
                if m < NM:
                    lo_of(qcT[:, LO, m, :], qcT[:, HI, m, :], bqd[:, m:m + 1])
                else:
                    lo_of(kvT[:, LO, :], kvT[:, HI, :], bkvd)
                pl.done("latent")

            def kv_row(hl):
                dve.wait_ge(m_full, pl.at("m", 1))
                nc.vector.tensor_copy(kvr[:, hl, :, :], mb[pl.slot("m")][:, :].rearrange("p (t n) -> p t n", t=NT)).then_inc(m_free, 1)
                pl.done("kv_row")

            def rotate(t, k):
                half = RD // 2
                u = pl.slot("ab")
                dve.wait_ge(m_full, pl.at("m", 1))
                free = pl.at("ab", 1 - RINGS["ab"])
                if not (isinstance(free, int) and free < 1):
                    dve.wait_ge(rotated, free)
                ps = mb[pl.slot("m")]
                v = ps[:, 0:KW].rearrange("p (j n) -> p j n", n=RD)
                a, r = (ab[:, u, i, :].rearrange("p (j n) -> p j n", n=RD) for i in (0, 1))
                nc.vector.tensor_tensor(a, v, cost[:, t, :].unsqueeze(1).broadcast_to([P, GH, RD]), ALU.mult)
                nc.vector.tensor_tensor(r[:, :, 0:half], v[:, :, half:RD],
                                        sint[:, t, 0:half].unsqueeze(1).broadcast_to([P, GH, half]), ALU.mult)
                if k == 0:
                    nc.vector.tensor_scalar(cbn[:, t, :], ps[:, KW:QW], -SCALE, None, ALU.mult)
                nc.vector.tensor_tensor(r[:, :, half:RD], v[:, :, 0:half],
                                        sint[:, t, half:RD].unsqueeze(1).broadcast_to([P, GH, half]), ALU.mult).then_inc(m_free, 1)
                pl.done("rotate")

            def ready(g):
                dve.wait_ge(m_free, pl.at("m"))
                dve.wait_ge(s_bias, pl.at("s"))
                nc.vector.tensor_copy(cb[:, :, :], cbn[:, :, :])
                nc.vector.tensor_copy(qbg[:, :], qbias[:, bass.ds(g * GH, GH)]).then_inc(grp_ready, 1)
                pl.done("group")

            def query(j):
                if j == 0:
                    dve.wait_ge(grp_ready, pl.at("grp"))
                lo_of(qa[:, j % 2, LO, :], qa[:, j % 2, HI, :], qbg[:, j:j + 1])
                pl.done("query")

            def rope(j, k):
                if k == 0:
                    low = slice(RD, P)
                    lo_of(q2[low, j % 2, :], q2[low, j % 2, :], rows=low)
                else:
                    lo_of(kk[:, j % 2, LO, :], kk[:, j % 2, HI, :])
                pl.done("rope")

            def score(j, i):
                w = (i + 1) * P
                ps = sk[i][:, 0:w]
                dve.wait_ge(s_full, pl.at("s", 1))
                carry()
                nc.vector.tensor_tensor_reduce(ps, ps, maskt[:, S - w:S], -SCALE, 3.0e38, ALU.add, ALU.min,
                                               nmx[:, j % 2, i:i + 1]).then_inc(s_min, 1)
                dve.wait_ge(s_min, pl.at("s", 1))
                nc.vector.scalar_tensor_tensor(out=nb[:, j % 2, i:i + 1], in0=nmx[:, j % 2, i:i + 1], scalar=cb[:, i, j:j + 1],
                                               in1=cb[:, i, j:j + 1], op0=ALU.add, op1=ALU.subtract).then_inc(s_bias, 1)
                pl.done("score")
                pl.mark(("s", i), "s")

            def reciprocal(j, i):
                dve.wait_ge(s_exp, pl.since(("s", i), S0))
                nc.vector.reciprocal(rsm[:, j % 2, i:i + 1], sm[:, j % 2, i:i + 1]).then_inc(s_rec, 1)

            def turn(i):
                w = (i + 1) * P
                dve.wait_ge(m_hi, pl.at("hi", 1))
                at = (slice(0, i + 1), slice(i * P, (i + 1) * P))
                nc.vector.tensor_tensor(pTv[:, LO, at[0], at[1]], mb[pl.slot("m")][:, 0:w].rearrange("p (k n) -> p k n", n=P),
                                        pTv[:, HI, at[0], at[1]], ALU.subtract).then_inc(m_free, 1)
                pl.done("turn")

            def context(j):
                lo_of(cx[:, LO, j, :], cx[:, HI, j, :])
                pl.done("context")

            def project(t):
                if t == 0:
                    dve.wait_ge(acc_in, pl.at("batch") * 16 + 16)
                dve.wait_ge(m_free, pl.at("m", -1))
                dve.wait_ge(m_full, pl.at("m", 1))
                nc.vector.tensor_tensor(acc[:, t, :], mb[pl.slot("m")][:, :], acc[:, t, :], ALU.add).then_inc(m_free, 1)
                pl.done("project")

            def step(ins):
                ins.then_inc(ln_step, 1)
                pl.done("step")
                dve.wait_ge(ln_step, pl.at("ln"))

            def row_stats(t):
                return nc.vector.bn_stats(stats[:, t, :], xn[:, t, :])

            def row_vars(ins):
                step(ins)
                carry()
                for t in range(NT):
                    ins = nc.vector.bn_aggr(mv[:, t, :], stats[:, t, :])
                step(ins)
                nc.vector.tensor_scalar(ve[:, :], mv[:, :, 1], EPS, None, ALU.add).then_inc(ln_var, 1)

            def rows_normed():
                dve.wait_ge(ln_rstd, pl.at("var", 1))
                for t in range(NT):
                    ins = nc.vector.tensor_scalar(xn[:, t, :], xn[:, t, :], mv[:, t, 0:1], rstd[:, t:t + 1], ALU.subtract, ALU.mult)
                ins.then_inc(ln_xn, 1)
                pl.done("normed")

            def gated(t):
                if t == 0:
                    dve.wait_ge(gab_in, pl.at("batch") * 16 + 16)
                dve.wait_ge(m_free, pl.at("m"))
                nc.vector.tensor_tensor(acc[:, t, :], acc[:, t, :], gab[:, 0, :], ALU.mult).then_inc(res_step, 1)

            def residual_stats(t):
                dve.wait_ge(res_sum, pl.at("res", 1))
                pl.done("summed")
                step(nc.vector.bn_stats(stats[:, t, :], acc[:, t, :]))
                carry()
                step(nc.vector.bn_aggr(mv[:, t, :], stats[:, t, :]))
                nc.vector.tensor_scalar(ve[:, t:t + 1], mv[:, t, 1:2], EPS, None, ALU.add).then_inc(ln_var, 1)

            def normed(t):
                dve.wait_ge(ln_rstd, pl.at("var", 1))
                nc.vector.tensor_scalar(xn[:, t, :], acc[:, t, :], mv[:, t, 0:1], rstd[:, t:t + 1],
                                        ALU.subtract, ALU.mult).then_inc(ln_xn, 1)
                pl.done("residual")

            def experts():
                for t in range(NT):
                    dve.wait_ge(m_full, pl.at("m", 1))
                    nc.vector.tensor_copy(mid[:, t, :], mb[pl.slot("m")][:, 0:FW]).then_inc(m_free, 1)
                    pl.done("expert")
                dve.wait_ge(m_free, pl.at("m"))

                def gstep(ins):
                    ins.then_inc(gate_step, 1)
                    pl.done("gate_step")
                    dve.wait_ge(gate_step, pl.at("gate"))

                def tile(i):
                    return sc[:, i, :].rearrange("p (t e) -> p t e", t=NT)

                def per_row(i):
                    return sc[:, i, 0:NT]

                def spread(ap, n=NE):
                    return ap.unsqueeze(2).broadcast_to([P, NT, n])

                logits = mid[:, :, NE * R:FW]
                gstep(nc.vector.tensor_reduce(per_row(2), logits, AX.X, ALU.max))
                nc.vector.tensor_tensor(tile(0), logits, spread(per_row(2)), ALU.subtract).then_inc(gate_max, 1)
                dve.wait_ge(gate_exp, pl.at("batch") + 1)
                gstep(nc.vector.tensor_reduce(per_row(3), tile(1), AX.X, ALU.add))
                gstep(nc.vector.reciprocal(per_row(4), per_row(3)))
                gstep(nc.vector.tensor_tensor(tile(5), tile(1), spread(per_row(4)), ALU.mult))
                carry()
                for t in range(NT):
                    ins = nc.vector.max(v8[:, t, :], tile(5)[:, t, :])
                gstep(ins)
                carry()
                for t in range(NT):
                    ins = nc.vector.max_index(i8[:, t, :], v8[:, t, :], tile(5)[:, t, :])
                gstep(ins)
                gstep(nc.vector.tensor_tensor(per_row(2), v8[:, :, 0], v8[:, :, 1], ALU.add))
                gstep(nc.vector.reciprocal(per_row(3), per_row(2)))
                w = sc[:, 4, 0:2 * NT].rearrange("p (t e) -> p t e", e=2)
                ix = sc[:, 6, 0:2 * NT].rearrange("p (t e) -> p t e", e=2)
                gstep(nc.vector.scalar_tensor_tensor(out=w, in0=v8[:, :, 0:2], scalar=LORA_SCALING, in1=spread(per_row(3), 2),
                                                     op0=ALU.mult, op1=ALU.mult))
                gstep(nc.vector.tensor_copy(ix, i8[:, :, 0:2]))
                io = iotat.unsqueeze(1).broadcast_to([P, NT, NE])
                gstep(nc.vector.tensor_tensor(tile(0), io, spread(ix[:, :, 0]), ALU.is_equal))
                gstep(nc.vector.tensor_tensor(tile(1), tile(0), spread(w[:, :, 0]), ALU.mult))
                gstep(nc.vector.tensor_tensor(tile(5), io, spread(ix[:, :, 1]), ALU.is_equal))
                gstep(nc.vector.tensor_tensor(tile(7), tile(5), spread(w[:, :, 1]), ALU.mult))
                gstep(nc.vector.tensor_tensor(tile(0), tile(1), tile(7), ALU.add))
            nc.vector.memset(nhalf[:, :], -0.5)
            nc.vector.memset(brow[:, :].bitcast(F32), 0.0).then_inc(zeroed, 1)
            for k in range(Y0):
                nc.vector.memset(tiny2[:, k:k + 1], 0.0).then_inc(y_mul, 1)

            def link(ins, n):
                ins.then_inc(set_step, 1)
                dve.wait_ge(set_step, n)

            dve.wait_ge(silu_e, 1)
            link(nc.vector.tensor_scalar(sE[:, 1, :], sE[:, 0, :], 1.0, None, ALU.add), 1)
            link(nc.vector.reciprocal(sE[:, 0, :], sE[:, 1, :]), 2)
            nc.vector.tensor_tensor(sT, sT, sE[:, 0, :], ALU.mult).then_inc(silu_done, 1)
            dve.wait_ge(c_in, 4 * 16)
            nc.vector.tensor_copy(selr[:, :, :], selt.rearrange("p (k n) -> p k n", k=3)).then_inc(sel_ready, 1)

            def split(k):
                src, dst = job_parts(k)
                dve.wait_ge(raw_hi, k + 1)
                nc.vector.tensor_tensor(dst[LO], src, dst[HI], ALU.subtract).then_inc(raw_lo, 1)

            for k in range(EARLY):
                split(k)
            dve.wait_ge(zeroed, 1)
            dve.wait_ge(raw_lo, EARLY)
            dve.wait_ge(x_in, 16)
            for t in range(NT):
                ins = row_stats(t)
            row_vars(ins)
            rows_normed()

            def mod(k):
                dve.wait_ge(m_full, pl.at("m", 1))
                ps = mb[pl.slot("m")][0:B, :]
                if k in (2, 5):
                    n = 3 + 3 * (k // 3)
                    link(nc.vector.tensor_scalar(grow, ps, -1.0, 0.25, ALU.mult, ALU.max), n)
                    link(nc.vector.scalar_tensor_tensor(out=grow, in0=ps, scalar=0.25, in1=grow, op0=ALU.max, op1=ALU.max), n + 1)
                    nc.vector.tensor_scalar(gab[0:B, k // 3, :], ps, 0.0, 2.0, ALU.is_ge, ALU.mult).then_inc(m_free, 1)
                    dve.wait_ge(m_free, pl.at("m", 1))
                    nc.vector.scalar_tensor_tensor(out=gab[0:B, k // 3, :], in0=gab[0:B, k // 3, :], scalar=1.0, in1=grow,
                                                   op0=ALU.subtract, op1=ALU.mult).then_inc(set_step, 1)
                    dve.wait_ge(set_step, n + 2)
                else:
                    r = (0, 1, None, 2, 3)[k]
                    nc.vector.tensor_scalar(modrow[:, r * HID:(r + 1) * HID], ps, float(k in (1, 4)), None, ALU.add).then_inc(m_free, 1)
                pl.done("one")

            for h in range(NH):
                dve.wait_ge(m_hi, pl.at("hi", 1))
                u = pl.slot("m")
                pv = mb[u][:, 0:387].rearrange("p (m n) -> p m n", m=NM)
                nc.vector.tensor_tensor(wps[h % 2][:, LO, :, :], pv[:, :, 0:KVC], wps[h % 2][:, HI, :, :], ALU.subtract)
                nc.vector.tensor_copy(gcol[:, :, h:h + 1], pv[:, :, KVC:KVC + 1])
                nc.vector.tensor_copy(crow[0:1, h:h + 1], mb[u][0:1, 391:392])
                nc.vector.tensor_copy(qbias[:, h:h + 1], mb[u][:, 390:391]).then_inc(m_free, 1)
                dve.wait_ge(m_hi, pl.at("hi", 2))
                nc.vector.tensor_tensor(wvs[h % 2][:, LO, :], mb[pl.slot("m", 1)][:, :], wvs[h % 2][:, HI, :], ALU.subtract).then_inc(m_free, 1)
                pl.done("absorb")
                if mod_after(h):
                    mod(h // 2)
                if EARLY + h < ROWS:
                    split(EARLY + h)
            dve.wait_ge(bias_full, 1)
            nc.vector.tensor_copy(bias_s[:, :], sk[0][0:1, :]).then_inc(bias_ev, 1)
            dve.wait_ge(m_free, pl.at("m"))
            dve.wait_ge(g_hi, 1)
            nc.vector.tensor_tensor(gsp[:, LO, :, :], gcol[:, :, :], gsp[:, HI, :, :], ALU.subtract).then_inc(g_lo, 1)
            for k in range(ROWS, ROWS + 2):
                dve.wait_ge(raw_in[k % 2], 16 * (k // 2 + 1))
                h0 = 2 * GH * (k - ROWS)
                nc.vector.tensor_copy(raw[k % 2][0:1, 0:2 * QW].rearrange("p (g n) -> p g n", g=2)[:, :, KW:QW],
                                      crow[0:1, h0:h0 + 2 * GH].rearrange("p (g n) -> p g n", g=2)).then_inc(crow_in, 1)
            for k in range(ROWS, NJ):
                split(k)
            for r in range(2):
                dve.wait_ge(m_full, pl.at("m", r + 1))
                nc.vector.tensor_copy(modT[:, 2 * NC * r:2 * NC * (r + 1), :],
                                      mb[pl.slot("m", r)][:, 0:2 * NC * B].rearrange("p (k b) -> p k b", b=B)).then_inc(m_free, 1)
            pl.done("modT")
            dve.wait_ge(m_free, pl.at("m"))
            nc.vector.tensor_copy(modb[:, :], modT[:, :, 0]).then_inc(mod_b, 1)
            for c in range(NC):
                feature(c)
            for m in range(NM + 1):
                latent(m)
            for hl in (HI, LO):
                kv_row(hl)
            nc.vector.tensor_copy(qbg[:, :], qbias[:, 0:GH]).then_inc(grp_ready, 1)
            pl.done("group")
            query(0)
            query(1)
            dve.wait_ge(bias_out, 16)
            for t in range(NT):
                rotate(t, 0)
                rotate(t, 1)
            dve.wait_ge(m_free, pl.at("m"))
            link(nc.vector.tensor_copy(cb[:, :, :], cbn[:, :, :]), 9)
            for j in range(2):
                rope(j, 0)
                rope(j, 1)
            for i in range(NT):
                score(0, i)
                if i:
                    reciprocal(0, i - 1)
            reciprocal(0, NT - 1)

            def group(g, first, last, more, x_loads=0):
                turn(0)
                turn(1)
                if first:
                    rope(2, 0)
                    turn(2)
                    rope(2, 1)
                    turn(3)
                    query(2)
                    for i in range(NT):
                        score(1, i)
                        if i:
                            reciprocal(1, i - 1)
                    rope(3, 0)
                    reciprocal(1, NT - 1)
                    rope(3, 1)
                    context(0)
                    query(3)
                else:
                    rope(2, 0)
                    score(1, 0)
                    score(1, 1)
                    reciprocal(1, 0)
                    score(1, 2)
                    turn(2)
                    reciprocal(1, 1)
                    if last and more:
                        dve.wait_ge(x_in, x_loads)
                        row_stats(0)
                        row_stats(1)
                    reciprocal(1, 2)
                    project(0)
                    rope(2, 1)
                    if last and more:
                        row_stats(2)
                        row_vars(row_stats(3))
                    project(1)
                    score(1, 3)
                    turn(3)
                    reciprocal(1, 3)
                    if last and more:
                        rows_normed()
                    project(2)
                    rope(3, 0)
                    query(2)
                    rope(3, 1)
                    project(3)
                    if not last:
                        query(3)
                    context(0)

                turn(0)
                turn(1)
                score(2, 0)
                score(2, 1)
                if not last:
                    reciprocal(2, 0)
                    rotate(0, 0)
                    turn(2)
                    reciprocal(2, 1)
                    score(2, 2)
                    rotate(0, 1)
                    reciprocal(2, 2)
                    rotate(1, 0)
                    turn(3)
                    score(2, 3)
                    rotate(1, 1)
                    reciprocal(2, 3)
                    rotate(2, 0)
                else:
                    turn(2)
                    reciprocal(2, 0)
                    score(2, 2)
                    turn(3)
                    reciprocal(2, 1)
                    score(2, 3)
                    reciprocal(2, 2)
                    reciprocal(2, 3)
                    if more:
                        feature(0)
                        feature(1)
                    query(3)
                context(1)
                if not last:
                    rotate(2, 1)
                elif more:
                    feature(2)
                    feature(3)

                turn(0)
                turn(1)
                score(3, 0)
                score(3, 1)
                reciprocal(3, 0)
                if not last:
                    rotate(3, 0)
                reciprocal(3, 1)
                if last and more:
                    latent(0)
                turn(2)
                score(3, 2)
                if not last:
                    rotate(3, 1)
                reciprocal(3, 2)
                turn(3)
                score(3, 3)
                if not last:
                    ready(g + 1)
                reciprocal(3, 3)
                if not last:
                    query(0)
                    rope(0, 0)
                    rope(0, 1)
                elif more:
                    latent(1)
                context(2)

                turn(0)
                turn(1)
                if not last:
                    query(1)
                    turn(2)
                    score(0, 0)
                    score(0, 1)
                    turn(3)
                    rope(1, 0)
                    reciprocal(0, 0)
                    score(0, 2)
                    reciprocal(0, 1)
                    rope(1, 1)
                    score(0, 3)
                    reciprocal(0, 2)
                else:
                    if more:
                        latent(2)
                    turn(2)
                    if more:
                        latent(3)
                    turn(3)
                    if more:
                        rotate(0, 0)
                context(3)
                if not last:
                    reciprocal(0, 3)

            def batch(b, more):
                group(0, True, False, more)
                with passes(dve, pl, 1, NG - 1, GROUP) as g:
                    group(g, False, False, more)
                if more:
                    nc.vector.tensor_copy(modb[:, 0:2 * NC], modT[:, 0:2 * NC, b + 1])
                nc.vector.tensor_copy(modb[:, 2 * NC:4 * NC], modT[:, 2 * NC:4 * NC, b]).then_inc(mod_b, 1)
                group(NG - 1, False, True, more, pl.at("batch") * 32 + 32)
                if more:
                    rotate(0, 1)
                    rotate(1, 0)
                    rotate(1, 1)
                for t in range(NT):
                    if more and t >= 2:
                        rotate(t, 0)
                        rotate(t, 1)
                    project(t)
                    gated(t)
                    if t >= 1:
                        residual_stats(t - 1)
                    if more and t < 2:
                        kv_row(t)
                    if t >= 2:
                        normed(t - 2)
                if more:
                    ready(0)
                    query(0)
                    residual_stats(3)
                    normed(2)
                    rope(0, 0)
                    normed(3)
                    rope(0, 1)
                    query(1)
                    rope(1, 0)
                    rope(1, 1)
                    feature(0)
                    feature(1)
                    feature(2)
                    score(0, 0)
                    feature(3)
                    score(0, 1)
                    reciprocal(0, 0)
                    score(0, 2)
                    reciprocal(0, 1)
                    score(0, 3)
                    reciprocal(0, 2)
                    reciprocal(0, 3)
                else:
                    residual_stats(3)
                    normed(2)
                    normed(3)
                    for c in range(NC):
                        feature(c)
                experts()
                for k in range(2):
                    dve.wait_ge(m_hi, pl.at("hi", 1))
                    at = slice(k * 256, (k + 1) * 256)
                    nc.vector.tensor_tensor(midT[:, LO, at], mb[pl.slot("m")][:, 0:256], midT[:, HI, at], ALU.subtract).then_inc(m_free, 1)
                    pl.done("turn_mid")
                for t in range(NT):
                    dve.wait_ge(f_full, pl.at("y", 1))
                    nc.vector.tensor_tensor(xn[:, t, :], sk[t][:, :], gab[:, 1, :], ALU.mult).then_inc(y_mul, 1)
                    pl.done("ffn_out")
                pl.done("batch")

            with passes(dve, pl, 0, B - 1, BATCH) as b:
                batch(b, True)
            batch(B - 1, False)

        @block.gpsimd
        def _(pool):
            pl = Place()

            def rotate(t, k):
                pool.wait_ge(m_free, pl.at("m", 1))
                u = pl.slot("ab")
                a, r = (ab[:, u, i, :].rearrange("p (j n) -> p j n", n=RD) for i in (0, 1))
                o = rq[:, k, t, :].rearrange("p (j d n) -> p j d n", d=2, n=RD)
                nc.gpsimd.tensor_tensor(o[:, :, 0, :], a, r, ALU.add)
                nc.gpsimd.tensor_tensor(o[:, :, 1, :], a, r, ALU.add).then_inc(rotated, 1)
                pl.done("rotate")

            def normalise(j, i):
                o, w = i * (i + 1) // 2 * P, (i + 1) * P
                pool.wait_ge(s_rec, pl.at("s", 1))
                nc.gpsimd.tensor_tensor(pr[:, j % 2, o:o + w], pr[:, j % 2, o:o + w],
                                        rsm[:, j % 2, i:i + 1].broadcast_to([P, w]), ALU.mult).then_inc(p_norm, 1)
                pl.done("score")

            def rstd_of(k, n):
                pool.wait_ge(ln_var, pl.at("var", 1))
                nc.gpsimd.tensor_tensor(rstd[:, k:k + n], ve[:, k:k + n], nhalf[:, k:k + n], ALU.pow).then_inc(ln_rstd, 1)

            def residual(t, x_loads):
                if t == 0:
                    pool.wait_ge(x_in, x_loads)
                a = acc[:, t, :]
                pool.wait_ge(res_step, pl.at("res", 1))
                nc.gpsimd.tensor_tensor(a, a, xn[:, t, :], ALU.add).then_inc(res_sum, 1)
                pl.done("summed")

            def load(k):
                src, rows, n, a, _, _ = JOBS[k]
                dst = raw[k % 2][0:rows, 0:n]
                pool.dma_start(v3(dst, a) if a > 1 else dst, src).then_inc(raw_in[k % 2], 16)

            def store(k):
                pool.wait_ge(raw_lo, k + 1)
                for dst, hl, n, a in JOBS[k][5]:
                    if hl is None:
                        src = stg[k % 2][0:JOBS[k][1], :, 0:n].bitcast(F32)
                    else:
                        src = v3(stg[k % 2][0:JOBS[k][1], hl, 0:n].bitcast(F32), a)
                    pool.dma_start(dst, src).then_inc(stg_out[k % 2], 16)

            load(0)
            load(1)
            pool.wait_ge(raw_lo, 1)
            load(2)
            for k in range(3, 5):
                pool.wait_ge(raw_lo, k - 1)
                load(k)
            pool.wait_ge(zeroed, 1)
            rstd_of(0, NT)
            pl.done("mod", "mod", "mod", "modT", "normed", *["feature"] * NC, *["latent"] * (NM + 1), *["absorb"] * NH)
            for k in range(EARLY, ROWS):
                store(k)
                load(k + 2)
            for k in range(2):
                pool.wait_ge(set_step, 5 + 3 * k)
                pool.dma_start(gate_d[:, k, :], gab[0:B, k, :]).then_inc(gate_out, 16)
            for k in range(ROWS, NJ):
                store(k)
            pl.done("kv_row", "kv_row", "query", "query")
            for t in range(NT):
                rotate(t, 0)
                rotate(t, 1)
            pl.done("group", *["rope"] * 4)
            for i in range(NT):
                normalise(0, i)

            def group(first, last, more):
                pl.done("turn", "turn")
                if first:
                    pl.done("rope", "turn", "rope", "turn", "query", "rope", "rope", "context", "query")
                else:
                    pl.done("project", "turn", "rope", "project", "rope", "project", "turn", "rope", "query", "rope",
                            "project", "query", "context")
                normalise(1, 0)
                normalise(1, 1)
                normalise(1, 2)
                if last and more:
                    rstd_of(0, NT)
                    pl.done("normed")
                normalise(1, 3)

                pl.done("turn", "turn")
                normalise(2, 0)
                if not last:
                    rotate(0, 0)
                    pl.done("turn")
                    normalise(2, 1)
                    rotate(0, 1)
                    normalise(2, 2)
                    rotate(1, 0)
                    pl.done("turn")
                    rotate(1, 1)
                    normalise(2, 3)
                    rotate(2, 0)
                    pl.done("context")
                    rotate(2, 1)
                else:
                    normalise(2, 1)
                    normalise(2, 2)
                    normalise(2, 3)
                    pl.done("turn", "turn", "context")
                    if more:
                        pl.done(*["feature"] * NC)

                pl.done("turn", "turn")
                normalise(3, 0)
                if not last:
                    rotate(3, 0)
                    pl.done("turn")
                normalise(3, 1)
                if not last:
                    rotate(3, 1)
                    pl.done("group", "turn", "query", "context", "rope", "rope")
                normalise(3, 2)
                normalise(3, 3)

                if not last:
                    pl.done("turn", "turn", "query", "turn", "rope", "turn", "rope", "context")
                    for i in range(NT):
                        normalise(0, i)
                else:
                    pl.done("turn", "turn", "context", *["turn"] * NT)
                    if more:
                        pl.done(*["latent"] * (NM + 1))
                        rotate(0, 0)
                    pl.done("context")

            def batch(b, more):
                group(True, False, more)
                with passes(pool, pl, 1, NG - 1, GROUP):
                    group(False, False, more)
                group(False, True, more)
                if more:
                    rotate(0, 1)
                    rotate(1, 0)
                    rotate(1, 1)
                for t in range(NT):
                    if more and t >= 2:
                        rotate(t, 0)
                        rotate(t, 1)
                    pl.done("project")
                    residual(t, pl.at("batch") * 32 + (48 if more else 32))
                    if t >= 1:
                        rstd_of(t - 1, 1)
                        pl.done("residual")
                    if more and t < 2:
                        pl.done("kv_row")
                rstd_of(NT - 1, 1)
                pl.done("residual")
                if more:
                    pl.done("group", "query", "rope", "rope", "query", "rope", "rope")
                pl.done(*["feature"] * NC)
                if more:
                    for i in range(NT):
                        normalise(0, i)
                pl.done(*["expert"] * NT)
                pool.wait_ge(gate_step, pl.at("gate", GATE_STEPS))
                gate = sc[:, 0, :].rearrange("p (t e) -> p t e", t=NT).unsqueeze(3).broadcast_to([P, NT, NE, R])
                nc.gpsimd.tensor_tensor(midg.rearrange("p t (e r) -> p t e r", r=R), mid[:, :, 0:NE * R].rearrange("p t (e r) -> p t e r", r=R),
                                        gate, ALU.mult).then_inc(mid_gated, 1)
                pl.done(*["gate_step"] * GATE_STEPS, "turn_mid", "turn_mid")
                for t in range(NT):
                    pool.wait_ge(y_mul, pl.at("y", Y0 + 1))
                    nc.gpsimd.tensor_tensor(xn[:, t, :], xn[:, t, :], acc[:, t, :], ALU.add).then_inc(y_done, 1)
                    pl.done("ffn_out")
                pl.done(*["step"] * (2 * NT + 2 * more), "batch")

            with passes(pool, pl, 0, B - 1, BATCH) as b:
                batch(b, True)
            batch(B - 1, False)


def constants():
    ident = np.eye(P, dtype=np.float32)
    mask = np.zeros((P, S), np.float32)
    mask[:, S - P:] = np.where(np.arange(P)[None, :] > np.arange(P)[:, None], np.float32(-1e30), np.float32(0))
    power = np.power(10000.0, (np.arange(0, RD, 2, dtype=np.float32) / np.float32(RD)).astype(np.float64)).astype(np.float32)
    inv_freq = np.float32(1) / power
    ang = (np.arange(S, dtype=np.float32)[:, None] * inv_freq[None, :]).astype(np.float64)
    c, s = np.cos(ang).astype(np.float32), np.sin(ang).astype(np.float32)
    tiles = [np.concatenate(h, 1).reshape(NT, P, RD).transpose(1, 0, 2).reshape(P, NT * RD) for h in ((c, c), (-s, s))]
    iota = np.tile(np.arange(NE, dtype=np.float32), (P, 1))
    sel = np.zeros((P, 3, P), np.float32)
    for k in range(3):
        sel[2 * k:2 * k + 2, k, :] = 1
    return np.concatenate([ident, mask, *tiles, iota, sel.reshape(P, 3 * P)], 1)


def kernel(**inputs):
    import concourse.bacc as bacc
    from concourse.bass_utils import run_bass_kernel_spmd

    a = {n: np.asarray(v) for n, v in inputs.items()}
    at, ff = "L0_attn_", "L0_ffn_"

    def by_head(b):
        return b.reshape(NH, HD).T

    laid = {
        "x": a[at + "x"],
        "inputs": np.concatenate([a["L0_c"].T.reshape(NC, P, B).transpose(1, 0, 2).reshape(P, NC * B),
                                  a[at + "b_qd"].reshape(NM, P).T, a[at + "b_kvd"].reshape(P, 1),
                                  by_head(a[at + "b_qu"]), by_head(a[at + "b_ku"]), by_head(a[at + "b_vu"])], 1),
        "consts": constants(),
        "b_o": a[at + "b_o"].reshape(1, HID),
        "wmod": a["L0_wmod"],
        "w_qd": a[at + "W_qd"],
        "w_kvd": a[at + "W_kvd"],
        "heads_w": np.concatenate([a[at + "W_qu"].T, a[at + "W_ku"].T, a[at + "b_ku"].reshape(NH * HD, 1),
                                   a[at + "W_vu"].T, a[at + "W_o"]], 1),
        "w_qr": a[at + "W_qr"],
        "w_kr": a[at + "W_kr"],
        "base_wT": a[ff + "base_w"].T,
        "ffn_a": np.concatenate([a[ff + "lora_A"].transpose(1, 0, 2).reshape(HID, NE * R), a[ff + "router_w"].T], 1),
        "ffn_b": a[ff + "lora_B"].reshape(NE * R, HID),
        "q_row": np.concatenate([a[at + "b_qr"].reshape(NG, KW), np.zeros((NG, GH), np.float32)], 1).reshape(1, NG * QW),
        "k_row": a[at + "b_kr"].reshape(1, NG * KW),
        "f_row": np.concatenate([a[ff + "base_b"], np.zeros(NE * R, np.float32), a[ff + "router_b"]]).reshape(1, HID + FW),
    }
    nc = bacc.Bacc("TRN2", target_bir_lowering=False, num_devices=1)
    arrays, args = {}, []
    for name, v in laid.items():
        v = np.ascontiguousarray(v)
        arrays[f"in_{name}"] = v
        args.append(nc.dram_tensor(f"in_{name}", v.shape, mybir.dt.from_np(v.dtype), kind="ExternalInput").ap())
    args.append(nc.dram_tensor("out_y", (B, S, HID), F32, kind="ExternalOutput").ap())
    build(nc, *args)
    r = run_bass_kernel_spmd(nc, [arrays], core_ids=[0])
    return r.results[0]["out_y"]
```
